# Optimizing a Trainium2 kernel written in Bass

```python
import numpy as np
import jax
import jax.numpy as jnp

def _softmax(x, axis=-1):
    return jax.nn.softmax(x, axis=axis)

def _gelu(x):
    return jax.nn.gelu(x, approximate=True)

def _silu(x):
    return jax.nn.silu(x)

def _sigmoid(x):
    return jax.nn.sigmoid(x)

def _layernorm(x, axis=-1, eps=1e-05):
    m = jnp.mean(x, axis=axis, keepdims=True)
    v = jnp.var(x, axis=axis, keepdims=True)
    return (x - m) / jnp.sqrt(v + eps)

def _scatter_add(tgt, idx, src, axis=0):
    return tgt.at[idx].add(src)

def _segment_sum(src, seg, n):
    return jax.ops.segment_sum(src, seg, n)
kernel_name = 'mk_vit_tower_d2_tok_img768_r4_1df698'

def setup_inputs(seed: int=0):
    np.random.seed(seed)
    _w = jnp.asarray

    def _rec_inputs():
        import jax
        import jax.numpy as jnp
        _rk = jax.random.key(seed)
        x = -0.000356955 + 1 * jax.random.normal(jax.random.fold_in(_rk, 1), (64, 3, 224, 224), jnp.float32)
        return x
    x = _rec_inputs()

    def _L0_tok_setup():
        import jax, jax.numpy as jnp
        import numpy as np
        IMAGE_SIZE = 224
        PATCH = 16
        EMBED = 192
        IN_FEAT = 3 * PATCH * PATCH
        NUM_PATCHES = (IMAGE_SIZE // PATCH) ** 2
        BATCH = 128

        def _patchify(x):
            B, C, H, Wd = x.shape
            p = PATCH
            Hp, Wp = (H // p, Wd // p)
            x = x.reshape(B, C, H, Wp, p)
            x = x.reshape(B, C, Hp, p, Wp, p)
            x = jnp.transpose(x, (0, 1, 2, 4, 5, 3))
            return x.reshape(B, NUM_PATCHES, IN_FEAT)
        key = jax.random.key(seed)
        k1, k2, k3 = jax.random.split(key, 3)
        x = jax.random.normal(k1, (BATCH, 3, IMAGE_SIZE, IMAGE_SIZE), dtype=jnp.float32)
        W = jax.random.normal(k2, (EMBED, IN_FEAT), dtype=jnp.float32) * (1.0 / np.sqrt(IN_FEAT))
        b = jax.random.normal(k3, (EMBED,), dtype=jnp.float32) * 0.01
        return {'x': x, 'W': W, 'b': b}
    _L0_tok_all = _L0_tok_setup()
    _L0_tok_in = {k: v for k, v in _L0_tok_all.items() if k in ('W', 'b')}
    del _L0_tok_all

    def _L0_attn_setup():
        import jax, jax.numpy as jnp
        import numpy as np
        import math
        B, L, D = (2, 512, 192)
        H, DK = (8, 64)
        DV = D // H
        N_POS = 32
        DFF = 2 * D
        EPS = 1e-05

        def _rel_basis(l: int, n: int) -> jnp.ndarray:
            pos = jnp.arange(l)
            distance = pos[None, :] - pos[:, None]
            pow_rate = jnp.exp(jnp.log(jnp.float32((l + 1) / 2.0)) / (n // 2))
            center_widths = pow_rate ** jnp.arange(1, n // 2 + 1, dtype=jnp.float32)
            d = distance[:, :, None].astype(jnp.float32)
            unsigned = (jnp.abs(d) <= center_widths).astype(jnp.float32)
            signed = jnp.sign(d) * unsigned
            return jnp.concatenate([unsigned, signed], axis=-1)

        def _rmsnorm(x, w):
            norm = jnp.mean(x * x, axis=-1, keepdims=True)
            return x * jax.lax.rsqrt(norm + EPS) * w
        key = jax.random.key(seed)
        ks = jax.random.split(key, 12)
        s = 0.02
        return {'x': jax.random.normal(ks[0], (B, L, D), jnp.float32), 'norm1_w': jnp.ones((D,), jnp.float32), 'norm2_w': jnp.ones((D,), jnp.float32), 'wq': jax.random.normal(ks[1], (D, H * DK), jnp.float32) * s, 'wk': jax.random.normal(ks[2], (D, H * DK), jnp.float32) * s, 'wv': jax.random.normal(ks[3], (D, H * DV), jnp.float32) * s, 'wo': jax.random.normal(ks[4], (H * DV, D), jnp.float32) * s, 'bo': jnp.zeros((D,), jnp.float32), 'u_param': jax.random.normal(ks[5], (H, DK), jnp.float32) * s, 'v_param': jax.random.normal(ks[6], (H, DK), jnp.float32) * s, 'w_pos': jax.random.normal(ks[7], (H, DK, N_POS), jnp.float32) * s, 'w1': jax.random.normal(ks[8], (D, DFF), jnp.float32) * s, 'b1': jnp.zeros((DFF,), jnp.float32), 'w2': jax.random.normal(ks[9], (DFF, D), jnp.float32) * s, 'b2': jnp.zeros((D,), jnp.float32)}
    _L0_attn_all = _L0_attn_setup()
    _L0_attn_in = {k: v for k, v in _L0_attn_all.items() if k in ('norm1_w', 'norm2_w', 'wq', 'wk', 'wv', 'wo', 'bo', 'u_param', 'v_param', 'w_pos', 'w1', 'b1', 'w2', 'b2')}
    del _L0_attn_all

    def _L0_ffn_setup():
        import jax, jax.numpy as jnp
        import numpy as np
        CAPACITY_FACTOR = 1.25
        key = jax.random.key(seed)
        ks = jax.random.split(key, 5)
        B, S, D, F, E = (8, 512, 192, 768, 8)
        return {'x': jax.random.normal(ks[0], (B, S, D), jnp.float32), 'switch_w': jax.random.normal(ks[1], (D, E), jnp.float32) * 0.02, 'switch_b': jnp.zeros((E,), jnp.float32), 'w1': jax.random.normal(ks[2], (E, D, F), jnp.float32) * 0.02, 'b1': jnp.zeros((E, F), jnp.float32), 'w2': jax.random.normal(ks[3], (E, F, D), jnp.float32) * 0.02, 'b2': jnp.zeros((E, D), jnp.float32)}
    _L0_ffn_all = _L0_ffn_setup()
    _L0_ffn_in = {k: v for k, v in _L0_ffn_all.items() if k in ('switch_w', 'switch_b', 'w1', 'b1', 'w2', 'b2')}
    del _L0_ffn_all

    def _L1_attn_setup():
        import jax, jax.numpy as jnp
        import numpy as np
        import math
        N_EMBD = 192
        N_HEAD = 12
        HEAD_DIM = N_EMBD // N_HEAD

        def rope_cache(T, dim):
            inv_freq = 1.0 / 10000.0 ** (2.0 * jnp.arange(dim // 2, dtype=jnp.float32) / dim)
            angles = jnp.arange(T, dtype=jnp.float32)[:, None] * inv_freq[None, :]
            return jnp.stack((jnp.cos(angles), jnp.sin(angles)), axis=-1)

        def apply_rope(x, rope):
            B, H, T, D = x.shape
            xp = x.reshape(B, H, T, D // 2, 2)
            x1, x2 = (xp[..., 0], xp[..., 1])
            cos = rope[None, None, :, :, 0]
            sin = rope[None, None, :, :, 1]
            out = jnp.stack((x1 * cos - x2 * sin, x1 * sin + x2 * cos), axis=-1)
            return out.reshape(B, H, T, D)
        key = jax.random.key(seed)
        ks = jax.random.split(key, 9)
        s = 0.02
        d = N_EMBD
        return {'x': jax.random.normal(ks[0], (2, 1024, d), dtype=jnp.float32), 'Wq': jax.random.normal(ks[1], (d, d), dtype=jnp.float32) * s, 'bq': jnp.zeros((d,), jnp.float32), 'Wk': jax.random.normal(ks[2], (d, d), dtype=jnp.float32) * s, 'bk': jnp.zeros((d,), jnp.float32), 'Wv': jax.random.normal(ks[3], (d, d), dtype=jnp.float32) * s, 'bv': jnp.zeros((d,), jnp.float32), 'Wp': jax.random.normal(ks[4], (d, d), dtype=jnp.float32) * s, 'bp': jnp.zeros((d,), jnp.float32)}
    _L1_attn_all = _L1_attn_setup()
    _L1_attn_in = {k: v for k, v in _L1_attn_all.items() if k in ('Wq', 'bq', 'Wk', 'bk', 'Wv', 'bv', 'Wp', 'bp')}
    del _L1_attn_all

    def _L1_ffn_setup():
        import jax, jax.numpy as jnp
        import numpy as np
        B, L, D, H, F = (4, 512, 192, 12, 768)
        ROUTE_FRAC = 0.15
        LN_EPS = 1e-05

        def _ln(x, g, b):
            m = jnp.mean(x, axis=-1, keepdims=True)
            v = jnp.mean((x - m) ** 2, axis=-1, keepdims=True)
            return (x - m) * jax.lax.rsqrt(v + LN_EPS) * g + b
        key = jax.random.key(seed)
        ks = jax.random.split(key, 20)
        s = 0.02
        return {'hidden_states': jax.random.normal(ks[0], (B, L, D), dtype=jnp.float32), 'g1': jnp.ones((D,), jnp.float32), 'b1': jnp.zeros((D,), jnp.float32), 'g2': jnp.ones((D,), jnp.float32), 'b2': jnp.zeros((D,), jnp.float32), 'Wr': jax.random.normal(ks[1], (D,), jnp.float32) * s, 'br': jnp.zeros((), jnp.float32), 'Wq': jax.random.normal(ks[2], (D, D), jnp.float32) * s, 'bq': jnp.zeros((D,), jnp.float32), 'Wk': jax.random.normal(ks[3], (D, D), jnp.float32) * s, 'bk': jnp.zeros((D,), jnp.float32), 'Wv': jax.random.normal(ks[4], (D, D), jnp.float32) * s, 'bv': jnp.zeros((D,), jnp.float32), 'Wo': jax.random.normal(ks[5], (D, D), jnp.float32) * s, 'bo': jnp.zeros((D,), jnp.float32), 'Wm': jax.random.normal(ks[6], (D, D), jnp.float32) * s, 'bm': jnp.zeros((D,), jnp.float32), 'W1': jax.random.normal(ks[7], (D, F), jnp.float32) * s, 'bf1': jnp.zeros((F,), jnp.float32), 'W2': jax.random.normal(ks[8], (F, D), jnp.float32) * s, 'bf2': jnp.zeros((D,), jnp.float32)}
    _L1_ffn_all = _L1_ffn_setup()
    _L1_ffn_in = {k: v for k, v in _L1_ffn_all.items() if k in ('g1', 'b1', 'g2', 'b2', 'Wr', 'br', 'Wq', 'bq', 'Wk', 'bk', 'Wv', 'bv', 'Wo', 'bo', 'Wm', 'bm', 'W1', 'bf1', 'W2', 'bf2')}
    del _L1_ffn_all
    return {'x': x, 'L0_tok_W': _L0_tok_in['W'], 'L0_tok_b': _L0_tok_in['b'], 'L0_attn_norm1_w': _L0_attn_in['norm1_w'], 'L0_attn_norm2_w': _L0_attn_in['norm2_w'], 'L0_attn_wq': _L0_attn_in['wq'], 'L0_attn_wk': _L0_attn_in['wk'], 'L0_attn_wv': _L0_attn_in['wv'], 'L0_attn_wo': _L0_attn_in['wo'], 'L0_attn_bo': _L0_attn_in['bo'], 'L0_attn_u_param': _L0_attn_in['u_param'], 'L0_attn_v_param': _L0_attn_in['v_param'], 'L0_attn_w_pos': _L0_attn_in['w_pos'], 'L0_attn_w1': _L0_attn_in['w1'], 'L0_attn_b1': _L0_attn_in['b1'], 'L0_attn_w2': _L0_attn_in['w2'], 'L0_attn_b2': _L0_attn_in['b2'], 'L0_ffn_switch_w': _L0_ffn_in['switch_w'], 'L0_ffn_switch_b': _L0_ffn_in['switch_b'], 'L0_ffn_w1': _L0_ffn_in['w1'], 'L0_ffn_b1': _L0_ffn_in['b1'], 'L0_ffn_w2': _L0_ffn_in['w2'], 'L0_ffn_b2': _L0_ffn_in['b2'], 'L1_attn_Wq': _L1_attn_in['Wq'], 'L1_attn_bq': _L1_attn_in['bq'], 'L1_attn_Wk': _L1_attn_in['Wk'], 'L1_attn_bk': _L1_attn_in['bk'], 'L1_attn_Wv': _L1_attn_in['Wv'], 'L1_attn_bv': _L1_attn_in['bv'], 'L1_attn_Wp': _L1_attn_in['Wp'], 'L1_attn_bp': _L1_attn_in['bp'], 'L1_ffn_g1': _L1_ffn_in['g1'], 'L1_ffn_b1': _L1_ffn_in['b1'], 'L1_ffn_g2': _L1_ffn_in['g2'], 'L1_ffn_b2': _L1_ffn_in['b2'], 'L1_ffn_Wr': _L1_ffn_in['Wr'], 'L1_ffn_br': _L1_ffn_in['br'], 'L1_ffn_Wq': _L1_ffn_in['Wq'], 'L1_ffn_bq': _L1_ffn_in['bq'], 'L1_ffn_Wk': _L1_ffn_in['Wk'], 'L1_ffn_bk': _L1_ffn_in['bk'], 'L1_ffn_Wv': _L1_ffn_in['Wv'], 'L1_ffn_bv': _L1_ffn_in['bv'], 'L1_ffn_Wo': _L1_ffn_in['Wo'], 'L1_ffn_bo': _L1_ffn_in['bo'], 'L1_ffn_Wm': _L1_ffn_in['Wm'], 'L1_ffn_bm': _L1_ffn_in['bm'], 'L1_ffn_W1': _L1_ffn_in['W1'], 'L1_ffn_bf1': _L1_ffn_in['bf1'], 'L1_ffn_W2': _L1_ffn_in['W2'], 'L1_ffn_bf2': _L1_ffn_in['bf2']}

def reference(x, L0_tok_W, L0_tok_b, L0_attn_norm1_w, L0_attn_norm2_w, L0_attn_wq, L0_attn_wk, L0_attn_wv, L0_attn_wo, L0_attn_bo, L0_attn_u_param, L0_attn_v_param, L0_attn_w_pos, L0_attn_w1, L0_attn_b1, L0_attn_w2, L0_attn_b2, L0_ffn_switch_w, L0_ffn_switch_b, L0_ffn_w1, L0_ffn_b1, L0_ffn_w2, L0_ffn_b2, L1_attn_Wq, L1_attn_bq, L1_attn_Wk, L1_attn_bk, L1_attn_Wv, L1_attn_bv, L1_attn_Wp, L1_attn_bp, L1_ffn_g1, L1_ffn_b1, L1_ffn_g2, L1_ffn_b2, L1_ffn_Wr, L1_ffn_br, L1_ffn_Wq, L1_ffn_bq, L1_ffn_Wk, L1_ffn_bk, L1_ffn_Wv, L1_ffn_bv, L1_ffn_Wo, L1_ffn_bo, L1_ffn_Wm, L1_ffn_bm, L1_ffn_W1, L1_ffn_bf1, L1_ffn_W2, L1_ffn_bf2):
    import jax
    import jax.numpy as jnp

    def _L0_tok_ref(x, W, b):
        import jax, jax.numpy as jnp
        import numpy as np
        IMAGE_SIZE = 224
        PATCH = 16
        EMBED = 192
        IN_FEAT = 3 * PATCH * PATCH
        NUM_PATCHES = (IMAGE_SIZE // PATCH) ** 2
        BATCH = 128

        def _patchify(x):
            B, C, H, Wd = x.shape
            p = PATCH
            Hp, Wp = (H // p, Wd // p)
            x = x.reshape(B, C, H, Wp, p)
            x = x.reshape(B, C, Hp, p, Wp, p)
            x = jnp.transpose(x, (0, 1, 2, 4, 5, 3))
            return x.reshape(B, NUM_PATCHES, IN_FEAT)
        patches = _patchify(x)
        return jnp.einsum('bnf,ef->bne', patches, W) + b

    def _L0_attn_ref(x, norm1_w, norm2_w, wq, wk, wv, wo, bo, u_param, v_param, w_pos, w1, b1, w2, b2):
        import jax, jax.numpy as jnp
        import numpy as np
        import math
        B, L, D = (2, 512, 192)
        H, DK = (8, 64)
        DV = D // H
        N_POS = 32
        DFF = 2 * D
        EPS = 1e-05

        def _rel_basis(l: int, n: int) -> jnp.ndarray:
            pos = jnp.arange(l)
            distance = pos[None, :] - pos[:, None]
            pow_rate = jnp.exp(jnp.log(jnp.float32((l + 1) / 2.0)) / (n // 2))
            center_widths = pow_rate ** jnp.arange(1, n // 2 + 1, dtype=jnp.float32)
            d = distance[:, :, None].astype(jnp.float32)
            unsigned = (jnp.abs(d) <= center_widths).astype(jnp.float32)
            signed = jnp.sign(d) * unsigned
            return jnp.concatenate([unsigned, signed], axis=-1)

        def _rmsnorm(x, w):
            norm = jnp.mean(x * x, axis=-1, keepdims=True)
            return x * jax.lax.rsqrt(norm + EPS) * w
        b, l, _ = x.shape
        skip = x
        h1 = _rmsnorm(x, norm1_w)
        q = (h1 @ wq).reshape(b, l, H, DK)
        k = (h1 @ wk).reshape(b, l, H, DK)
        v = (h1 @ wv).reshape(b, l, H, DV)
        basis = _rel_basis(l, N_POS)
        scale = 1.0 / math.sqrt(DK)
        qw = jnp.einsum('bihd,hdn->bihn', q, w_pos)
        qr = jnp.einsum('bihn,ijn->bhij', qw, basis)
        uk = jnp.einsum('hd,bjhd->bhj', u_param, k)[:, :, None, :]
        vw = jnp.einsum('hd,hdn->hn', v_param, w_pos)
        vr = jnp.einsum('hn,ijn->hij', vw, basis)[None]
        bias = (qr + uk + vr) * scale
        scores = jnp.einsum('bihd,bjhd->bhij', q, k) * scale + bias
        attn = jax.nn.softmax(scores, axis=-1)
        out = jnp.einsum('bhij,bjhd->bihd', attn, v)
        out = out.reshape(b, l, H * DV) @ wo + bo
        x = out + skip
        skip = x
        h2 = _rmsnorm(x, norm2_w)
        h2 = jax.nn.gelu(h2 @ w1 + b1, approximate=False) @ w2 + b2
        return h2 + skip

    def _L0_ffn_ref(x, switch_w, switch_b, w1, b1, w2, b2):
        import jax, jax.numpy as jnp
        import numpy as np
        CAPACITY_FACTOR = 1.25
        B, S, D = x.shape
        E = w1.shape[0]
        xf = x.reshape(-1, D)
        N = xf.shape[0]
        capacity = int(CAPACITY_FACTOR * N / E)
        probs = jax.nn.softmax(xf @ switch_w + switch_b, axis=-1)
        prob_max = jnp.max(probs, axis=-1)
        routes = jnp.argmax(probs, axis=-1)
        sort_idx = jnp.lexsort((-prob_max, routes))
        counts = jnp.bincount(routes, length=E)
        starts = jnp.concatenate([jnp.zeros((1,), counts.dtype), jnp.cumsum(counts)[:-1]])
        rank_sorted = jnp.arange(N) - starts[routes[sort_idx]]
        rank = jnp.zeros((N,), jnp.int32).at[sort_idx].set(rank_sorted.astype(jnp.int32))
        keep = rank < capacity
        dest_e = jnp.where(keep, routes, E)
        dest_c = jnp.where(keep, rank, 0)
        buf = jnp.zeros((E + 1, capacity, D), xf.dtype).at[dest_e, dest_c].set(xf)
        h = jax.nn.gelu(jnp.einsum('ecd,edf->ecf', buf[:E], w1) + b1[:, None, :], approximate=False)
        o = jnp.einsum('ecf,efd->ecd', h, w2) + b2[:, None, :]
        y_exp = o[routes, dest_c]
        y = jnp.where(keep[:, None], y_exp, xf)
        out = y * prob_max[:, None]
        return out.reshape(B, S, D)

    def _L1_attn_ref(x, Wq, bq, Wk, bk, Wv, bv, Wp, bp):
        import jax, jax.numpy as jnp
        import numpy as np
        import math
        N_EMBD = 192
        N_HEAD = 12
        HEAD_DIM = N_EMBD // N_HEAD

        def rope_cache(T, dim):
            inv_freq = 1.0 / 10000.0 ** (2.0 * jnp.arange(dim // 2, dtype=jnp.float32) / dim)
            angles = jnp.arange(T, dtype=jnp.float32)[:, None] * inv_freq[None, :]
            return jnp.stack((jnp.cos(angles), jnp.sin(angles)), axis=-1)

        def apply_rope(x, rope):
            B, H, T, D = x.shape
            xp = x.reshape(B, H, T, D // 2, 2)
            x1, x2 = (xp[..., 0], xp[..., 1])
            cos = rope[None, None, :, :, 0]
            sin = rope[None, None, :, :, 1]
            out = jnp.stack((x1 * cos - x2 * sin, x1 * sin + x2 * cos), axis=-1)
            return out.reshape(B, H, T, D)
        B, T, C = x.shape
        H, D = (N_HEAD, HEAD_DIM)

        def heads(W, b):
            return (x @ W.T + b).reshape(B, T, H, D).transpose(0, 2, 1, 3)
        q = heads(Wq, bq)
        k = heads(Wk, bk)
        v = heads(Wv, bv)
        rope = rope_cache(T, D)
        q = apply_rope(q, rope)
        k = apply_rope(k, rope)
        att = jnp.einsum('bhqd,bhkd->bhqk', q, k) * (1.0 / math.sqrt(D))
        causal = jnp.tril(jnp.ones((T, T), dtype=bool))
        att = jnp.where(causal[None, None], att, -jnp.inf)
        att = jax.nn.softmax(att, axis=-1)
        y = jnp.einsum('bhqk,bhkd->bhqd', att, v)
        y = y.transpose(0, 2, 1, 3).reshape(B, T, C)
        return y @ Wp.T + bp

    def _L1_ffn_ref(hidden_states, g1, b1, g2, b2, Wr, br, Wq, bq, Wk, bk, Wv, bv, Wo, bo, Wm, bm, W1, bf1, W2, bf2):
        import jax, jax.numpy as jnp
        import numpy as np
        B, L, D, H, F = (4, 512, 192, 12, 768)
        ROUTE_FRAC = 0.15
        LN_EPS = 1e-05

        def _ln(x, g, b):
            m = jnp.mean(x, axis=-1, keepdims=True)
            v = jnp.mean((x - m) ** 2, axis=-1, keepdims=True)
            return (x - m) * jax.lax.rsqrt(v + LN_EPS) * g + b
        b, l, d = hidden_states.shape
        dh = d // H
        normed = _ln(hidden_states, g1, b1)
        scores = jax.nn.sigmoid(jnp.einsum('bld,d->bl', normed, Wr) + br)
        k = max(1, int(round(ROUTE_FRAC * l)))
        _, idx = jax.lax.top_k(-scores, k)
        attn_mask = jnp.zeros((b, l), bool).at[jnp.arange(b)[:, None], idx].set(True)
        q = (normed @ Wq + bq).reshape(b, l, H, dh)
        kk = (normed @ Wk + bk).reshape(b, l, H, dh)
        v = (normed @ Wv + bv).reshape(b, l, H, dh)
        logits = jnp.einsum('blhd,bmhd->bhlm', q, kk) / jnp.sqrt(jnp.float32(dh))
        probs = jax.nn.softmax(logits, axis=-1)
        ctx = jnp.einsum('bhlm,bmhd->blhd', probs, v).reshape(b, l, d)
        attn_out = ctx @ Wo + bo
        w = scores / (jnp.sum(scores, axis=1, keepdims=True) + 1e-06)
        pooled = jnp.einsum('bl,bld->bd', w, normed)
        mix_out = (normed + scores[..., None] * pooled[:, None, :]) @ Wm + bm
        merged = jnp.where(attn_mask[..., None], attn_out, mix_out)
        h = hidden_states + merged
        n2 = _ln(h, g2, b2)
        ffn = jax.nn.gelu(n2 @ W1 + bf1, approximate=False) @ W2 + bf2
        return h + ffn
    h = _L0_tok_ref(x, L0_tok_W, L0_tok_b)
    h = h + _L0_attn_ref(_layernorm(h, axis=-1), L0_attn_norm1_w, L0_attn_norm2_w, L0_attn_wq, L0_attn_wk, L0_attn_wv, L0_attn_wo, L0_attn_bo, L0_attn_u_param, L0_attn_v_param, L0_attn_w_pos, L0_attn_w1, L0_attn_b1, L0_attn_w2, L0_attn_b2)
    h = h + _L0_ffn_ref(_layernorm(h, axis=-1), L0_ffn_switch_w, L0_ffn_switch_b, L0_ffn_w1, L0_ffn_b1, L0_ffn_w2, L0_ffn_b2)
    h = h + _L1_attn_ref(_layernorm(h, axis=-1), L1_attn_Wq, L1_attn_bq, L1_attn_Wk, L1_attn_bk, L1_attn_Wv, L1_attn_bv, L1_attn_Wp, L1_attn_bp)
    h = h + _L1_ffn_ref(_layernorm(h, axis=-1), L1_ffn_g1, L1_ffn_b1, L1_ffn_g2, L1_ffn_b2, L1_ffn_Wr, L1_ffn_br, L1_ffn_Wq, L1_ffn_bq, L1_ffn_Wk, L1_ffn_bk, L1_ffn_Wv, L1_ffn_bv, L1_ffn_Wo, L1_ffn_bo, L1_ffn_Wm, L1_ffn_bm, L1_ffn_W1, L1_ffn_bf1, L1_ffn_W2, L1_ffn_bf2)
    return h

_drawn_inputs = setup_inputs


def setup_inputs(seed=0):
    import zlib

    import numpy as np

    out = dict(_drawn_inputs(seed))
    spreads = {'L0_attn_norm1_w': (1.0, 0.6),
     'L0_attn_norm2_w': (1.0, 0.6),
     'L0_attn_bo': (0.0, 0.1),
     'L0_attn_b1': (0.0, 0.732),
     'L0_attn_b2': (0.0, 0.1),
     'L0_ffn_switch_b': (0.0, 0.4),
     'L0_ffn_b1': (0.0, 0.8),
     'L0_ffn_b2': (0.0, 0.8),
     'L1_attn_bq': (0.0, 0.8),
     'L1_attn_bk': (0.0, 0.8),
     'L1_attn_bv': (0.0, 0.604),
     'L1_attn_bp': (0.0, 0.308),
     'L1_ffn_g1': (1.0, 0.6),
     'L1_ffn_b1': (0.0, 0.594),
     'L1_ffn_g2': (1.0, 0.6),
     'L1_ffn_b2': (0.0, 2.0),
     'L1_ffn_bq': (0.0, 0.8),
     'L1_ffn_bk': (0.0, 2.0),
     'L1_ffn_bv': (0.0, 0.8),
     'L1_ffn_bo': (0.0, 1.832),
     'L1_ffn_bm': (0.0, 0.726),
     'L1_ffn_bf1': (0.0, 0.8),
     'L1_ffn_bf2': (0.0, 0.643)}
    factors = {'L0_tok_b': 5.221,
     'L0_attn_wq': 8.0,
     'L0_attn_wk': 8.0,
     'L0_attn_wv': 8.0,
     'L0_attn_wo': 8.0,
     'L0_attn_u_param': 8.0,
     'L0_attn_v_param': 8.0,
     'L0_attn_w_pos': 8.0,
     'L0_ffn_w1': 7.161,
     'L0_ffn_w2': 6.685,
     'L1_attn_Wq': 8.0,
     'L1_attn_Wk': 8.0,
     'L1_attn_Wv': 7.116,
     'L1_attn_Wp': 3.614,
     'L1_ffn_Wq': 8.0,
     'L1_ffn_Wk': 8.0,
     'L1_ffn_Wv': 8.0,
     'L1_ffn_Wo': 8.0,
     'L1_ffn_W1': 2.772}
    for name, (base, spread) in spreads.items():
        noise = np.random.default_rng([zlib.crc32(name.encode()), seed]).standard_normal(out[name].shape)
        drawn = base * np.exp(spread * noise) if base else spread * noise
        out[name] = jnp.asarray(drawn.astype(out[name].dtype))
    for name, factor in factors.items():
        out[name] = (out[name] * factor).astype(out[name].dtype)
    return out
```

```python
from contextlib import ExitStack

import concourse.bass as bass
from concourse import mybir

FP32 = mybir.dt.float32
INT32 = mybir.dt.int32
ALU = mybir.AluOpType
ACT = mybir.ActivationFunctionType
AX = mybir.AxisListType

IMAGES, SEQ, D = 64, 196, 192
T = 98
F = 96
FB = F + 1
COLS = 2 * IMAGES
TOKENS = IMAGES * SEQ
ROUNDS = IMAGES // 2
H0, DK0, DV0, NPOS = 8, 64, 24, 32
BAND = 197
PITCH = 294
E, HID = 8, 768
CAPACITY = int(1.25 * TOKENS / E)
SLOTS = 2048
BATCH = 512
ROWS = E * SLOTS + TOKENS
H1N, DH = 12, 16
K_ROUTED = max(1, int(round(0.15 * SEQ)))
EPS = 1e-5


def spread(ap, axis, n):
    dims = [list(d) for d in ap.ap]
    dims.insert(axis, [0, n])
    return bass.AP(tensor=ap.tensor, offset=ap.offset, ap=dims)


class Link:

    def __init__(self, eng, sem, per_round):
        self.eng, self.sem, self.per, self.i, self.n = eng, sem, per_round, 0, 0

    def round(self, i):
        assert self.n in (0, self.per), (self.sem, self.n)
        self.i, self.n = i, 0

    def __call__(self, ins):
        self.n += 1
        ins.then_inc(self.sem, 1)
        self.eng.wait_ge(self.sem, self.i * self.per + self.n)

    def end(self):
        assert self.n == self.per, f"links in a round: {self.n}, not {self.per}"


def allocators(nc, ctx):
    def sb(name, shape, dt=FP32):
        return ctx.enter_context(nc.sbuf_tensor(name, shape, dt))

    def sb2(name, shape, dt=FP32):
        return [sb(f"{name}_{im}", shape, dt) for im in range(2)]

    taken = []

    def sem(name):
        taken.append(nc.alloc_semaphore(name=name))
        return taken[-1]

    def hand_back():
        nc.clear_and_free_semaphores(taken)
        nc.all_engine_barrier()

    ctx.callback(hand_back)

    def sem2(name):
        return [sem(f"{name}_{im}") for im in range(2)]

    return sb, sb2, sem, sem2


def load_all(sp, pairs, arrived):
    for tile, dram in pairs:
        sp.dma_start(tile, dram).then_inc(arrived, 16)
    sp.wait_ge(arrived, 16 * len(pairs))


def stage_a(nc, dr):
    with ExitStack() as ctx:
        sb, sb2, sem, sem2 = allocators(nc, ctx)
        ident = sb("a_ident", [128, 128])
        basis = sb("a_basis", [128, BAND])
        we = sb("a_we", [128, 6, D])
        be = sb("a_be", [1, D])
        ones_row = sb("a_ones_row", [1, 128])
        zero = sb("a_zero", [128, 1356])
        half = sb("a_half", [T, 2])
        eps = sb("a_eps", [T, 2])
        wq = sb("a_wq", [FB, 2, H0 * DK0])
        wk = sb("a_wk", [FB, 2, H0 * DK0])
        wv = sb("a_wv", [FB, 2, D])
        wqp = sb("a_wqp", [FB, 2, H0 * NPOS])
        wo = sb("a_wo", [FB, 2, D])
        w1 = sb("a_w1", [FB, 2, 2 * D])
        w2 = sb("a_w2", [128, 3, D])
        b2 = sb("a_b2", [1, D])
        ws = sb("a_ws", [FB, 2, E])
        n1 = sb("a_n1", [F, 2])
        n2 = sb("a_n2", [F, 2])
        wq_t = sb("a_wq_t", [DK0, H0, D])
        wpos = sb("a_wpos", [DK0, H0, NPOS])
        vpar = sb("a_vpar", [DK0, H0])
        vw = sb("a_vw", [1, H0 * NPOS])

        xin = sb2("a_xin", [128, 6, SEQ])
        h0 = sb2("a_h0", [T, 2, D])
        xn = sb2("a_xn", [T, 2, D])
        xr = sb2("a_xr", [T, 2, D])
        st = sb2("a_st", [T, 2, 6])
        mv = sb2("a_mv", [T, 2, 2])
        sm = sb2("a_sm", [T, 8, 2])
        hT = sb2("a_hT", [FB, 2, SEQ])
        qT = sb2("a_qT", [128, 4, SEQ])
        kT = sb2("a_kT", [128, 4, SEQ])
        qwT = sb2("a_qwT", [128, 2, SEQ])
        vx = sb2("a_vx", [T, 2, H0, DV0 + 1])
        band = sb2("a_band", [T, H0, 2 * BAND])
        pos = sb2("a_pos", [T, H0, 2 * SEQ])
        s_sb = sb2("a_s", [T, 4, 2 * SEQ])
        mx = sb2("a_mx", [T, H0])
        nmx = sb2("a_nmx", [T, H0])
        pT = sb2("a_pT", [T, 4, 2 * SEQ])
        rs = sb2("a_rs", [T, 2, 4])
        o_sb = sb2("a_o", [T, 2, D])
        x1 = sb2("a_x1", [T, 2, D])
        gT = sb2("a_gT", [128, 3, SEQ])
        h1 = sb2("a_h1", [T, 2, D])
        xf = sb2("a_xf", [T, 2, D])
        lg = sb2("a_lg", [T, 2, E])
        ps = [ctx.enter_context(nc.psum_tensor(f"a_ps{im}", [128, 4, 512], FP32)) for im in range(2)]

        weights_in = sem("a_weights_in")
        vw_done = sem("a_vw_done")
        wqp_done = sem("a_wqp_done")
        wqp_copied = sem("a_wqp_copied")
        vw_placed = sem("a_vw_placed")
        consts_set = sem("a_consts_set")
        pads_zero = sem("a_pads_zero")
        rows_zero = sem("a_rows_zero")
        v_link = sem("a_v_link")
        fence = sem("a_fence")
        p_link = sem("a_p_link")
        x_in = sem2("a_x_in")
        embedded = sem2("a_embedded")
        stats = sem2("a_stats")
        rstd = sem2("a_rstd")
        normed = sem2("a_normed")
        flipped = sem2("a_flipped")
        feat = sem2("a_feat")
        q_proj = sem2("a_q_proj")
        qw_proj = sem2("a_qw_proj")
        v_proj = sem2("a_v_proj")
        k_proj = sem2("a_k_proj")
        q_copied = sem2("a_q_copied")
        qw_copied = sem2("a_qw_copied")
        v_copied = sem2("a_v_copied")
        k_copied = sem2("a_k_copied")
        band_done = sem2("a_band_done")
        band_copied = sem2("a_band_copied")
        band_out = sem2("a_band_out")
        pos_in = sem2("a_pos_in")
        scored = sem2("a_scored")
        added = sem2("a_added")
        maxed = sem2("a_maxed")
        exped = sem2("a_exped")
        p_flipped = sem2("a_p_flipped")
        p_copied = sem2("a_p_copied")
        pv_done = sem2("a_pv_done")
        o_done = sem2("a_o_done")
        projected = sem2("a_projected")
        x1_done = sem2("a_x1_done")
        up_done = sem2("a_up_done")
        gelued = sem2("a_gelued")
        down_done = sem2("a_down_done")
        h1_done = sem2("a_h1_done")
        logits = sem2("a_logits")
        lg_done = sem2("a_lg_done")
        out_sent = sem2("a_out_sent")

        block = ctx.enter_context(nc.Block())

        @block.sync
        def _(sp):
            load_all(sp, [(ident[:], dr["ident"]), (basis[:], dr["basis"]), (we[:], dr["we"]), (be[:], dr["be"]),
                          (wq[:], dr["wq"]), (wk[:], dr["wk"]), (wv[:], dr["wv"]), (wo[:], dr["wo"]),
                          (w1[:], dr["w1"]), (w2[:], dr["w2"]), (b2[:], dr["b2"]), (ws[:], dr["ws"]),
                          (n1[:], dr["n1"]), (n2[:], dr["n2"]), (wq_t[:], dr["wq_t"]), (wpos[:], dr["wpos"]),
                          (vpar[:], dr["vpar"])], weights_in)
            sp.wait_ge(wqp_copied, 3)
            sp.dma_start(wqp[F:FB, 1, :], vw[0:1, :]).then_inc(vw_placed, 16)
            sp.wait_ge(consts_set, 8)
            for im in range(2):
                sp.dma_start(dr["band"][im].rearrange("p (a f) -> p a f", f=1176),
                             spread(zero[0:T, 0:1176], 1, 4)).then_inc(pads_zero, 16)
            sp.wait_ge(pads_zero, 32)
            for im in range(2):
                sp.sem_inc(embedded[im], 1)
                sp.sem_inc(added[im], 2)
            with sp.Fori(0, ROUNDS) as i:
                for im in range(2):
                    sp.wait_ge(embedded[im], i + 1)
                    sp.dma_start(xin[im][:], dr["x"][bass.ds(2 * i + im, 1)].rearrange("a p k n -> (a p) k n")
                                 ).then_inc(x_in[im], 16)
                sp.dma_start(dr["rows_flat"][bass.ds(i, 1)].rearrange("a p f -> (a p) f"), zero[:]).then_inc(rows_zero, 16)
                for im in range(2):
                    sp.wait_ge(band_copied[im], 2 * i + 2)
                    sp.dma_start(dr["band_skew"][im], band[im][:].rearrange("p h (c b) -> p (h c) b", c=2)
                                 ).then_inc(band_out[im], 16)
                for im in range(2):
                    sp.wait_ge(band_out[im], 16 * i + 32)
                    sp.wait_ge(added[im], 2 * i + 2)
                    sp.dma_start(pos[im][:], dr["band_read"][im]).then_inc(pos_in[im], 16)
                for im in range(2):
                    img = 2 * i + im
                    sp.wait_ge(h1_done[im], i + 1)
                    sp.dma_start(dr["h1"][bass.ds(img, 1)].rearrange("a p f -> (a p) f"),
                                 h1[im][:].rearrange("p c f -> p (c f)")).then_inc(out_sent[im], 16)
                    sp.wait_ge(normed[im], 3 * i + 3)
                    sp.dma_start(dr["xf"][bass.ds(img, 1)].rearrange("a p f -> (a p) f"),
                                 xf[im][:].rearrange("p c f -> p (c f)")).then_inc(out_sent[im], 16)
                    sp.wait_ge(lg_done[im], i + 2)
                    sp.dma_start(dr["lg"][bass.ds(img, 1)].rearrange("a p f -> (a p) f"),
                                 lg[im][:].rearrange("p c f -> p (c f)")).then_inc(out_sent[im], 16)
            sp.wait_ge(rows_zero, 16 * ROUNDS)
            for im in range(2):
                sp.wait_ge(out_sent[im], 48 * ROUNDS + 48)

        @block.gpsimd
        def _(pool):
            pool.memset(zero[:], 0.0).then_inc(consts_set, 1)
            pool.memset(half[:], -0.5).then_inc(consts_set, 1)
            pool.memset(eps[:], EPS).then_inc(consts_set, 1)
            pool.wait_ge(consts_set, 8)
            link = Link(pool, p_link, 20)
            with pool.Fori(0, ROUNDS) as i:
                link.round(i)
                for im in range(2):
                    s, var = sm[im], mv[im][:, :, 1]
                    pool.wait_ge(stats[im], 3 * i + 1)
                    link(pool.tensor_tensor(s[:, 0, :], var, eps[:], ALU.add))
                    link(pool.tensor_tensor(s[:, 1, :], s[:, 0, :], half[:], ALU.pow))
                    link(pool.tensor_tensor(s[:, 2, :], s[:, 1, :], s[:, 1, :], ALU.mult))
                    link(pool.tensor_tensor(s[:, 3, :], s[:, 2, :], var, ALU.mult))
                    link(pool.tensor_tensor(s[:, 4, :], s[:, 3, :], eps[:], ALU.add))
                    link(pool.tensor_tensor(s[:, 5, :], s[:, 4, :], half[:], ALU.pow))
                    pool.tensor_tensor(s[:, 6, :], s[:, 5, :], s[:, 1, :], ALU.mult).then_inc(rstd[im], 1)
                for im in range(2):
                    s, mean, var = sm[im], mv[im][:, :, 0], mv[im][:, :, 1]
                    pool.wait_ge(stats[im], 3 * i + 2)
                    link(pool.tensor_tensor(s[:, 0, :], mean, mean, ALU.mult))
                    link(pool.tensor_tensor(s[:, 2, :], s[:, 0, :], var, ALU.add))
                    link(pool.tensor_tensor(s[:, 3, :], s[:, 2, :], eps[:], ALU.add))
                    pool.tensor_tensor(s[:, 1, :], s[:, 3, :], half[:], ALU.pow).then_inc(rstd[im], 1)
                for im in range(2):
                    s, var = sm[im], mv[im][:, :, 1]
                    pool.wait_ge(stats[im], 3 * i + 3)
                    link(pool.tensor_tensor(s[:, 0, :], var, eps[:], ALU.add))
                    pool.tensor_tensor(s[:, 1, :], s[:, 0, :], half[:], ALU.pow).then_inc(rstd[im], 1)
                link.end()

        @block.scalar
        def _(act):
            act.wait_ge(weights_in, 16 * 17)
            act.wait_ge(consts_set, 8)
            for im in range(2):
                act.sem_inc(band_out[im], 16)
            with act.Fori(0, ROUNDS) as i:
                for im in range(2):
                    act.wait_ge(flipped[im], 4 * i + 1)
                    act.activation(hT[im][0:F, 0, :], ps[im][0:F, 1, 0:SEQ], ACT.Identity, scale=n1[:, 0:1])
                    act.activation(hT[im][0:F, 1, :], ps[im][0:F, 1, SEQ:2 * SEQ], ACT.Identity,
                                   scale=n1[:, 1:2]).then_inc(feat[im], 1)
                for im in range(2):
                    act.wait_ge(q_proj[im], i + 1)
                    act.activation(qT[im][:].rearrange("p (b m) n -> p b (m n)", b=2), ps[im][:, 2:4, 0:2 * SEQ],
                                   ACT.Copy).then_inc(q_copied[im], 1)
                for im in range(2):
                    act.wait_ge(k_proj[im], i + 1)
                    act.activation(kT[im][:].rearrange("p (b m) n -> p b (m n)", b=2), ps[im][:, 2:4, 0:2 * SEQ],
                                   ACT.Copy).then_inc(k_copied[im], 1)
                for g in range(2):
                    for im in range(2):
                        act.wait_ge(band_done[im], 2 * i + g + 1)
                        if g == 0:
                            act.wait_ge(band_out[im], 16 * i + 16)
                        act.activation(band[im][:, 4 * g:4 * g + 4, :], ps[im][0:T, :, 0:2 * BAND],
                                       ACT.Copy).then_inc(band_copied[im], 1)
                for g in range(2):
                    for im in range(2):
                        act.wait_ge(maxed[im], 2 * i + g + 1)
                        for hh in range(4):
                            for c in range(2):
                                part = s_sb[im][:, hh, c * SEQ:(c + 1) * SEQ]
                                last = act.activation(part, part, ACT.Exp, scale=DK0 ** -0.5,
                                                      bias=nmx[im][:, 2 * hh + c:2 * hh + c + 1])
                        last.then_inc(exped[im], 1)
                    for im in range(2):
                        act.wait_ge(p_flipped[im], 2 * i + g + 1)
                        act.activation(pT[im][:, 2:4, :], ps[im][0:T, 2:4, 0:2 * SEQ], ACT.Copy).then_inc(p_copied[im], 1)
                for im in range(2):
                    act.wait_ge(flipped[im], 4 * i + 2)
                    act.activation(hT[im][0:F, :, :].rearrange("p k n -> p (k n)"), ps[im][0:F, 1, 0:2 * SEQ],
                                   ACT.Copy).then_inc(feat[im], 1)
                for im in range(2):
                    act.wait_ge(flipped[im], 4 * i + 3)
                    act.activation(hT[im][0:F, 0, :], ps[im][0:F, 1, 0:SEQ], ACT.Identity, scale=n2[:, 0:1])
                    act.activation(hT[im][0:F, 1, :], ps[im][0:F, 1, SEQ:2 * SEQ], ACT.Identity,
                                   scale=n2[:, 1:2]).then_inc(feat[im], 1)
                for im in range(2):
                    act.wait_ge(up_done[im], i + 1)
                    act.activation(gT[im][:, 0:2, :].rearrange("p m n -> p (m n)"), ps[im][:, 2, 0:2 * SEQ], ACT.Gelu)
                    act.activation(gT[im][:, 2, :], ps[im][:, 3, 0:SEQ], ACT.Gelu).then_inc(gelued[im], 1)
                for im in range(2):
                    act.wait_ge(flipped[im], 4 * i + 4)
                    act.activation(hT[im][0:F, :, :].rearrange("p k n -> p (k n)"), ps[im][0:F, 1, 0:2 * SEQ],
                                   ACT.Copy).then_inc(feat[im], 1)

        @block.tensor
        def _(pe):
            pe.wait_ge(weights_in, 16 * 17)
            pe.wait_ge(consts_set, 8)
            for k in range(2):
                for h in range(H0):
                    last = pe.matmul(ps[0][0:F, k, h * NPOS:(h + 1) * NPOS], wq_t[:, h, F * k:F * k + F],
                                     wpos[:, h, :], start=True, stop=True)
            last.then_inc(wqp_done, 1)
            for h in range(H0):
                last = pe.matmul(ps[0][0:1, 2, h * NPOS:(h + 1) * NPOS], vpar[:, h:h + 1],
                                 wpos[:, h, :], start=True, stop=True)
            last.then_inc(vw_done, 1)
            pe.wait_ge(wqp_copied, 3)
            pe.wait_ge(vw_placed, 16)

            def flip(im, src, bank):
                for k in range(2):
                    for c in range(2):
                        last = pe.transpose(ps[im][0:F, bank, k * SEQ + c * T:k * SEQ + (c + 1) * T],
                                            src[:, c, k * F:(k + 1) * F], ident[0:T, 0:T])
                last.then_inc(flipped[im], 1)

            def to_tokens(im, bank, w, n, done):
                for c in range(2):
                    for k in range(2):
                        last = pe.matmul(ps[im][0:T, bank, c * n:(c + 1) * n], hT[im][:, k, c * T:(c + 1) * T],
                                         w[:, k, :], start=(k == 0), stop=(k == 1))
                last.then_inc(done[im], 1)

            def to_features(im, banks, w, done):
                for m in range(w.shape[2] // 128):
                    at = (m % 2) * SEQ
                    for k in range(2):
                        last = pe.matmul(ps[im][:, banks[m // 2], at:at + SEQ], w[:, k, m * 128:(m + 1) * 128],
                                         hT[im][:, k, :], start=(k == 0), stop=(k == 1))
                last.then_inc(done[im], 1)

            for im in range(2):
                pe.sem_inc(lg_done[im], 1)
            with pe.Fori(0, ROUNDS) as i:
                for im in range(2):
                    pe.wait_ge(x_in[im], 16 * i + 16)
                    pe.wait_ge(lg_done[im], i + 1)
                    for c in range(2):
                        out = ps[im][0:T, 0, c * D:(c + 1) * D]
                        for k in range(6):
                            pe.matmul(out, xin[im][:, k, c * T:(c + 1) * T], we[:, k, :], start=(k == 0), stop=False)
                        last = pe.matmul(out, ones_row[0:1, 0:T], be[0:1, :], start=False, stop=True)
                    last.then_inc(embedded[im], 1)
                for im in range(2):
                    pe.wait_ge(normed[im], 3 * i + 1)
                    flip(im, xr[im], 1)
                for im in range(2):
                    pe.wait_ge(feat[im], 4 * i + 1)
                    to_features(im, (2, 3), wq, q_proj)
                    to_tokens(im, 0, wv, D, v_proj)
                    to_features(im, (1,), wqp, qw_proj)
                for im in range(2):
                    pe.wait_ge(q_copied[im], i + 1)
                    to_features(im, (2, 3), wk, k_proj)
                for g in range(2):
                    for im in range(2):
                        if g == 0:
                            pe.wait_ge(qw_copied[im], i + 1)
                            pe.wait_ge(v_copied[im], i + 1)
                            pe.wait_ge(k_copied[im], i + 1)
                        else:
                            pe.wait_ge(band_copied[im], 2 * i + 1)
                        for hh in range(4):
                            at = slice(32 * hh, 32 * hh + 32)
                            for c in range(2):
                                last = pe.matmul(ps[im][0:T, hh, c * BAND:(c + 1) * BAND],
                                                 qwT[im][at, g, c * T:(c + 1) * T], basis[at, :], start=True, stop=True)
                        last.then_inc(band_done[im], 1)
                for g in range(2):
                    for im in range(2):
                        if g == 0:
                            pe.wait_ge(band_copied[im], 2 * i + 2)
                        else:
                            pe.wait_ge(o_done[im], 2 * i + 1)
                        for hh in range(4):
                            h = 4 * g + hh
                            at = slice(64 * (h % 2), 64 * (h % 2) + 64)
                            for c in range(2):
                                last = pe.matmul(ps[im][0:T, hh, c * SEQ:(c + 1) * SEQ],
                                                 qT[im][at, h // 2, c * T:(c + 1) * T], kT[im][at, h // 2, :],
                                                 start=True, stop=True)
                        last.then_inc(scored[im], 1)
                    for im in range(2):
                        pe.wait_ge(exped[im], 2 * i + g + 1)
                        for hh in range(4):
                            for cj in range(2):
                                for ci in range(2):
                                    last = pe.transpose(ps[im][0:T, hh, cj * SEQ + ci * T:cj * SEQ + (ci + 1) * T],
                                                        s_sb[im][:, hh, ci * SEQ + cj * T:ci * SEQ + (cj + 1) * T],
                                                        ident[0:T, 0:T])
                        last.then_inc(p_flipped[im], 1)
                    for im in range(2):
                        pe.wait_ge(p_copied[im], 4 * i + 2 * g + 2)
                        for ci in range(2):
                            for hh in range(4):
                                at = (4 * ci + hh) * (DV0 + 1)
                                for cj in range(2):
                                    last = pe.matmul(ps[im][0:T, 0, at:at + DV0 + 1],
                                                     pT[im][:, hh, cj * SEQ + ci * T:cj * SEQ + (ci + 1) * T],
                                                     vx[im][:, cj, 4 * g + hh, :], start=(cj == 0), stop=(cj == 1))
                        last.then_inc(pv_done[im], 1)
                for im in range(2):
                    pe.wait_ge(o_done[im], 2 * i + 2)
                    flip(im, o_sb[im], 1)
                for im in range(2):
                    pe.wait_ge(feat[im], 4 * i + 2)
                    to_tokens(im, 2, wo, D, projected)
                for im in range(2):
                    pe.wait_ge(normed[im], 3 * i + 2)
                    flip(im, xr[im], 1)
                for im in range(2):
                    pe.wait_ge(feat[im], 4 * i + 3)
                    to_features(im, (2, 3), w1, up_done)
                for im in range(2):
                    pe.wait_ge(gelued[im], i + 1)
                    for c in range(2):
                        out = ps[im][0:T, 0, c * D:(c + 1) * D]
                        for m in range(3):
                            pe.matmul(out, gT[im][:, m, c * T:(c + 1) * T], w2[:, m, :], start=(m == 0), stop=False)
                        last = pe.matmul(out, ones_row[0:1, 0:T], b2[0:1, :], start=False, stop=True)
                    last.then_inc(down_done[im], 1)
                for im in range(2):
                    pe.wait_ge(normed[im], 3 * i + 3)
                    flip(im, xf[im], 1)
                for im in range(2):
                    pe.wait_ge(feat[im], 4 * i + 4)
                    to_tokens(im, 2, ws, E, logits)

        @block.vector
        def _(dve):
            dve.memset(ones_row[:], 1.0).then_inc(consts_set, 1)
            for im in range(2):
                dve.memset(hT[im][F:FB, :, :], 1.0).then_inc(consts_set, 1)
                dve.memset(vx[im][:, :, :, DV0:DV0 + 1], 1.0).then_inc(consts_set, 1)
            dve.memset(wqp[F:FB, 0, :], 0.0)
            dve.wait_ge(wqp_done, 1)
            for k in range(2):
                dve.tensor_copy(wqp[0:F, k, :], ps[0][0:F, k, 0:H0 * NPOS]).then_inc(wqp_copied, 1)
            dve.wait_ge(vw_done, 1)
            dve.tensor_copy(vw[0:1, :], ps[0][0:1, 2, 0:H0 * NPOS]).then_inc(wqp_copied, 1)
            for im in range(2):
                dve.sem_inc(out_sent[im], 48)
            link = Link(dve, v_link, 18)

            def statistics(im, rows):
                dve.bn_stats(st[im][:, 0, :], rows[:, 0, :])
                link(dve.bn_stats(st[im][:, 1, :], rows[:, 1, :]))
                dve.sem_inc(fence, 1)
                dve.bn_aggr(mv[im][:, 0, :], st[im][:, 0, :])
                dve.bn_aggr(mv[im][:, 1, :], st[im][:, 1, :]).then_inc(stats[im], 1)

            with dve.Fori(0, ROUNDS) as i:
                link.round(i)
                for im in range(2):
                    dve.wait_ge(embedded[im], i + 2)
                    link(dve.tensor_copy(h0[im][:].rearrange("p c f -> p (c f)"), ps[im][0:T, 0, 0:2 * D]))
                    statistics(im, h0[im])
                for im in range(2):
                    dve.wait_ge(rstd[im], 3 * i + 1)
                    for c in range(2):
                        last = dve.tensor_scalar(xr[im][:, c, :], h0[im][:, c, :], mv[im][:, c, 0:1],
                                                 sm[im][:, 6, c:c + 1], ALU.subtract, ALU.mult)
                    last.then_inc(normed[im], 1)
                    for c in range(2):
                        dve.tensor_scalar(xn[im][:, c, :], h0[im][:, c, :], mv[im][:, c, 0:1],
                                          sm[im][:, 1, c:c + 1], ALU.subtract, ALU.mult)
                for im in range(2):
                    dve.wait_ge(v_proj[im], i + 1)
                    dve.tensor_copy(vx[im][:, :, :, 0:DV0],
                                    ps[im][0:T, 0, 0:2 * D].rearrange("p (c h d) -> p c h d", c=2, d=DV0)
                                    ).then_inc(v_copied[im], 1)
                    dve.wait_ge(qw_proj[im], i + 1)
                    dve.tensor_copy(qwT[im][:].rearrange("p m n -> p (m n)"), ps[im][:, 1, 0:2 * SEQ]
                                    ).then_inc(qw_copied[im], 1)
                for g in range(2):
                    for im in range(2):
                        dve.wait_ge(scored[im], 2 * i + g + 1)
                        if g == 0:
                            dve.wait_ge(pos_in[im], 16 * i + 16)
                        dve.tensor_tensor(s_sb[im][:], ps[im][0:T, :, 0:2 * SEQ], pos[im][:, 4 * g:4 * g + 4, :],
                                          ALU.add).then_inc(added[im], 1)
                        dve.wait_ge(added[im], 2 * i + g + 3)
                        link(dve.tensor_reduce(mx[im][:], s_sb[im][:].rearrange("p h (c j) -> p (h c) j", c=2),
                                               AX.X, ALU.max))
                        dve.tensor_scalar(nmx[im][:], mx[im][:], -(DK0 ** -0.5), None, ALU.mult).then_inc(maxed[im], 1)
                    for im in range(2):
                        dve.wait_ge(p_flipped[im], 2 * i + g + 1)
                        dve.tensor_copy(pT[im][:, 0:2, :], ps[im][0:T, 0:2, 0:2 * SEQ]).then_inc(p_copied[im], 1)
                    for im in range(2):
                        dve.wait_ge(pv_done[im], 2 * i + g + 1)
                        o_ps = ps[im][0:T, 0, 0:8 * (DV0 + 1)].rearrange("p (c h d) -> p c h d", c=2, d=DV0 + 1)
                        link(dve.reciprocal(rs[im][:], o_ps[:, :, :, DV0]))
                        dve.tensor_tensor(o_sb[im][:, :, g * F:(g + 1) * F].rearrange("p c (h d) -> p c h d", d=DV0),
                                          o_ps[:, :, :, 0:DV0], spread(rs[im][:], 3, DV0), ALU.mult
                                          ).then_inc(o_done[im], 1)
                for im in range(2):
                    dve.wait_ge(projected[im], i + 1)
                    link(dve.tensor_tensor(x1[im][:].rearrange("p c f -> p (c f)"), ps[im][0:T, 2, 0:2 * D],
                                           xn[im][:].rearrange("p c f -> p (c f)"), ALU.add))
                    statistics(im, x1[im])
                for im in range(2):
                    dve.wait_ge(rstd[im], 3 * i + 2)
                    for c in range(2):
                        last = dve.tensor_scalar(xr[im][:, c, :], x1[im][:, c, :], sm[im][:, 1, c:c + 1], None, ALU.mult)
                    last.then_inc(normed[im], 1)
                    dve.tensor_tensor(xn[im][:], x1[im][:], h0[im][:], ALU.add).then_inc(x1_done[im], 1)
                for im in range(2):
                    dve.wait_ge(down_done[im], i + 1)
                    dve.wait_ge(x1_done[im], i + 1)
                    dve.wait_ge(out_sent[im], 48 * i + 48)
                    dve.tensor_tensor(h1[im][:].rearrange("p c f -> p (c f)"), ps[im][0:T, 0, 0:2 * D],
                                      xn[im][:].rearrange("p c f -> p (c f)"), ALU.add).then_inc(h1_done[im], 1)
                    dve.wait_ge(h1_done[im], i + 1)
                    statistics(im, h1[im])
                for im in range(2):
                    dve.wait_ge(rstd[im], 3 * i + 3)
                    for c in range(2):
                        last = dve.tensor_scalar(xf[im][:, c, :], h1[im][:, c, :], mv[im][:, c, 0:1],
                                                 sm[im][:, 1, c:c + 1], ALU.subtract, ALU.mult)
                    last.then_inc(normed[im], 1)
                for im in range(2):
                    dve.wait_ge(logits[im], i + 1)
                    dve.tensor_copy(lg[im][:].rearrange("p c e -> p (c e)"), ps[im][0:T, 2, 0:2 * E]).then_inc(lg_done[im], 1)
                link.end()


def stage_b(nc, dr, scattered):
    W = E * COLS
    with ExitStack() as ctx:
        sb, sb2, sem, sem2 = allocators(nc, ctx)
        lg = sb("b_lg", [T, COLS, E])
        ex = sb("b_ex", [T, COLS, E])
        top = sb("b_top", [T, COLS])
        gain = sb("b_gain", [T, COLS])
        total = sb("b_total", [T, COLS])
        order = sb("b_order", [T, E])
        offset = sb("b_offset", [T, E])
        spare = sb("b_spare", [T, COLS])
        before = sb("b_before", [T, T])
        ones = sb("b_ones", [T, T])
        flat1 = sb("b_flat1", [T, W])
        mine = sb("b_mine", [T, E, COLS])
        own = sb("b_own", [T, E, COLS])
        hit = sb("b_hit", [T, E, COLS])
        above = sb("b_above", [T, E, COLS])
        tie = sb("b_tie", [T, E, COLS])
        keep = sb("b_keep", [T, E, COLS])
        sums = sb("b_sums", [T, E, COLS])
        rank = sb("b_rank", [T, E, COLS])
        base = sb("b_base", [T, E])
        cnt = sb("b_cnt", [T, E])
        need = sb("b_need", [T, E])
        bit_f = sb("b_bit_f", [T, E])
        bit_i = sb("b_bit_i", [T, E], INT32)
        cand = sb("b_cand", [T, E], INT32)
        won = sb("b_won", [T, E], INT32)
        bound = sb("b_bound", [T, E], INT32)
        kept = sb("b_kept", [T, COLS])
        slot_f = sb("b_slot_f", [T, COLS])
        slot = sb("b_slot", [T, COLS], INT32)
        xrow = [sb(f"b_xrow{n}", [T, 2, D]) for n in range(4)]
        idx = [sb(f"b_idx{n}", [T, 2], INT32) for n in range(4)]
        ps = ctx.enter_context(nc.psum_tensor("b_ps", [128, 8, 512], FP32))
        ps_pre = ps[0:T, 0:2, :].rearrange("p b n -> p (b n)")
        ps_tot = ps[0:T, 2:4, :].rearrange("p b n -> p (b n)")
        ps_cnt = ps[0:T, 4, 0:E]
        ps_above = ps[0:T, 5, 0:E]

        loaded = sem("b_loaded")
        shifted = sem("b_shifted")
        exped = sem("b_exped")
        v_link = sem("b_v_link")
        s_link = sem("b_s_link")
        counted = sem("b_counted")
        summed = sem("b_summed")
        above_counted = sem("b_above_counted")
        above_summed = sem("b_above_summed")
        marked = sem("b_marked")
        prefixed = sem("b_prefixed")
        slots_done = sem("b_slots_done")
        tables_out = sem("b_tables_out")
        fence = sem("b_fence")
        x_in = [sem(f"b_x_in{n}") for n in range(4)]
        idx_done = [sem(f"b_idx_done{n}") for n in range(4)]
        row_free = [sem(f"b_row_free{n}") for n in range(4)]
        BITS = 30

        block = ctx.enter_context(nc.Block())

        @block.sync
        def _(sp):
            load_all(sp, [(lg[:].rearrange("p (i c) e -> p i (c e)", c=2), dr["lg"].rearrange("i p f -> p i f")),
                          (order[:], dr["order"]), (offset[:], dr["offset"]), (spare[:], dr["spare"]),
                          (before[:], dr["before"]), (ones[:], dr["ones"])], loaded)
            sp.wait_ge(slots_done, 1)
            sp.dma_start(dr["slot"], slot[:]).then_inc(tables_out, 16)
            sp.dma_start(dr["gain"], gain[:]).then_inc(tables_out, 16)
            with sp.Fori(0, IMAGES // 4) as i:
                for n in range(4):
                    sp.wait_ge(row_free[n], i + 1)
                    sp.dma_start(xrow[n][:].rearrange("p c f -> p (c f)"),
                                 dr["xf"][bass.ds(4 * i + n, 1)].rearrange("a p f -> (a p) f")).then_inc(x_in[n], 16)
            sp.wait_ge(tables_out, 32)

        @block.gpsimd
        def _(pool):
            pool.wait_ge(slots_done, 1)
            for n in range(4):
                pool.sem_inc(row_free[n], 1)
            with pool.Fori(0, IMAGES // 4) as i:
                for n in range(4):
                    pool.tensor_copy(idx[n][:], slot[:, bass.ds(8 * i + 2 * n, 2)]).then_inc(idx_done[n], 1)
                for n in range(4):
                    pool.wait_ge(x_in[n], 16 * i + 16)
                    pool.wait_ge(idx_done[n], i + 1)
                    pool.sem_inc(fence, 1)
                    for c in range(2):
                        pool.indirect_dma_start(out=dr["rows"], out_offset=bass.IndirectOffsetOnAxis(
                            ap=idx[n][:, c:c + 1], axis=0), in_=xrow[n][:, c, :], in_offset=None
                            ).then_inc(scattered[n], 16)
                for n in range(4):
                    pool.wait_ge(scattered[n], 32 * i + 32)
                    pool.sem_inc(row_free[n], 1)

        @block.scalar
        def _(act):
            act.wait_ge(shifted, 1)
            act.activation(ex[:], ex[:], ACT.Exp).then_inc(exped, 1)

        @block.tensor
        def _(pe):
            pe.wait_ge(loaded, 16 * 6)
            with pe.Fori(0, BITS) as i:
                pe.wait_ge(counted, i + 1)
                pe.matmul(ps_cnt, ones[:], cnt[:], start=True, stop=True).then_inc(summed, 1)
            pe.wait_ge(above_counted, 1)
            pe.matmul(ps_above, ones[:], cnt[:], start=True, stop=True).then_inc(above_summed, 1)
            for n, marks in enumerate((tie, keep)):
                flat = marks[:].rearrange("p e c -> p (e c)")
                pe.wait_ge(marked, n + 1)
                for b in range(2):
                    at = slice(512 * b, 512 * b + 512)
                    pe.matmul(ps_pre[:, at], before[:], flat[:, at], start=True, stop=True)
                    last = pe.matmul(ps_tot[:, at], ones[:], flat[:, at], start=True, stop=True)
                last.then_inc(prefixed, 1)

        @block.vector
        def _(dve):
            link = Link(dve, v_link, 0)
            link.per = None

            def vlink(ins):
                link.n += 1
                ins.then_inc(v_link, 1)
                dve.wait_ge(v_link, link.n)

            def cols(ap):
                return ap.rearrange("p e c -> p c e")

            dve.memset(flat1[:], 1.0)
            dve.memset(bound[:], 0)
            dve.memset(bit_f[:], float(2 ** (BITS - 1)))
            dve.wait_ge(loaded, 16 * 6)
            vlink(dve.tensor_reduce(top[:], lg[:], AX.X, ALU.max))
            dve.tensor_tensor(ex[:], lg[:], spread(top[:], 2, E), ALU.subtract).then_inc(shifted, 1)
            dve.wait_ge(exped, 1)
            dve.tensor_reduce(total[:], ex[:], AX.X, ALU.add)
            vlink(dve.tensor_reduce(top[:], ex[:], AX.X, ALU.max))
            dve.reciprocal(gain[:], total[:])
            vlink(dve.tensor_tensor(cols(mine[:]), ex[:], spread(top[:], 2, E), ALU.is_equal))
            vlink(dve.tensor_tensor(cols(hit[:]), cols(mine[:]), spread(order[:], 1, COLS), ALU.mult))
            vlink(dve.tensor_reduce(top[:], cols(hit[:]), AX.X, ALU.max))
            vlink(dve.tensor_tensor(mine[:], hit[:], spread(top[:], 1, E), ALU.is_equal))
            vlink(dve.tensor_tensor(own[:], mine[:], spread(gain[:], 1, E), ALU.mult))
            step = Link(dve, s_link, 6)
            with dve.Fori(0, BITS) as i:
                step.round(i)
                step(dve.tensor_copy(bit_i[:], bit_f[:]))
                step(dve.tensor_tensor(cand[:], bound[:], bit_i[:], ALU.bitwise_or))
                step(dve.tensor_tensor(hit[:], own[:], spread(cand[:].bitcast(FP32), 2, COLS), ALU.is_ge))
                dve.tensor_reduce(cnt[:], hit[:], AX.X, ALU.add).then_inc(counted, 1)
                dve.wait_ge(summed, i + 1)
                step(dve.scalar_tensor_tensor(won[:], ps_cnt, float(CAPACITY), bit_f[:], ALU.is_ge, ALU.mult))
                step(dve.tensor_tensor(bound[:], bound[:], won[:], ALU.bitwise_or))
                step(dve.tensor_scalar(bit_f[:], bit_f[:], 0.5, None, ALU.mult))
                step.end()
            level = spread(bound[:].bitcast(FP32), 2, COLS)
            dve.tensor_tensor(above[:], own[:], level, ALU.is_gt)
            vlink(dve.tensor_tensor(hit[:], own[:], level, ALU.is_equal))
            dve.tensor_reduce(cnt[:], above[:], AX.X, ALU.add).then_inc(above_counted, 1)
            dve.tensor_tensor(tie[:], hit[:], mine[:], ALU.mult).then_inc(marked, 1)
            dve.wait_ge(above_summed, 1)
            vlink(dve.tensor_scalar(need[:], ps_above, -1.0, float(CAPACITY), ALU.mult, ALU.add))

            def prefix(n):
                dve.wait_ge(prefixed, n)
                flat = sums[:].rearrange("p e c -> p (e c)")
                out = rank[:].rearrange("p e c -> p (e c)")
                vlink(dve.tensor_tensor_scan(flat, flat1[:], ps_tot, 0.0, ALU.mult, ALU.add))
                vlink(dve.tensor_tensor(flat, flat, ps_tot, ALU.subtract))
                dve.tensor_copy(base[:], sums[:, :, 0])
                vlink(dve.tensor_tensor(out, flat, ps_pre, ALU.add))
                vlink(dve.tensor_tensor(rank[:], rank[:], spread(base[:], 2, COLS), ALU.subtract))

            prefix(1)
            vlink(dve.tensor_tensor(hit[:], rank[:], spread(need[:], 2, COLS), ALU.is_lt))
            vlink(dve.tensor_tensor(hit[:], hit[:], tie[:], ALU.mult))
            dve.tensor_tensor(keep[:], hit[:], above[:], ALU.add).then_inc(marked, 1)
            prefix(2)
            vlink(dve.tensor_tensor(rank[:], rank[:], spread(offset[:], 2, COLS), ALU.add))
            dve.tensor_reduce(kept[:], cols(keep[:]), AX.X, ALU.add)
            vlink(dve.tensor_tensor(hit[:], rank[:], keep[:], ALU.mult))
            vlink(dve.tensor_reduce(slot_f[:], cols(hit[:]), AX.X, ALU.add))
            vlink(dve.tensor_tensor(total[:], kept[:], spare[:], ALU.mult))
            vlink(dve.tensor_tensor(slot_f[:], slot_f[:], total[:], ALU.subtract))
            dve.tensor_tensor(slot[:], slot_f[:], spare[:], ALU.add).then_inc(slots_done, 1)


def stage_c(nc, dr, y_out):
    PER = SLOTS // BATCH
    SUB = BATCH // 128
    M = HID // 128
    with ExitStack() as ctx:
        sb, sb2, sem, sem2 = allocators(nc, ctx)
        ident = sb("c_ident", [128, 128])
        ones_row = sb("c_ones_row", [1, 128])
        w1 = sb2("c_w1", [FB, 2, HID])
        w2 = sb2("c_w2", [128, M, D])
        b2 = sb2("c_b2", [1, D])
        xs = sb2("c_xs", [128, SUB, D])
        xT = sb2("c_xT", [FB, 2, BATCH])
        gT = sb2("c_gT", [128, M, BATCH])
        yo = sb2("c_yo", [128, SUB, D])
        ps = ctx.enter_context(nc.psum_tensor("c_ps", [128, 8, 512], FP32))
        UP, DOWN, UPS = 2, 6, 4

        loaded = sem("c_loaded")
        ones_set = sem("c_ones_set")
        w_in = sem2("c_w_in")
        w_free = sem2("c_w_free")
        x_in = sem2("c_x_in")
        flipped = sem2("c_flipped")
        xT_done = sem2("c_xT_done")
        up_done = sem("c_up_done")
        gelued = sem("c_gelued")
        down_done = sem("c_down_done")
        y_done = sem("c_y_done")
        yo_free = sem2("c_yo_free")

        view = dr["rows"][0:E * SLOTS, :].rearrange("(n p s) f -> n p (s f)", p=128, s=SUB)
        batches = [(e2, b) for e2 in range(2) for b in range(PER)]
        NB = len(batches)
        block = ctx.enter_context(nc.Block())

        @block.sync
        def _(sp):
            sp.dma_start(ident[:], dr["ident"]).then_inc(loaded, 16)
            for e2 in range(2):
                sp.sem_inc(w_free[e2], 1)
                sp.sem_inc(flipped[e2], 1)
            with sp.Fori(0, E // 2) as i:
                for n, (e2, b) in enumerate(batches):
                    if b == 0:
                        e = 2 * i + e2
                        sp.wait_ge(w_free[e2], i + 1)
                        sp.dma_start(w1[e2][:], dr["we1"][bass.ds(e, 1)].rearrange("a p k m -> (a p) k m")).then_inc(w_in[e2], 16)
                        sp.dma_start(w2[e2][:], dr["we2"][bass.ds(e, 1)].rearrange("a p k m -> (a p) k m")).then_inc(w_in[e2], 16)
                        sp.dma_start(b2[e2][:], dr["be2"][bass.ds(e, 1)]).then_inc(w_in[e2], 16)
                    sp.wait_ge(flipped[n % 2], i * (NB // 2) + n // 2 + 1)
                    sp.dma_start(xs[n % 2][:].rearrange("p s f -> p (s f)"),
                                 view[bass.ds(NB * i + n, 1)].rearrange("a p f -> (a p) f")).then_inc(x_in[n % 2], 16)

        @block.gpsimd
        def _(pool):
            pool.sem_inc(yo_free[0], 1)
            pool.sem_inc(yo_free[1], 1)
            with pool.Fori(0, E // 2) as i:
                for n in range(NB):
                    pool.wait_ge(y_done, i * NB + n + 2)
                    pool.dma_start(view[bass.ds(NB * i + n, 1)].rearrange("a p f -> (a p) f"),
                                   yo[n % 2][:].rearrange("p s f -> p (s f)")).then_inc(y_out[n % 2], 16)
                    pool.wait_ge(y_out[n % 2], 16 * (i * (NB // 2) + n // 2 + 1))
                    pool.sem_inc(yo_free[n % 2], 1)

        @block.scalar
        def _(act):
            with act.Fori(0, E // 2) as i:
                for n in range(NB):
                    for m in range(M):
                        at = n * M + m
                        act.wait_ge(up_done, i * NB * M + at + 1)
                        act.activation(gT[n % 2][:, m, :], ps[:, UP + at % UPS, :], ACT.Gelu).then_inc(gelued, 1)

        @block.tensor
        def _(pe):
            pe.wait_ge(loaded, 16)
            pe.wait_ge(ones_set, 3)
            pe.sem_inc(gelued, UPS)
            pe.sem_inc(y_done, 1)

            def flip(i, n):
                pe.wait_ge(x_in[n % 2], 16 * (i * (NB // 2) + n // 2 + 1))
                for k in range(2):
                    for s in range(SUB):
                        last = pe.transpose(ps[0:F, k, s * 128:(s + 1) * 128], xs[n % 2][:, s, k * F:(k + 1) * F], ident[:])
                last.then_inc(flipped[n % 2], 1)

            with pe.Fori(0, E // 2) as i:
                for n, (e2, b) in enumerate(batches):
                    if n == 0:
                        flip(i, 0)
                    if b == 0:
                        pe.wait_ge(w_in[e2], 48 * i + 48)
                    pe.wait_ge(xT_done[n % 2], i * (NB // 2) + n // 2 + 1)
                    for m in range(M):
                        at = n * M + m
                        pe.wait_ge(gelued, i * NB * M + at + 1)
                        for k in range(2):
                            last = pe.matmul(ps[:, UP + at % UPS, :], w1[e2][:, k, m * 128:(m + 1) * 128],
                                             xT[n % 2][:, k, :], start=(k == 0), stop=(k == 1))
                        last.then_inc(up_done, 1)
                    if n + 1 < NB:
                        flip(i, n + 1)
                    pe.wait_ge(gelued, i * NB * M + (n + 1) * M + UPS)
                    pe.wait_ge(y_done, i * NB + n + 1)
                    for s in range(SUB):
                        out = ps[:, DOWN + s // 2, (s % 2) * D:(s % 2 + 1) * D]
                        for m in range(M):
                            pe.matmul(out, gT[n % 2][:, m, s * 128:(s + 1) * 128], w2[e2][:, m, :],
                                      start=(m == 0), stop=False)
                        last = pe.matmul(out, ones_row[0:1, :], b2[e2][0:1, :], start=False, stop=True)
                    last.then_inc(down_done, 1)
                    if b == PER - 1:
                        pe.sem_inc(w_free[e2], 1)

        @block.vector
        def _(dve):
            dve.memset(ones_row[:], 1.0).then_inc(ones_set, 1)
            for q in range(2):
                dve.memset(xT[q][F:FB, :, :], 1.0).then_inc(ones_set, 1)

            def features(i, n):
                dve.wait_ge(flipped[n % 2], i * (NB // 2) + n // 2 + 2)
                dve.tensor_copy(xT[n % 2][0:F, :, :], ps[0:F, 0:2, :]).then_inc(xT_done[n % 2], 1)

            with dve.Fori(0, E // 2) as i:
                for n in range(NB):
                    if n == 0:
                        features(i, 0)
                    if n + 1 < NB:
                        features(i, n + 1)
                    dve.wait_ge(down_done, i * NB + n + 1)
                    dve.wait_ge(yo_free[n % 2], i * (NB // 2) + n // 2 + 1)
                    dve.tensor_copy(yo[n % 2][:].rearrange("p (b s) f -> p b (s f)", b=2), ps[:, DOWN:DOWN + 2, 0:2 * D]
                                    ).then_inc(y_done, 1)


def stage_d(nc, dr, gathered):
    KR = K_ROUTED
    G4 = 3 * KR
    CW = 3 * T
    HG = 4 * 32
    with ExitStack() as ctx:
        sb, sb2, sem, sem2 = allocators(nc, ctx)
        ident = sb("d_ident", [128, 128])
        ones_row = sb("d_ones_row", [1, 128])
        half = sb("d_half", [T, 2])
        eps = sb("d_eps", [T, 2])
        rope = sb("d_rope", [128, 2, SEQ])
        causal = sb("d_causal", [T, CW])
        earlier = sb("d_earlier", [T, 2, SEQ])
        places = sb("d_places", [T, KR])
        blocks = sb("d_blocks", [F, 2, 6, KR])
        wq = sb("d_wq", [FB, 2, 2, 3 * HG])
        wk = sb("d_wk", [FB, 2, 2, 3 * HG])
        wv = sb("d_wv", [FB, 2, D])
        wp = sb("d_wp", [FB, 2, D])
        wr = sb("d_wr", [FB, 2, 1])
        uq = sb("d_uq", [FB, 2, D])
        uk = sb("d_uk", [FB, 2, D])
        uv = sb("d_uv", [FB, 2, D])
        uo = sb("d_uo", [FB, 2, D])
        um = sb("d_um", [FB, 2, D])
        w1 = sb("d_w1", [FB, 2, HID])
        w2 = sb("d_w2", [128, 6, D])
        b2 = sb("d_b2", [1, D])
        g1 = sb("d_g1", [F, 2])
        c1 = sb("d_c1", [F, 2])
        g2 = sb("d_g2", [F, 2])
        c2 = sb("d_c2", [F, 2])

        h1 = sb2("d_h1", [T, 2, D])
        yx = sb2("d_yx", [T, 2, D])
        idx = sb2("d_idx", [T, 2], INT32)
        gain = sb2("d_gain", [T, 2])
        h2 = sb2("d_h2", [T, 2, D])
        st = sb2("d_st", [T, 2, 6])
        mv = sb2("d_mv", [T, 2, 2])
        sm = sb2("d_sm", [T, 7, 2])
        xr = sb2("d_xr", [T, 2, D])
        aT = sb2("d_aT", [FB, 2, SEQ])
        rot = sb2("d_rot", [128, 3, 2, SEQ])
        qT = sb2("d_qT", [128, 3, SEQ])
        kT = sb2("d_kT", [128, 3, SEQ])
        vx = sb2("d_vx", [T, 2, H1N, DH + 1])
        s_sb = sb2("d_s", [T, 4, CW])
        mx = sb2("d_mx", [T, 4, 2])
        nmx = sb2("d_nmx", [T, 4, 2])
        pT = sb2("d_pT", [T, 4, CW])
        rs = sb2("d_rs", [T, 2, 4])
        o_sb = sb2("d_o", [T, 2, D])
        h3 = sb2("d_h3", [T, 2, D])
        hid = sb2("d_hid", [T, 2, D])
        nT = sb2("d_nT", [FB, 2, SEQ])
        kT2 = sb2("d_kT2", [F, 2, SEQ])
        v2 = sb2("d_v2", [T, 2, D])
        sg = sb2("d_sg", [T, 2])
        score = sb2("d_score", [T, 2])
        wide = sb2("d_wide", [T, 2, T])
        srow = sb2("d_srow", [T, SEQ])
        junk = sb2("d_junk", [T, SEQ])
        less = sb2("d_less", [T, 2])
        ties = sb2("d_ties", [T, 2])
        rank = sb2("d_rank", [T, 2])
        away = sb2("d_away", [T, 2])
        sel = sb2("d_sel", [T, 2, KR])
        selT = sb2("d_selT", [KR, SEQ])
        ssum = sb2("d_ssum", [T, 1])
        pool_r = sb2("d_pool_r", [F, 2])
        pool_t = sb2("d_pool_t", [F, 2])
        mT = sb2("d_mT", [FB, 2, SEQ])
        xq = sb2("d_xq", [FB, 2, KR])
        qb = sb2("d_qb", [F, 2, 6, KR])
        mx2 = sb2("d_mx2", [G4, 4])
        nmx2 = sb2("d_nmx2", [G4, 4])
        p2 = sb2("d_p2", [G4, 4, SEQ])
        sum2 = sb2("d_sum2", [G4, 4])
        rs2 = sb2("d_rs2", [G4, 4])
        pT2 = sb2("d_pT2", [T, 4, 2, G4])
        cb = sb2("d_cb", [F, 2, 6, KR])
        cT = sb2("d_cT", [FB, 2, KR])
        ao = sb2("d_ao", [KR, D])
        hm = sb2("d_hm", [T, 2, D])
        gT = sb2("d_gT", [128, 6, SEQ])
        y = sb2("d_y", [T, 2, D])
        ps = [ctx.enter_context(nc.psum_tensor(f"d_ps{im}", [128, 4, 512], FP32)) for im in range(2)]

        weights = [(ident, "ident"), (rope, "rope"), (causal, "causal"), (earlier, "earlier"), (places, "places"),
                   (blocks, "blocks"), (wq, "dq"), (wk, "dk"), (wv, "dv"), (wp, "dp"), (wr, "wr"), (uq, "uq"),
                   (uk, "uk"), (uv, "uv"), (uo, "uo"), (um, "um"), (w1, "u1"), (w2, "u2"), (b2, "ub2"),
                   (g1, "g1"), (c1, "c1"), (g2, "g2"), (c2, "c2")]
        W_IN = 16 * len(weights)
        CONSTS = 13
        weights_in = sem("d_weights_in")
        consts_set = sem("d_consts_set")
        v_link = sem("d_v_link")
        p_link = sem("d_p_link")
        fence = sem("d_fence")
        rows_in = sem2("d_rows_in")
        h2_done = sem2("d_h2_done")
        stats = sem2("d_stats")
        rstd = sem2("d_rstd")
        normed = sem2("d_normed")
        flipped = sem2("d_flipped")
        feat = sem2("d_feat")
        q_proj = sem2("d_q_proj")
        v_proj = sem2("d_v_proj")
        k_proj = sem2("d_k_proj")
        turned = sem2("d_turned")
        q_done = sem2("d_q_done")
        k_done = sem2("d_k_done")
        v_copied = sem2("d_v_copied")
        scored = sem2("d_scored")
        masked = sem2("d_masked")
        maxed = sem2("d_maxed")
        exped = sem2("d_exped")
        p_flipped = sem2("d_p_flipped")
        p_copied = sem2("d_p_copied")
        pv_done = sem2("d_pv_done")
        o_done = sem2("d_o_done")
        projected = sem2("d_projected")
        z_done = sem2("d_z_done")
        z_exped = sem2("d_z_exped")
        kv2_proj = sem2("d_kv2_proj")
        kv2_copied = sem2("d_kv2_copied")
        wide_done = sem2("d_wide_done")
        srow_done = sem2("d_srow_done")
        sel_done = sem2("d_sel_done")
        mix_in = sem2("d_mix_in")
        mixed = sem2("d_mixed")
        picked = sem2("d_picked")
        xq_copied = sem2("d_xq_copied")
        selT_copied = sem2("d_selT_copied")
        q2_proj = sem2("d_q2_proj")
        qb_done = sem2("d_qb_done")
        scored2 = sem2("d_scored2")
        maxed2 = sem2("d_maxed2")
        exped2 = sem2("d_exped2")
        p2_done = sem2("d_p2_done")
        p2_flipped = sem2("d_p2_flipped")
        p2_copied = sem2("d_p2_copied")
        pv2_done = sem2("d_pv2_done")
        c_done = sem2("d_c_done")
        ao_proj = sem2("d_ao_proj")
        ao_copied = sem2("d_ao_copied")
        placed = sem2("d_placed")
        up_done = sem2("d_up_done")
        gelued = sem2("d_gelued")
        down_done = sem2("d_down_done")
        y_done = sem2("d_y_done")
        y_out = sem2("d_y_out")

        block = ctx.enter_context(nc.Block())

        @block.sync
        def _(sp):
            load_all(sp, [(tile[:], dr[name]) for tile, name in weights], weights_in)
            with sp.Fori(0, ROUNDS) as i:
                for im in range(2):
                    img = 2 * i + im
                    sp.wait_ge(h2_done[im], i + 1)
                    sp.dma_start(idx[im][:], dr["slot"][:, bass.ds(2 * img, 2)]).then_inc(rows_in[im], 16)
                    sp.dma_start(gain[im][:], dr["gain"][:, bass.ds(2 * img, 2)]).then_inc(rows_in[im], 16)
                    sp.dma_start(h1[im][:].rearrange("p c f -> p (c f)"),
                                 dr["h1"][bass.ds(img, 1)].rearrange("a p f -> (a p) f")).then_inc(rows_in[im], 16)
                for im in range(2):
                    sp.wait_ge(y_done[im], i + 2)
                    sp.dma_start(dr["out"][bass.ds(2 * i + im, 1)].rearrange("a c p f -> p (a c) f"),
                                 y[im][:]).then_inc(y_out[im], 16)
            for im in range(2):
                sp.wait_ge(y_out[im], 16 * ROUNDS + 16)

        @block.gpsimd
        def _(pool):
            pool.memset(half[:], -0.5).then_inc(consts_set, 1)
            pool.memset(eps[:], EPS).then_inc(consts_set, 1)
            pool.wait_ge(consts_set, CONSTS)
            for im in range(2):
                pool.sem_inc(h2_done[im], 1)
            link = Link(pool, p_link, 16)

            def deviation(i, n, im):
                pool.wait_ge(stats[im], 3 * i + n)
                link(pool.tensor_tensor(sm[im][:, 0, :], mv[im][:, :, 1], eps[:], ALU.add))
                pool.tensor_tensor(sm[im][:, 1, :], sm[im][:, 0, :], half[:], ALU.pow).then_inc(rstd[im], 1)

            with pool.Fori(0, ROUNDS) as i:
                link.round(i)
                for im in range(2):
                    pool.wait_ge(rows_in[im], 48 * i + 48)
                    pool.sem_inc(fence, 1)
                    for c in range(2):
                        pool.indirect_dma_start(out=yx[im][:, c, :], out_offset=None, in_=dr["rows"],
                                                in_offset=bass.IndirectOffsetOnAxis(ap=idx[im][:, c:c + 1], axis=0)
                                                ).then_inc(gathered[im], 16)
                for im in range(2):
                    deviation(i, 1, im)
                for im in range(2):
                    pool.wait_ge(turned[im], 2 * i + 1)
                    pool.tensor_tensor(qT[im][:], rot[im][:, :, 0, :], rot[im][:, :, 1, :], ALU.add).then_inc(q_done[im], 1)
                for im in range(2):
                    pool.wait_ge(turned[im], 2 * i + 2)
                    pool.tensor_tensor(kT[im][:], rot[im][:, :, 0, :], rot[im][:, :, 1, :], ALU.add).then_inc(k_done[im], 1)
                for im in range(2):
                    s, var = sm[im], mv[im][:, :, 1]
                    pool.wait_ge(stats[im], 3 * i + 2)
                    link(pool.tensor_tensor(s[:, 0, :], var, eps[:], ALU.add))
                    link(pool.tensor_tensor(s[:, 1, :], s[:, 0, :], half[:], ALU.pow))
                    link(pool.tensor_tensor(s[:, 2, :], s[:, 1, :], s[:, 1, :], ALU.mult))
                    link(pool.tensor_tensor(s[:, 3, :], s[:, 2, :], var, ALU.mult))
                    link(pool.tensor_tensor(s[:, 4, :], s[:, 3, :], eps[:], ALU.add))
                    link(pool.tensor_tensor(s[:, 5, :], s[:, 4, :], half[:], ALU.pow))
                    pool.tensor_tensor(s[:, 6, :], s[:, 5, :], s[:, 1, :], ALU.mult).then_inc(rstd[im], 1)
                for im in range(2):
                    deviation(i, 3, im)
                link.end()

        @block.scalar
        def _(act):
            act.wait_ge(weights_in, W_IN)
            act.wait_ge(consts_set, CONSTS)

            def features(i, n, im, bank, out, g=None, b=None):
                act.wait_ge(flipped[im], 4 * i + n)
                if g is None:
                    act.activation(out[0:F, :, :].rearrange("p k n -> p (k n)"), ps[im][0:F, bank, 0:2 * SEQ],
                                   ACT.Copy).then_inc(feat[im], 1)
                else:
                    for k in range(2):
                        last = act.activation(out[0:F, k, :], ps[im][0:F, bank, k * SEQ:(k + 1) * SEQ], ACT.Identity,
                                              scale=g[:, k:k + 1], bias=b[:, k:k + 1])
                    last.then_inc(feat[im], 1)

            with act.Fori(0, ROUNDS) as i:
                for im in range(2):
                    features(i, 1, im, 3, aT[im])
                for im in range(2):
                    act.wait_ge(v_proj[im], i + 1)
                    act.activation(vx[im][:, :, :, 0:DH],
                                   ps[im][0:T, 3, 0:2 * D].rearrange("p (c h d) -> p c h d", c=2, d=DH),
                                   ACT.Copy).then_inc(v_copied[im], 1)
                for g in range(3):
                    for im in range(2):
                        act.wait_ge(maxed[im], 3 * i + g + 1)
                        for hh in range(4):
                            for ci, at in enumerate((slice(0, T), slice(T, CW))):
                                last = act.activation(s_sb[im][:, hh, at], s_sb[im][:, hh, at], ACT.Exp,
                                                      scale=DH ** -0.5, bias=nmx[im][:, hh, ci:ci + 1])
                        last.then_inc(exped[im], 1)
                    for im in range(2):
                        act.wait_ge(p_flipped[im], 3 * i + g + 1)
                        act.activation(pT[im][:, 2:4, :], ps[im][0:T, 2:4, 0:CW], ACT.Copy).then_inc(p_copied[im], 1)
                for im in range(2):
                    features(i, 2, im, 1, aT[im])
                for im in range(2):
                    features(i, 3, im, 0, nT[im], g1, c1)
                for im in range(2):
                    act.wait_ge(z_done[im], i + 1)
                    act.activation(sg[im][:], ps[im][0:T, 1, 0:2], ACT.Exp, scale=-1.0).then_inc(z_exped[im], 1)
                for im in range(2):
                    act.wait_ge(kv2_proj[im], i + 1)
                    act.activation(kT2[im][:].rearrange("p m n -> p (m n)"), ps[im][0:F, 2, 0:2 * SEQ], ACT.Copy)
                    act.activation(v2[im][:].rearrange("p c f -> p (c f)"), ps[im][0:T, 3, 0:2 * D],
                                   ACT.Copy).then_inc(kv2_copied[im], 1)
                for im in range(2):
                    act.wait_ge(picked[im], i + 1)
                    for k in range(2):
                        act.activation(xq[im][0:F, k, :], ps[im][0:F, 2, k * KR:(k + 1) * KR], ACT.Identity,
                                       scale=g1[:, k:k + 1], bias=c1[:, k:k + 1]).then_inc(xq_copied[im], 1)
                    act.activation(selT[im][:], ps[im][0:KR, 3, 0:SEQ], ACT.Copy).then_inc(selT_copied[im], 1)
                for im in range(2):
                    act.wait_ge(maxed2[im], i + 1)
                    for gr in range(4):
                        src = ps[im][0:G4, 1 + 2 * (gr // 2), (gr % 2) * SEQ:(gr % 2 + 1) * SEQ]
                        last = act.activation(p2[im][:, gr, :], src, ACT.Exp, scale=DH ** -0.5,
                                              bias=nmx2[im][:, gr:gr + 1], accum_out=sum2[im][:, gr:gr + 1])
                    last.then_inc(exped2[im], 1)
                for im in range(2):
                    act.wait_ge(p2_flipped[im], i + 1)
                    act.activation(pT2[im][:].rearrange("p (b g) c n -> p b (g c n)", b=2), ps[im][0:T, 1:4:2, 0:4 * G4],
                                   ACT.Copy).then_inc(p2_copied[im], 1)
                for im in range(2):
                    act.wait_ge(ao_proj[im], i + 1)
                    act.activation(ao[im][:], ps[im][0:KR, 1, 0:D], ACT.Copy).then_inc(ao_copied[im], 1)
                for im in range(2):
                    features(i, 4, im, 0, aT[im], g2, c2)
                for im in range(2):
                    act.wait_ge(up_done[im], i + 1)
                    act.activation(gT[im][:].rearrange("p (b m) n -> p b (m n)", m=2), ps[im][:, 1:4, 0:2 * SEQ],
                                   ACT.Gelu).then_inc(gelued[im], 1)

        @block.tensor
        def _(pe):
            pe.wait_ge(weights_in, W_IN)
            pe.wait_ge(consts_set, CONSTS)
            for im in range(2):
                pe.sem_inc(y_done[im], 1)

            def flip(im, src, bank):
                for k in range(2):
                    for c in range(2):
                        last = pe.transpose(ps[im][0:F, bank, k * SEQ + c * T:k * SEQ + (c + 1) * T],
                                            src[:, c, k * F:(k + 1) * F], ident[0:T, 0:T])
                last.then_inc(flipped[im], 1)

            def to_tokens(im, bank, src, w, n):
                for c in range(2):
                    for k in range(2):
                        last = pe.matmul(ps[im][0:T, bank, c * n:(c + 1) * n], src[:, k, c * T:(c + 1) * T],
                                         w[:, k, :], start=(k == 0), stop=(k == 1))
                return last

            def rotary(im, w):
                for m in range(3):
                    for v in range(2):
                        for k in range(2):
                            last = pe.matmul(ps[im][:, m, v * SEQ:(v + 1) * SEQ], w[:, k, v, m * HG:(m + 1) * HG],
                                             aT[im][:, k, :], start=(k == 0), stop=(k == 1))
                return last

            with pe.Fori(0, ROUNDS) as i:
                for im in range(2):
                    pe.wait_ge(normed[im], 3 * i + 1)
                    pe.wait_ge(y_done[im], i + 1)
                    flip(im, xr[im], 3)
                for im in range(2):
                    pe.wait_ge(feat[im], 4 * i + 1)
                    rotary(im, wq).then_inc(q_proj[im], 1)
                    to_tokens(im, 3, aT[im], wv, D).then_inc(v_proj[im], 1)
                for im in range(2):
                    pe.wait_ge(turned[im], 2 * i + 1)
                    rotary(im, wk).then_inc(k_proj[im], 1)
                for g in range(3):
                    for im in range(2):
                        if g == 0:
                            pe.wait_ge(q_done[im], i + 1)
                            pe.wait_ge(k_done[im], i + 1)
                            pe.wait_ge(v_copied[im], i + 1)
                        else:
                            pe.wait_ge(o_done[im], 3 * i + g)
                        for hh in range(4):
                            at = slice(32 * hh, 32 * hh + 32)
                            pe.matmul(ps[im][0:T, hh, 0:T], qT[im][at, g, 0:T], kT[im][at, g, 0:T], start=True, stop=True)
                            last = pe.matmul(ps[im][0:T, hh, T:CW], qT[im][at, g, T:SEQ], kT[im][at, g, :],
                                             start=True, stop=True)
                        last.then_inc(scored[im], 1)
                    for im in range(2):
                        pe.wait_ge(exped[im], 3 * i + g + 1)
                        for hh in range(4):
                            for b in range(3):
                                last = pe.transpose(ps[im][0:T, hh, b * T:(b + 1) * T], s_sb[im][:, hh, b * T:(b + 1) * T],
                                                    ident[0:T, 0:T])
                        last.then_inc(p_flipped[im], 1)
                    for im in range(2):
                        pe.wait_ge(p_copied[im], 6 * i + 2 * g + 2)
                        for ci in range(2):
                            for hh in range(4):
                                at = (4 * ci + hh) * (DH + 1)
                                for cj in range(ci + 1):
                                    b = ci + cj
                                    last = pe.matmul(ps[im][0:T, 0, at:at + DH + 1], pT[im][:, hh, b * T:(b + 1) * T],
                                                     vx[im][:, cj, 4 * g + hh, :], start=(cj == 0), stop=(cj == ci))
                        last.then_inc(pv_done[im], 1)
                for im in range(2):
                    pe.wait_ge(o_done[im], 3 * i + 3)
                    flip(im, o_sb[im], 1)
                for im in range(2):
                    pe.wait_ge(feat[im], 4 * i + 2)
                    to_tokens(im, 2, aT[im], wp, D).then_inc(projected[im], 1)
                for im in range(2):
                    pe.wait_ge(normed[im], 3 * i + 2)
                    flip(im, xr[im], 0)
                for im in range(2):
                    pe.wait_ge(feat[im], 4 * i + 3)
                    to_tokens(im, 1, nT[im], wr, 1).then_inc(z_done[im], 1)
                    for m in range(2):
                        for k in range(2):
                            pe.matmul(ps[im][0:F, 2, m * SEQ:(m + 1) * SEQ], uk[:, k, m * F:(m + 1) * F], nT[im][:, k, :],
                                      start=(k == 0), stop=(k == 1))
                    to_tokens(im, 3, nT[im], uv, D).then_inc(kv2_proj[im], 1)
                for im in range(2):
                    pe.wait_ge(wide_done[im], i + 1)
                    for c in range(2):
                        last = pe.transpose(ps[im][0:T, 1, c * T:(c + 1) * T], wide[im][:, c, :], ident[0:T, 0:T])
                    last.then_inc(srow_done[im], 1)
                for im in range(2):
                    pe.wait_ge(sel_done[im], i + 1)
                    pe.wait_ge(kv2_copied[im], i + 1)
                    for k in range(2):
                        for c in range(2):
                            pe.matmul(ps[im][0:F, 2, k * KR:(k + 1) * KR], xr[im][:, c, k * F:(k + 1) * F],
                                      sel[im][:, c, :], start=(c == 0), stop=(c == 1))
                    for c in range(2):
                        last = pe.transpose(ps[im][0:KR, 3, c * T:(c + 1) * T], sel[im][:, c, :], ident[0:T, 0:T])
                    last.then_inc(picked[im], 1)
                for im in range(2):
                    pe.wait_ge(mix_in[im], i + 1)
                    to_tokens(im, 0, mT[im], um, D).then_inc(mixed[im], 1)
                for im in range(2):
                    pe.wait_ge(xq_copied[im], 2 * i + 2)
                    for m in range(2):
                        for k in range(2):
                            last = pe.matmul(ps[im][0:F, 2, m * KR:(m + 1) * KR], uq[:, k, m * F:(m + 1) * F],
                                             xq[im][:, k, :], start=(k == 0), stop=(k == 1))
                    last.then_inc(q2_proj[im], 1)
                for im in range(2):
                    pe.wait_ge(qb_done[im], i + 1)
                    pe.wait_ge(selT_copied[im], i + 1)
                    for m in range(2):
                        for t in range(2):
                            last = pe.matmul(ps[im][0:G4, 1 + 2 * m, t * SEQ:(t + 1) * SEQ],
                                             qb[im][:, m, 3 * t:3 * t + 3, :].rearrange("p h r -> p (h r)"),
                                             kT2[im][:, m, :], start=True, stop=True)
                    last.then_inc(scored2[im], 1)
                for im in range(2):
                    pe.wait_ge(p2_done[im], i + 1)
                    for gr in range(4):
                        for cj in range(2):
                            at = ((gr % 2) * 2 + cj) * G4
                            last = pe.transpose(ps[im][0:T, 1 + 2 * (gr // 2), at:at + G4],
                                                p2[im][:, gr, cj * T:(cj + 1) * T], ident[0:G4, 0:G4])
                    last.then_inc(p2_flipped[im], 1)
                for im in range(2):
                    pe.wait_ge(p2_copied[im], i + 1)
                    for m in range(2):
                        for cj in range(2):
                            last = pe.matmul(ps[im][0:F, 2, m * 2 * G4:(m + 1) * 2 * G4], v2[im][:, cj, m * F:(m + 1) * F],
                                             pT2[im][:, 2 * m:2 * m + 2, cj, :], start=(cj == 0), stop=(cj == 1))
                    last.then_inc(pv2_done[im], 1)
                for im in range(2):
                    pe.wait_ge(c_done[im], i + 1)
                    for k in range(2):
                        last = pe.matmul(ps[im][0:KR, 1, 0:D], cT[im][:, k, :], uo[:, k, :], start=(k == 0), stop=(k == 1))
                    last.then_inc(ao_proj[im], 1)
                for im in range(2):
                    pe.wait_ge(ao_copied[im], i + 1)
                    for c in range(2):
                        last = pe.matmul(ps[im][0:T, 3, c * D:(c + 1) * D], selT[im][:, c * T:(c + 1) * T], ao[im][:],
                                         start=True, stop=True)
                    last.then_inc(placed[im], 1)
                for im in range(2):
                    pe.wait_ge(normed[im], 3 * i + 3)
                    flip(im, xr[im], 0)
                for im in range(2):
                    pe.wait_ge(feat[im], 4 * i + 4)
                    for m in range(6):
                        at = (m % 2) * SEQ
                        for k in range(2):
                            last = pe.matmul(ps[im][:, 1 + m // 2, at:at + SEQ], w1[:, k, m * 128:(m + 1) * 128],
                                             aT[im][:, k, :], start=(k == 0), stop=(k == 1))
                    last.then_inc(up_done[im], 1)
                for im in range(2):
                    pe.wait_ge(gelued[im], i + 1)
                    for c in range(2):
                        out = ps[im][0:T, 0, c * D:(c + 1) * D]
                        for m in range(6):
                            pe.matmul(out, gT[im][:, m, c * T:(c + 1) * T], w2[:, m, :], start=(m == 0), stop=False)
                        last = pe.matmul(out, ones_row[0:1, 0:T], b2[0:1, :], start=False, stop=True)
                    last.then_inc(down_done[im], 1)

        @block.vector
        def _(dve):
            dve.memset(ones_row[:], 1.0).then_inc(consts_set, 1)
            for im in range(2):
                for tile in (aT, nT, mT, xq):
                    dve.memset(tile[im][F:FB, :, :], 1.0).then_inc(consts_set, 1)
                dve.memset(cT[im][F:FB, :, :], 1.0)
                dve.memset(vx[im][:, :, :, DH:DH + 1], 1.0).then_inc(consts_set, 1)
                dve.sem_inc(y_out[im], 16)
            dve.wait_ge(weights_in, W_IN)
            link = Link(dve, v_link, 62)

            def statistics(im, rows):
                dve.bn_stats(st[im][:, 0, :], rows[:, 0, :])
                link(dve.bn_stats(st[im][:, 1, :], rows[:, 1, :]))
                dve.sem_inc(fence, 1)
                dve.bn_aggr(mv[im][:, 0, :], st[im][:, 0, :])
                dve.bn_aggr(mv[im][:, 1, :], st[im][:, 1, :]).then_inc(stats[im], 1)

            def normalise(i, n, im, rows, scale=1):
                dve.wait_ge(rstd[im], 3 * i + n)
                for c in range(2):
                    last = dve.tensor_scalar(xr[im][:, c, :], rows[:, c, :], mv[im][:, c, 0:1],
                                             sm[im][:, scale, c:c + 1], ALU.subtract, ALU.mult)
                last.then_inc(normed[im], 1)

            def flat(tile):
                return tile[:].rearrange("p c f -> p (c f)")

            with dve.Fori(0, ROUNDS) as i:
                link.round(i)
                for im in range(2):
                    dve.wait_ge(gathered[im], 32 * i + 32)
                    for c in range(2):
                        last = dve.scalar_tensor_tensor(h2[im][:, c, :], yx[im][:, c, :], gain[im][:, c:c + 1],
                                                        h1[im][:, c, :], ALU.mult, ALU.add)
                    last.then_inc(h2_done[im], 1)
                    dve.wait_ge(h2_done[im], i + 2)
                    statistics(im, h2[im])
                for im in range(2):
                    normalise(i, 1, im, h2[im])
                for n, proj in enumerate((q_proj, k_proj)):
                    for im in range(2):
                        dve.wait_ge(proj[im], i + 1)
                        if n == 1:
                            dve.wait_ge(q_done[im], i + 1)
                        dve.tensor_tensor(rot[im][:].rearrange("p m v n -> p m (v n)"), ps[im][:, 0:3, 0:2 * SEQ],
                                          spread(rope[:].rearrange("p v n -> p (v n)"), 1, 3), ALU.mult
                                          ).then_inc(turned[im], 1)
                for g in range(3):
                    for im in range(2):
                        dve.wait_ge(scored[im], 3 * i + g + 1)
                        dve.tensor_tensor(s_sb[im][:], ps[im][0:T, :, 0:CW], spread(causal[:], 1, 4), ALU.add
                                          ).then_inc(masked[im], 1)
                        dve.wait_ge(masked[im], 3 * i + g + 1)
                        dve.tensor_reduce(mx[im][:, :, 0], s_sb[im][:, :, 0:T], AX.X, ALU.max)
                        link(dve.tensor_reduce(mx[im][:, :, 1], s_sb[im][:, :, T:CW], AX.X, ALU.max))
                        dve.tensor_scalar(nmx[im][:], mx[im][:], -(DH ** -0.5), None, ALU.mult).then_inc(maxed[im], 1)
                    for im in range(2):
                        dve.wait_ge(p_flipped[im], 3 * i + g + 1)
                        dve.tensor_copy(pT[im][:, 0:2, :], ps[im][0:T, 0:2, 0:CW]).then_inc(p_copied[im], 1)
                    for im in range(2):
                        dve.wait_ge(pv_done[im], 3 * i + g + 1)
                        o_ps = ps[im][0:T, 0, 0:8 * (DH + 1)].rearrange("p (c h d) -> p c h d", c=2, d=DH + 1)
                        link(dve.reciprocal(rs[im][:], o_ps[:, :, :, DH]))
                        dve.tensor_tensor(o_sb[im][:, :, g * 64:(g + 1) * 64].rearrange("p c (h d) -> p c h d", d=DH),
                                          o_ps[:, :, :, 0:DH], spread(rs[im][:], 3, DH), ALU.mult).then_inc(o_done[im], 1)
                for im in range(2):
                    dve.wait_ge(projected[im], i + 1)
                    link(dve.tensor_tensor(flat(h3[im]), ps[im][0:T, 2, 0:2 * D], flat(h2[im]), ALU.add))
                    statistics(im, h3[im])
                for im in range(2):
                    normalise(i, 2, im, h3[im], scale=6)
                    for c in range(2):
                        dve.tensor_scalar(hid[im][:, c, :], h3[im][:, c, :], mv[im][:, c, 0:1],
                                          sm[im][:, 1, c:c + 1], ALU.subtract, ALU.mult)
                for im in range(2):
                    dve.wait_ge(z_exped[im], i + 1)
                    link(dve.tensor_scalar(sg[im][:], sg[im][:], 1.0, None, ALU.add))
                    link(dve.reciprocal(score[im][:], sg[im][:]))
                    dve.tensor_copy(wide[im][:], spread(score[im][:], 2, T)).then_inc(wide_done[im], 1)
                for im in range(2):
                    dve.wait_ge(srow_done[im], i + 1)
                    link(dve.tensor_copy(srow[im][:], ps[im][0:T, 1, 0:SEQ]))
                    for c in range(2):
                        link(dve.tensor_scalar(junk[im][:], srow[im][:], score[im][:, c:c + 1], None, ALU.is_lt, ALU.add,
                                               accum_out=less[im][:, c:c + 1]))
                        link(dve.scalar_tensor_tensor(junk[im][:], srow[im][:], score[im][:, c:c + 1], earlier[:, c, :],
                                                      ALU.is_equal, ALU.mult, accum_out=ties[im][:, c:c + 1]))
                    link(dve.tensor_tensor(rank[im][:], less[im][:], ties[im][:], ALU.add))
                    dve.tensor_scalar(away[im][:], rank[im][:], float(KR), None, ALU.is_ge)
                    for c in range(2):
                        last = dve.tensor_scalar(sel[im][:, c, :], places[:], rank[im][:, c:c + 1], None, ALU.is_equal)
                    last.then_inc(sel_done[im], 1)
                    for k in range(2):
                        link(dve.tensor_tensor_reduce(out=junk[im][0:F, :], in0=nT[im][0:F, k, :], in1=srow[im][0:F, :],
                                                      scale=1.0, scalar=0.0, op0=ALU.mult, op1=ALU.add,
                                                      accum_out=pool_r[im][:, k:k + 1]))
                    link(dve.tensor_reduce(ssum[im][:], srow[im][:], AX.X, ALU.add))
                    link(dve.tensor_scalar(ssum[im][:], ssum[im][:], 1e-6, None, ALU.add))
                    link(dve.reciprocal(ssum[im][:], ssum[im][:]))
                    link(dve.tensor_scalar(pool_t[im][:], pool_r[im][:], ssum[im][0:F, :], None, ALU.mult))
                    for k in range(2):
                        last = dve.scalar_tensor_tensor(mT[im][0:F, k, :], srow[im][0:F, :], pool_t[im][:, k:k + 1],
                                                        nT[im][0:F, k, :], ALU.mult, ALU.add)
                    last.then_inc(mix_in[im], 1)
                for im in range(2):
                    dve.wait_ge(q2_proj[im], i + 1)
                    dve.tensor_tensor(qb[im][:], spread(ps[im][0:F, 2, 0:2 * KR].rearrange("p (m r) -> p m r", m=2), 2, 6),
                                      blocks[:], ALU.mult).then_inc(qb_done[im], 1)
                for im in range(2):
                    dve.wait_ge(scored2[im], i + 1)
                    link(dve.tensor_reduce(mx2[im][:].rearrange("p (b g) -> p b g", b=2),
                                           ps[im][0:G4, 1:4:2, 0:2 * SEQ].rearrange("p b (g n) -> p b g n", g=2),
                                           AX.X, ALU.max))
                    dve.tensor_scalar(nmx2[im][:], mx2[im][:], -(DH ** -0.5), None, ALU.mult).then_inc(maxed2[im], 1)
                for im in range(2):
                    dve.wait_ge(exped2[im], i + 1)
                    link(dve.reciprocal(rs2[im][:], sum2[im][:]))
                    dve.tensor_tensor(p2[im][:], p2[im][:], spread(rs2[im][:], 2, SEQ), ALU.mult).then_inc(p2_done[im], 1)
                for im in range(2):
                    dve.wait_ge(pv2_done[im], i + 1)
                    link(dve.tensor_tensor(cb[im][:].rearrange("p m h r -> p (m h r)"), ps[im][0:F, 2, 0:4 * G4],
                                           blocks[:].rearrange("p m h r -> p (m h r)"), ALU.mult))
                    dve.tensor_reduce(cT[im][0:F, :, :], cb[im][:].rearrange("p m h r -> p m r h"), AX.X, ALU.add
                                      ).then_inc(c_done[im], 1)
                for im in range(2):
                    dve.wait_ge(mixed[im], i + 1)
                    for c in range(2):
                        link(dve.scalar_tensor_tensor(hm[im][:, c, :], ps[im][0:T, 0, c * D:(c + 1) * D],
                                                      away[im][:, c:c + 1], hid[im][:, c, :], ALU.mult, ALU.add))
                    dve.wait_ge(placed[im], i + 1)
                    link(dve.tensor_tensor(flat(hm[im]), flat(hm[im]), ps[im][0:T, 3, 0:2 * D], ALU.add))
                    statistics(im, hm[im])
                for im in range(2):
                    normalise(i, 3, im, hm[im])
                    link(dve.tensor_tensor(flat(h3[im]), flat(h3[im]), flat(hm[im]), ALU.add))
                for im in range(2):
                    dve.wait_ge(down_done[im], i + 1)
                    dve.wait_ge(y_out[im], 16 * i + 16)
                    dve.tensor_tensor(flat(y[im]), ps[im][0:T, 0, 0:2 * D], flat(h3[im]), ALU.add).then_inc(y_done[im], 1)
                link.end()


def build(nc, dr):
    with ExitStack() as ctx:
        scattered = [ctx.enter_context(nc.semaphore(f"b_scattered{n}")) for n in range(4)]
        y_out = [ctx.enter_context(nc.semaphore(f"c_y_out{n}")) for n in range(2)]
        gathered = [ctx.enter_context(nc.semaphore(f"d_gathered{n}")) for n in range(2)]
        stage_a(nc, dr)
        stage_b(nc, dr, scattered)
        stage_c(nc, dr, y_out)
        stage_d(nc, dr, gathered)


def dram_views(nc, given):
    dr = dict(given)

    def scratch(name, shape, dt=FP32):
        return nc.dram_tensor(name, shape, dt, kind="Internal").ap()

    band = scratch("band_rows", [2, T, H0 * 2 * PITCH])
    row = H0 * 2 * PITCH
    dr["band"] = [band[im] for im in range(2)]
    dr["band_skew"] = [bass.AP(tensor=band.tensor, offset=im * T * row, ap=[[row + 1, T], [PITCH, 2 * H0], [1, BAND]])
                       for im in range(2)]
    dr["band_read"] = [bass.AP(tensor=band.tensor, offset=im * T * row + PITCH - SEQ,
                               ap=[[row, T], [2 * PITCH, H0], [1, 2 * SEQ]]) for im in range(2)]
    dr["h1"] = scratch("h1_rows", [IMAGES, T, 2 * D])
    dr["xf"] = scratch("xf_rows", [IMAGES, T, 2 * D])
    dr["lg"] = scratch("router_logits", [IMAGES, T, 2 * E])
    dr["slot"] = scratch("slots", [T, COLS], INT32)
    dr["gain"] = scratch("gains", [T, COLS])
    dr["rows"] = scratch("rows", [ROWS, D])
    share = ROWS * D // ROUNDS
    assert share * ROUNDS == ROWS * D and share % 128 == 0
    dr["rows_flat"] = bass.AP(tensor=dr["rows"].tensor, offset=0,
                              ap=[[share, ROUNDS], [share // 128, 128], [1, share // 128]])
    return dr


def lay_out(np, a):
    f32 = np.float32

    def chunks(w, bias=None):
        out = np.zeros((FB, 2, w.shape[1]), w.dtype)
        out[:F] = w.reshape(2, F, -1).transpose(1, 0, 2)
        if bias is not None:
            out[F, 1] = bias.reshape(-1)
        return out

    def cols(v):
        return np.ascontiguousarray(v.reshape(2, F).T)

    def rows128(w):
        return np.ascontiguousarray(w.reshape(-1, 128, w.shape[1]).transpose(1, 0, 2))

    out = {}
    x = a["x"].reshape(IMAGES, 3, 14, 16, 14, 16).transpose(0, 1, 2, 4, 5, 3).reshape(IMAGES, SEQ, 6, 128)
    out["x"] = np.ascontiguousarray(x.transpose(0, 3, 2, 1))
    out["we"] = rows128(a["L0_tok_W"].T)
    out["be"] = a["L0_tok_b"].reshape(1, D)
    out["wq"] = chunks(a["L0_attn_wq"], a["L0_attn_u_param"])
    out["wk"] = chunks(a["L0_attn_wk"])
    out["wv"] = chunks(a["L0_attn_wv"])
    out["wo"] = chunks(a["L0_attn_wo"], a["L0_attn_bo"])
    out["w1"] = chunks(a["L0_attn_w1"], a["L0_attn_b1"])
    out["w2"] = rows128(a["L0_attn_w2"])
    out["b2"] = a["L0_attn_b2"].reshape(1, D)
    out["ws"] = chunks(a["L0_ffn_switch_w"], a["L0_ffn_switch_b"])
    out["n1"] = cols(a["L0_attn_norm1_w"])
    out["n2"] = cols(a["L0_attn_norm2_w"])
    out["wq_t"] = np.ascontiguousarray(a["L0_attn_wq"].T.reshape(H0, DK0, D).transpose(1, 0, 2))
    out["wpos"] = np.ascontiguousarray(a["L0_attn_w_pos"].transpose(1, 0, 2))
    out["vpar"] = np.ascontiguousarray(a["L0_attn_v_param"].T)
    out["we1"] = np.stack([chunks(a["L0_ffn_w1"][e], a["L0_ffn_b1"][e]) for e in range(E)])
    out["we2"] = np.stack([rows128(a["L0_ffn_w2"][e]) for e in range(E)])
    out["be2"] = a["L0_ffn_b2"]
    def rotary(w, bias):
        w, bias = w.T.reshape(D, H1N, DH // 2, 2), bias.reshape(1, H1N, DH // 2, 2)
        both = []
        for swap in (slice(None), slice(None, None, -1)):
            ww = np.zeros((D, H1N, 32), w.dtype)
            bb = np.zeros((1, H1N, 32), w.dtype)
            ww[:, :, :DH] = w[:, :, :, swap].reshape(D, H1N, DH)
            bb[:, :, :DH] = bias[:, :, :, swap].reshape(1, H1N, DH)
            both.append(chunks(ww.reshape(D, -1), bb.reshape(1, -1)))
        return np.stack(both, axis=2)

    out["dq"] = rotary(a["L1_attn_Wq"], a["L1_attn_bq"])
    out["dk"] = rotary(a["L1_attn_Wk"], a["L1_attn_bk"])
    out["dv"] = chunks(a["L1_attn_Wv"].T, a["L1_attn_bv"])
    out["dp"] = chunks(a["L1_attn_Wp"].T, a["L1_attn_bp"])
    out["wr"] = chunks(a["L1_ffn_Wr"].reshape(D, 1), a["L1_ffn_br"].reshape(1, 1))
    for name, w in (("uq", "q"), ("uk", "k"), ("uv", "v"), ("uo", "o"), ("um", "m")):
        out[name] = chunks(a["L1_ffn_W" + w], a["L1_ffn_b" + w])
    out["u1"] = chunks(a["L1_ffn_W1"], a["L1_ffn_bf1"])
    out["u2"] = rows128(a["L1_ffn_W2"])
    out["ub2"] = a["L1_ffn_bf2"].reshape(1, D)
    out["g1"], out["c1"] = cols(a["L1_ffn_g1"]), cols(a["L1_ffn_b1"])
    out["g2"], out["c2"] = cols(a["L1_ffn_g2"]), cols(a["L1_ffn_b2"])
    inv = (f32(1.0) / f32(10000.0) ** (f32(2.0) * np.arange(DH // 2, dtype=f32) / f32(DH))).astype(f32)
    angle = (np.arange(SEQ, dtype=f32)[:, None] * inv[None, :]).astype(f32)
    table = np.zeros((4, 32, 2, SEQ), f32)
    for j in range(DH):
        table[:, j, 0] = np.cos(angle[:, j // 2])
        table[:, j, 1] = np.sin(angle[:, j // 2]) * (-1 if j % 2 == 0 else 1)
    out["rope"] = table.reshape(128, 2, SEQ)
    later = np.where(np.arange(T)[None, :] > np.arange(T)[:, None], f32(-1e30), f32(0))
    out["causal"] = np.concatenate([later, np.zeros((T, T)), later], axis=1).astype(f32)
    token = np.arange(2)[None, :, None] * T + np.arange(T)[:, None, None]
    out["earlier"] = (np.arange(SEQ)[None, None, :] < token).astype(f32)
    out["places"] = np.tile(np.arange(K_ROUTED, dtype=f32), (T, 1))
    head = (np.arange(F)[:, None] // DH == np.arange(6)[None, :]).astype(f32)
    out["blocks"] = np.ascontiguousarray(np.broadcast_to(head[:, None, :, None], (F, 2, 6, K_ROUTED)))
    out["order"] = np.tile(np.arange(E, 0, -1, dtype=f32), (T, 1))
    out["offset"] = np.tile(np.arange(E, dtype=f32) * SLOTS, (T, 1))
    out["spare"] = (E * SLOTS + np.arange(COLS)[None, :] * T + np.arange(T)[:, None]).astype(f32)
    out["before"] = np.triu(np.ones((T, T), f32), 1)
    out["ones"] = np.ones((T, T), f32)
    out["ident"] = np.eye(128, dtype=f32)
    rate = np.exp(np.log(f32((SEQ + 1) / 2.0)) / f32(NPOS // 2))
    widths = rate ** np.arange(1, NPOS // 2 + 1, dtype=f32)
    d = np.arange(-98, 99)[None, :].astype(f32)
    near = (np.abs(d) <= widths[:, None]).astype(f32)
    assert widths[-1] < 99
    out["basis"] = np.tile(np.concatenate([near, np.sign(d) * near]), (4, 1)).astype(f32)
    return out


def kernel(**inputs):
    import numpy as np
    import concourse.bacc as bacc
    from concourse.bass_utils import run_bass_kernel_spmd

    nc = bacc.Bacc("TRN2", target_bir_lowering=False, num_devices=1)
    arrays = lay_out(np, {name: np.asarray(v) for name, v in inputs.items()})
    given = {name: nc.dram_tensor(f"in_{name}", v.shape, mybir.dt.from_np(v.dtype), kind="ExternalInput").ap()
             for name, v in arrays.items()}
    given["out"] = nc.dram_tensor("out", [IMAGES, 2, T, D], FP32, kind="ExternalOutput").ap()
    build(nc, dram_views(nc, given))
    run = run_bass_kernel_spmd(nc, [{f"in_{name}": v for name, v in arrays.items()}], core_ids=[0])
    return run.results[0]["out"].reshape(IMAGES, SEQ, D)
```

```python
from contextlib import ExitStack

import concourse.bass as bass
from concourse import mybir

FP32 = mybir.dt.float32
INT32 = mybir.dt.int32
ALU = mybir.AluOpType
ACT = mybir.ActivationFunctionType
AX = mybir.AxisListType

IMAGES, SEQ, D = 64, 196, 192
T = 98
F = 96
FB = F + 1
COLS = 2 * IMAGES
TOKENS = IMAGES * SEQ
ROUNDS = IMAGES // 2
H0, DK0, DV0, NPOS = 8, 64, 24, 32
BAND = 197
PITCH = 294
E, HID = 8, 768
CAPACITY = int(1.25 * TOKENS / E)
SLOTS = 2048
BATCH = 512
ROWS = E * SLOTS + TOKENS
H1N, DH = 12, 16
K_ROUTED = max(1, int(round(0.15 * SEQ)))
EPS = 1e-5


def spread(ap, axis, n):
    dims = [list(d) for d in ap.ap]
    dims.insert(axis, [0, n])
    return bass.AP(tensor=ap.tensor, offset=ap.offset, ap=dims)


class Link:

    def __init__(self, eng, sem, per_round):
        self.eng, self.sem, self.per, self.i, self.n = eng, sem, per_round, 0, 0

    def round(self, i):
        assert self.n in (0, self.per), (self.sem, self.n)
        self.i, self.n = i, 0

    def __call__(self, ins):
        self.n += 1
        ins.then_inc(self.sem, 1)
        self.eng.wait_ge(self.sem, self.i * self.per + self.n)

    def end(self):
        assert self.n == self.per, f"links in a round: {self.n}, not {self.per}"


def allocators(nc, ctx):
    def sb(name, shape, dt=FP32):
        return ctx.enter_context(nc.sbuf_tensor(name, shape, dt))

    def sb2(name, shape, dt=FP32):
        return [sb(f"{name}_{im}", shape, dt) for im in range(2)]

    taken = []

    def sem(name):
        taken.append(nc.alloc_semaphore(name=name))
        return taken[-1]

    def hand_back():
        nc.clear_and_free_semaphores(taken)
        nc.all_engine_barrier()

    ctx.callback(hand_back)

    def sem2(name):
        return [sem(f"{name}_{im}") for im in range(2)]

    return sb, sb2, sem, sem2


def load_all(sp, pairs, arrived):
    for tile, dram in pairs:
        sp.dma_start(tile, dram).then_inc(arrived, 16)
    sp.wait_ge(arrived, 16 * len(pairs))


def stage_a(nc, dr):
    with ExitStack() as ctx:
        sb, sb2, sem, sem2 = allocators(nc, ctx)
        ident = sb("a_ident", [128, 128])
        basis = sb("a_basis", [128, 4, BAND])
        we = sb("a_we", [128, 6, D])
        be = sb("a_be", [1, D])
        ones_row = sb("a_ones_row", [1, 128])
        zero = sb("a_zero", [128, 1356])
        half = sb("a_half", [T, 4])
        wq = sb("a_wq", [FB, 2, H0 * DK0])
        wk = sb("a_wk", [FB, 2, H0 * DK0])
        wv = sb("a_wv", [FB, 2, D])
        wqp = sb("a_wqp", [FB, 2, H0 * NPOS])
        wo = sb("a_wo", [FB, 2, D])
        w1 = sb("a_w1", [FB, 2, 2 * D])
        w2 = sb("a_w2", [128, 3, D])
        b2 = sb("a_b2", [1, D])
        ws = sb("a_ws", [FB, 2, E])
        n1 = sb("a_n1", [F, 2])
        n2 = sb("a_n2", [F, 2])
        wq_t = sb("a_wq_t", [DK0, H0, D])
        wpos = sb("a_wpos", [DK0, H0, NPOS])
        vpar = sb("a_vpar", [DK0, H0])
        vw = sb("a_vw", [1, H0 * NPOS])

        xin = sb2("a_xin", [128, 6, SEQ])
        h0 = sb2("a_h0", [T, 2, D])
        xn = sb2("a_xn", [T, 2, D])
        xr = sb2("a_xr", [T, 2, D])
        st = sb2("a_st", [T, 2, 6])
        mv = sb2("a_mv", [T, 2, 2])
        vv = sb2("a_vv", [T, 2, 2])
        rr = sb2("a_rr", [T, 2, 2])
        hT = sb2("a_hT", [FB, 2, SEQ])
        qz = sb2("a_qz", [128, H0, SEQ])
        kT = sb2("a_kT", [128, 4, SEQ])
        qwT = sb2("a_qwT", [128, 2, SEQ])
        vx = sb2("a_vx", [T, 2, H0, DV0 + 1])
        band = sb2("a_band", [T, H0, 2 * BAND])
        pos = sb2("a_pos", [T, H0, 2 * SEQ])
        s_sb = sb2("a_s", [T, 4, 2 * SEQ])
        mx = sb2("a_mx", [T, 4, 4])
        nmx = sb2("a_nmx", [T, 4, 4])
        pT = sb2("a_pT", [T, 4, 2 * SEQ])
        rs = sb2("a_rs", [T, 2, 2])
        o_sb = sb2("a_o", [T, 2, D])
        x1 = sb2("a_x1", [T, 2, D])
        gT = sb2("a_gT", [128, 3, SEQ])
        h1 = sb2("a_h1", [T, 2, D])
        xf = sb2("a_xf", [T, 2, D])
        lg = sb2("a_lg", [T, 2, E])
        ps = [ctx.enter_context(nc.psum_tensor(f"a_ps{im}", [128, 4, 512], FP32)) for im in range(2)]

        weights_in = sem("a_weights_in")
        vw_done = sem("a_vw_done")
        wqp_done = sem("a_wqp_done")
        wqp_copied = sem("a_wqp_copied")
        vw_placed = sem("a_vw_placed")
        consts_set = sem("a_consts_set")
        pads_zero = sem("a_pads_zero")
        rows_zero = sem("a_rows_zero")
        v_link = sem("a_v_link")
        fence = sem("a_fence")
        x_in = sem2("a_x_in")
        embedded = sem2("a_embedded")
        stats = sem2("a_stats")
        rstd = sem2("a_rstd")
        normed = sem2("a_normed")
        flipped = sem2("a_flipped")
        feat = sem2("a_feat")
        q_proj = sem2("a_q_proj")
        qw_proj = sem2("a_qw_proj")
        v_proj = sem2("a_v_proj")
        k_proj = sem2("a_k_proj")
        q_copied = sem2("a_q_copied")
        qw_copied = sem2("a_qw_copied")
        v_copied = sem2("a_v_copied")
        k_copied = sem2("a_k_copied")
        band_done = sem2("a_band_done")
        band_copied = sem2("a_band_copied")
        band_out = sem2("a_band_out")
        pos_in = sem2("a_pos_in")
        scored = sem2("a_scored")
        added = sem2("a_added")
        maxed = sem2("a_maxed")
        exped = sem2("a_exped")
        p_flipped = sem2("a_p_flipped")
        p_copied = sem2("a_p_copied")
        pv_done = sem2("a_pv_done")
        o_done = sem2("a_o_done")
        projected = sem2("a_projected")
        x1_done = sem2("a_x1_done")
        up_done = sem2("a_up_done")
        gelued = sem2("a_gelued")
        down_done = sem2("a_down_done")
        h1_done = sem2("a_h1_done")
        logits = sem2("a_logits")
        lg_done = sem2("a_lg_done")
        out_sent = sem2("a_out_sent")

        block = ctx.enter_context(nc.Block())

        @block.sync
        def _(sp):
            load_all(sp, [(ident[:], dr["ident"]), (basis[:], dr["basis"]), (we[:], dr["we"]), (be[:], dr["be"]),
                          (wq[:], dr["wq"]), (wk[:], dr["wk"]), (wv[:], dr["wv"]), (wo[:], dr["wo"]),
                          (w1[:], dr["w1"]), (w2[:], dr["w2"]), (b2[:], dr["b2"]), (ws[:], dr["ws"]),
                          (n1[:], dr["n1"]), (n2[:], dr["n2"]), (wq_t[:], dr["wq_t"]), (wpos[:], dr["wpos"]),
                          (vpar[:], dr["vpar"])], weights_in)
            sp.wait_ge(wqp_copied, 3)
            sp.dma_start(wqp[F:FB, 1, :], vw[0:1, :]).then_inc(vw_placed, 16)
            sp.wait_ge(consts_set, 7)
            for im in range(2):
                sp.dma_start(dr["band"][im].rearrange("p (a f) -> p a f", f=1176),
                             spread(zero[0:T, 0:1176], 1, 4)).then_inc(pads_zero, 16)
            sp.wait_ge(pads_zero, 32)
            for im in range(2):
                sp.sem_inc(embedded[im], 1)
                sp.sem_inc(added[im], 4)
            with sp.Fori(0, ROUNDS) as i:
                for im in range(2):
                    sp.wait_ge(embedded[im], i + 1)
                    sp.dma_start(xin[im][:], dr["x"][bass.ds(2 * i + im, 1)].rearrange("a p k n -> (a p) k n")
                                 ).then_inc(x_in[im], 16)
                sp.dma_start(dr["rows_flat"][bass.ds(i, 1)].rearrange("a p f -> (a p) f"), zero[:]).then_inc(rows_zero, 16)
                for im in range(2):
                    sp.wait_ge(band_copied[im], 2 * i + 2)
                    sp.dma_start(dr["band_skew"][im], band[im][:].rearrange("p h (c b) -> p (h c) b", c=2)
                                 ).then_inc(band_out[im], 16)
                for im in range(2):
                    sp.wait_ge(band_out[im], 16 * i + 32)
                    sp.wait_ge(added[im], 4 * i + 4)
                    sp.dma_start(pos[im][:], dr["band_read"][im]).then_inc(pos_in[im], 16)
            sp.wait_ge(rows_zero, 16 * ROUNDS)
            for im in range(2):
                sp.wait_ge(out_sent[im], 48 * ROUNDS + 48)

        @block.gpsimd
        def _(pool):
            pool.memset(zero[:], 0.0).then_inc(consts_set, 1)
            pool.memset(half[:], -0.5).then_inc(consts_set, 1)
            pool.wait_ge(consts_set, 7)

            def scale(im, n, kinds):
                pool.wait_ge(stats[im], n)
                pool.tensor_tensor(rr[im][:, 0:kinds, :], vv[im][:, 0:kinds, :],
                                   half[:, 0:2 * kinds].rearrange("p (a c) -> p a c", c=2), ALU.pow
                                   ).then_inc(rstd[im], 1)

            with pool.Fori(0, ROUNDS) as i:
                for n, kinds in ((1, 2), (2, 1), (3, 1)):
                    for im in range(2):
                        scale(im, 3 * i + n, kinds)

        @block.scalar
        def _(act):
            act.wait_ge(weights_in, 16 * 17)
            act.wait_ge(consts_set, 7)
            for im in range(2):
                act.sem_inc(band_out[im], 16)
            with act.Fori(0, ROUNDS) as i:
                for im in range(2):
                    act.wait_ge(flipped[im], 4 * i + 1)
                    act.activation(hT[im][0:F, 0, :], ps[im][0:F, 1, 0:SEQ], ACT.Identity, scale=n1[:, 0:1])
                    act.activation(hT[im][0:F, 1, :], ps[im][0:F, 1, SEQ:2 * SEQ], ACT.Identity,
                                   scale=n1[:, 1:2]).then_inc(feat[im], 1)
                for g in range(2):
                    for im in range(2):
                        act.wait_ge(band_done[im], 2 * i + g + 1)
                        if g == 0:
                            act.wait_ge(band_out[im], 16 * i + 16)
                        act.activation(band[im][:, 4 * g:4 * g + 4, :], ps[im][0:T, :, 0:2 * BAND],
                                       ACT.Copy).then_inc(band_copied[im], 1)
                for im in range(2):
                    act.wait_ge(q_proj[im], i + 1)
                    act.activation(qz[im][0:64, 0:H0:2, :].rearrange("p (b m) n -> p b m n", b=2),
                                   ps[im][0:64, 2:4, 0:2 * SEQ].rearrange("p b (m n) -> p b m n", m=2),
                                   ACT.Copy).then_inc(q_copied[im], 1)
                for im in range(2):
                    act.wait_ge(k_proj[im], i + 1)
                    act.activation(kT[im][:].rearrange("p (b m) n -> p b (m n)", b=2), ps[im][:, 2:4, 0:2 * SEQ],
                                   ACT.Copy).then_inc(k_copied[im], 1)

                def exps(p, im):
                    act.wait_ge(maxed[im], 4 * i + p + 1)
                    for n in range(4):
                        part = s_sb[im][:, 2 * (p % 2) + n // 2, (n % 2) * SEQ:(n % 2 + 1) * SEQ]
                        last = act.activation(part, part, ACT.Exp, scale=DK0 ** -0.5, bias=nmx[im][:, p, n:n + 1])
                    last.then_inc(exped[im], 1)

                for im in range(2):
                    exps(0, im)
                for p in range(4):
                    for im in range(2):
                        bank = 2 * (p % 2) + 1
                        act.wait_ge(p_flipped[im], 4 * i + p + 1)
                        act.activation(pT[im][:, bank, :], ps[im][0:T, bank, 0:2 * SEQ], ACT.Copy).then_inc(p_copied[im], 1)
                    for im in range(2):
                        if p < 3:
                            exps(p + 1, im)
                for im in range(2):
                    act.wait_ge(flipped[im], 4 * i + 2)
                    act.activation(hT[im][0:F, :, :].rearrange("p k n -> p (k n)"), ps[im][0:F, 1, 0:2 * SEQ],
                                   ACT.Copy).then_inc(feat[im], 1)
                for im in range(2):
                    act.wait_ge(flipped[im], 4 * i + 3)
                    act.activation(hT[im][0:F, 0, :], ps[im][0:F, 1, 0:SEQ], ACT.Identity, scale=n2[:, 0:1])
                    act.activation(hT[im][0:F, 1, :], ps[im][0:F, 1, SEQ:2 * SEQ], ACT.Identity,
                                   scale=n2[:, 1:2]).then_inc(feat[im], 1)
                for im in range(2):
                    act.wait_ge(up_done[im], i + 1)
                    act.activation(gT[im][:, 0:2, :].rearrange("p m n -> p (m n)"), ps[im][:, 2, 0:2 * SEQ], ACT.Gelu)
                    act.activation(gT[im][:, 2, :], ps[im][:, 3, 0:SEQ], ACT.Gelu).then_inc(gelued[im], 1)
                for im in range(2):
                    act.wait_ge(flipped[im], 4 * i + 4)
                    act.activation(hT[im][0:F, :, :].rearrange("p k n -> p (k n)"), ps[im][0:F, 1, 0:2 * SEQ],
                                   ACT.Copy).then_inc(feat[im], 1)

                for im in range(2):
                    img = 2 * i + im
                    act.wait_ge(h1_done[im], i + 1)
                    act.dma_start(dr["h1"][bass.ds(img, 1)].rearrange("a p f -> (a p) f"),
                                  h1[im][:].rearrange("p c f -> p (c f)")).then_inc(out_sent[im], 16)
                    act.wait_ge(normed[im], 3 * i + 3)
                    act.dma_start(dr["xf"][bass.ds(img, 1)].rearrange("a p f -> (a p) f"),
                                  xf[im][:].rearrange("p c f -> p (c f)")).then_inc(out_sent[im], 16)
                for im in range(2):
                    act.wait_ge(lg_done[im], i + 2)
                    act.dma_start(dr["lg"][bass.ds(2 * i + im, 1)].rearrange("a p f -> (a p) f"),
                                  lg[im][:].rearrange("p c f -> p (c f)")).then_inc(out_sent[im], 16)

        @block.tensor
        def _(pe):
            pe.wait_ge(weights_in, 16 * 17)
            pe.wait_ge(consts_set, 7)
            for k in range(2):
                for h in range(H0):
                    last = pe.matmul(ps[0][0:F, k, h * NPOS:(h + 1) * NPOS], wq_t[:, h, F * k:F * k + F],
                                     wpos[:, h, :], start=True, stop=True)
            last.then_inc(wqp_done, 1)
            for h in range(H0):
                last = pe.matmul(ps[0][0:1, 2, h * NPOS:(h + 1) * NPOS], vpar[:, h:h + 1],
                                 wpos[:, h, :], start=True, stop=True)
            last.then_inc(vw_done, 1)
            pe.wait_ge(wqp_copied, 3)
            pe.wait_ge(vw_placed, 16)

            def flip(im, src, bank):
                for k in range(2):
                    for c in range(2):
                        last = pe.transpose(ps[im][0:F, bank, k * SEQ + c * T:k * SEQ + (c + 1) * T],
                                            src[:, c, k * F:(k + 1) * F], ident[0:T, 0:T])
                last.then_inc(flipped[im], 1)

            def to_tokens(im, bank, w, n, done):
                for c in range(2):
                    for k in range(2):
                        last = pe.matmul(ps[im][0:T, bank, c * n:(c + 1) * n], hT[im][:, k, c * T:(c + 1) * T],
                                         w[:, k, :], start=(k == 0), stop=(k == 1))
                last.then_inc(done[im], 1)

            def to_features(im, banks, w, done):
                for m in range(w.shape[2] // 128):
                    at = (m % 2) * SEQ
                    for k in range(2):
                        last = pe.matmul(ps[im][:, banks[m // 2], at:at + SEQ], w[:, k, m * 128:(m + 1) * 128],
                                         hT[im][:, k, :], start=(k == 0), stop=(k == 1))
                last.then_inc(done[im], 1)

            for im in range(2):
                pe.sem_inc(lg_done[im], 1)
            with pe.Fori(0, ROUNDS) as i:
                for im in range(2):
                    pe.wait_ge(x_in[im], 16 * i + 16)
                    pe.wait_ge(lg_done[im], i + 1)
                    for c in range(2):
                        out = ps[im][0:T, 0, c * D:(c + 1) * D]
                        for k in range(6):
                            pe.matmul(out, xin[im][:, k, c * T:(c + 1) * T], we[:, k, :], start=(k == 0), stop=False)
                        last = pe.matmul(out, ones_row[0:1, 0:T], be[0:1, :], start=False, stop=True)
                    last.then_inc(embedded[im], 1)
                for im in range(2):
                    pe.wait_ge(normed[im], 3 * i + 1)
                    flip(im, xr[im], 1)
                for im in range(2):
                    pe.wait_ge(feat[im], 4 * i + 1)
                    to_features(im, (0,), wqp, qw_proj)
                for g in range(2):
                    for im in range(2):
                        if g == 0:
                            pe.wait_ge(qw_copied[im], i + 1)
                        else:
                            pe.wait_ge(band_copied[im], 2 * i + 1)
                        for hh in range(4):
                            for c in range(2):
                                last = pe.matmul(ps[im][0:T, hh, c * BAND:(c + 1) * BAND],
                                                 qwT[im][:, g, c * T:(c + 1) * T], basis[:, hh, :], start=True, stop=True)
                        last.then_inc(band_done[im], 1)
                for im in range(2):
                    pe.wait_ge(band_copied[im], 2 * i + 2)
                    to_features(im, (2, 3), wq, q_proj)
                    to_tokens(im, 0, wv, D, v_proj)
                for im in range(2):
                    pe.wait_ge(q_copied[im], 2 * i + 2)
                    to_features(im, (2, 3), wk, k_proj)

                def score(p, im):
                    if p == 0:
                        pe.wait_ge(v_copied[im], i + 1)
                        pe.wait_ge(k_copied[im], i + 1)
                    elif p > 1:
                        pe.wait_ge(o_done[im], 4 * i + p - 1)
                    for n in range(2):
                        for c in range(2):
                            last = pe.matmul(ps[im][0:T, 2 * (p % 2) + n, c * SEQ:(c + 1) * SEQ],
                                             qz[im][:, 2 * p + n, c * T:(c + 1) * T], kT[im][:, p, :],
                                             start=True, stop=True)
                    last.then_inc(scored[im], 1)

                for im in range(2):
                    score(0, im)
                for p in range(4):
                    for im in range(2):
                        pe.wait_ge(exped[im], 4 * i + p + 1)
                        for n in range(2):
                            b = 2 * (p % 2) + n
                            for cj in range(2):
                                for ci in range(2):
                                    last = pe.transpose(ps[im][0:T, b, cj * SEQ + ci * T:cj * SEQ + (ci + 1) * T],
                                                        s_sb[im][:, b, ci * SEQ + cj * T:ci * SEQ + (cj + 1) * T],
                                                        ident[0:T, 0:T])
                        last.then_inc(p_flipped[im], 1)
                    for im in range(2):
                        if p < 3:
                            score(p + 1, im)
                    for im in range(2):
                        pe.wait_ge(p_copied[im], 8 * i + 2 * p + 2)
                        for ci in range(2):
                            for n in range(2):
                                b = 2 * (p % 2) + n
                                at = (2 * ci + n) * (DV0 + 1)
                                for cj in range(2):
                                    last = pe.matmul(ps[im][0:T, 2 * (p % 2), at:at + DV0 + 1],
                                                     pT[im][:, b, cj * SEQ + ci * T:cj * SEQ + (ci + 1) * T],
                                                     vx[im][:, cj, 2 * p + n, :], start=(cj == 0), stop=(cj == 1))
                        last.then_inc(pv_done[im], 1)
                for im in range(2):
                    pe.wait_ge(o_done[im], 4 * i + 4)
                    flip(im, o_sb[im], 1)
                for im in range(2):
                    pe.wait_ge(feat[im], 4 * i + 2)
                    to_tokens(im, 2, wo, D, projected)
                for im in range(2):
                    pe.wait_ge(normed[im], 3 * i + 2)
                    flip(im, xr[im], 1)
                for im in range(2):
                    pe.wait_ge(feat[im], 4 * i + 3)
                    to_features(im, (2, 3), w1, up_done)
                for im in range(2):
                    pe.wait_ge(gelued[im], i + 1)
                    for c in range(2):
                        out = ps[im][0:T, 0, c * D:(c + 1) * D]
                        for m in range(3):
                            pe.matmul(out, gT[im][:, m, c * T:(c + 1) * T], w2[:, m, :], start=(m == 0), stop=False)
                        last = pe.matmul(out, ones_row[0:1, 0:T], b2[0:1, :], start=False, stop=True)
                    last.then_inc(down_done[im], 1)
                for im in range(2):
                    pe.wait_ge(normed[im], 3 * i + 3)
                    flip(im, xf[im], 1)
                for im in range(2):
                    pe.wait_ge(feat[im], 4 * i + 4)
                    to_tokens(im, 2, ws, E, logits)

        @block.vector
        def _(dve):
            dve.memset(ones_row[:], 1.0).then_inc(consts_set, 1)
            for im in range(2):
                dve.memset(hT[im][F:FB, :, :], 1.0).then_inc(consts_set, 1)
                dve.memset(vx[im][:, :, :, DV0:DV0 + 1], 1.0).then_inc(consts_set, 1)
                dve.memset(qz[im][:], 0.0)
            dve.memset(wqp[F:FB, 0, :], 0.0)
            dve.wait_ge(wqp_done, 1)
            for k in range(2):
                dve.tensor_copy(wqp[0:F, k, :], ps[0][0:F, k, 0:H0 * NPOS]).then_inc(wqp_copied, 1)
            dve.wait_ge(vw_done, 1)
            dve.tensor_copy(vw[0:1, :], ps[0][0:1, 2, 0:H0 * NPOS]).then_inc(wqp_copied, 1)
            for im in range(2):
                dve.sem_inc(out_sent[im], 48)
            link = Link(dve, v_link, 34)

            def statistics(im, rows, kind):
                dve.bn_stats(st[im][:, 0, :], rows[:, 0, :])
                link(dve.bn_stats(st[im][:, 1, :], rows[:, 1, :]))
                dve.sem_inc(fence, 1)
                dve.bn_aggr(mv[im][:, 0, :], st[im][:, 0, :])
                link(dve.bn_aggr(mv[im][:, 1, :], st[im][:, 1, :]))
                mean, var = mv[im][:, :, 0], mv[im][:, :, 1]
                if kind == "rms":
                    link(dve.tensor_tensor(vv[im][:, 1, :], mean, mean, ALU.mult))
                    last = dve.scalar_tensor_tensor(vv[im][:, 0, :], vv[im][:, 1, :], EPS, var, ALU.add, ALU.add)
                else:
                    last = dve.tensor_scalar(vv[im][:, 0, :], var, EPS, None, ALU.add)
                    if kind == "both":
                        last = dve.tensor_scalar(vv[im][:, 1, :], var, 1 + EPS, EPS * EPS, ALU.mult, ALU.add)
                last.then_inc(stats[im], 1)

            with dve.Fori(0, ROUNDS) as i:
                link.round(i)
                for im in range(2):
                    dve.wait_ge(embedded[im], i + 2)
                    statistics(im, ps[im][0:T, 0, 0:2 * D].rearrange("p (c f) -> p c f", c=2), "both")
                    link(dve.tensor_copy(h0[im][:].rearrange("p c f -> p (c f)"), ps[im][0:T, 0, 0:2 * D]))
                for im in range(2):
                    dve.wait_ge(rstd[im], 3 * i + 1)
                    for c in range(2):
                        last = dve.tensor_scalar(xr[im][:, c, :], h0[im][:, c, :], mv[im][:, c, 0:1],
                                                 rr[im][:, 1, c:c + 1], ALU.subtract, ALU.mult)
                    last.then_inc(normed[im], 1)
                    for c in range(2):
                        dve.tensor_scalar(xn[im][:, c, :], h0[im][:, c, :], mv[im][:, c, 0:1],
                                          rr[im][:, 0, c:c + 1], ALU.subtract, ALU.mult)
                for im in range(2):
                    dve.wait_ge(qw_proj[im], i + 1)
                    dve.tensor_copy(qwT[im][:].rearrange("p m n -> p (m n)"), ps[im][:, 0, 0:2 * SEQ]
                                    ).then_inc(qw_copied[im], 1)
                for im in range(2):
                    dve.wait_ge(q_proj[im], i + 1)
                    dve.tensor_copy(qz[im][64:128, 1:H0:2, :].rearrange("p (b m) n -> p b m n", b=2),
                                    ps[im][64:128, 2:4, 0:2 * SEQ].rearrange("p b (m n) -> p b m n", m=2)
                                    ).then_inc(q_copied[im], 1)
                    dve.wait_ge(v_proj[im], i + 1)
                    dve.tensor_copy(vx[im][:, :, :, 0:DV0],
                                    ps[im][0:T, 0, 0:2 * D].rearrange("p (c h d) -> p c h d", c=2, d=DV0)
                                    ).then_inc(v_copied[im], 1)

                def add_max(p, im):
                    at = slice(2 * (p % 2), 2 * (p % 2) + 2)
                    dve.wait_ge(scored[im], 4 * i + p + 1)
                    if p == 0:
                        dve.wait_ge(pos_in[im], 16 * i + 16)
                    dve.tensor_tensor(s_sb[im][:, at, :], ps[im][0:T, at, 0:2 * SEQ], pos[im][:, 2 * p:2 * p + 2, :],
                                      ALU.add).then_inc(added[im], 1)
                    dve.wait_ge(added[im], 4 * i + p + 5)
                    link(dve.tensor_reduce(mx[im][:, p, :], s_sb[im][:, at, :].rearrange("p h (c j) -> p (h c) j", c=2),
                                           AX.X, ALU.max))
                    dve.tensor_scalar(nmx[im][:, p, :], mx[im][:, p, :], -(DK0 ** -0.5), None, ALU.mult
                                      ).then_inc(maxed[im], 1)

                for im in range(2):
                    add_max(0, im)
                for p in range(4):
                    bank = 2 * (p % 2)
                    for im in range(2):
                        dve.wait_ge(p_flipped[im], 4 * i + p + 1)
                        dve.tensor_copy(pT[im][:, bank, :], ps[im][0:T, bank, 0:2 * SEQ]).then_inc(p_copied[im], 1)
                    for im in range(2):
                        if p < 3:
                            add_max(p + 1, im)
                    for im in range(2):
                        dve.wait_ge(pv_done[im], 4 * i + p + 1)
                        o_ps = ps[im][0:T, bank, 0:4 * (DV0 + 1)].rearrange("p (c h d) -> p c h d", c=2, d=DV0 + 1)
                        link(dve.reciprocal(rs[im][:], o_ps[:, :, :, DV0]))
                        at = slice(2 * p * DV0, 2 * (p + 1) * DV0)
                        dve.tensor_tensor(o_sb[im][:, :, at].rearrange("p c (h d) -> p c h d", d=DV0),
                                          o_ps[:, :, :, 0:DV0], spread(rs[im][:], 3, DV0), ALU.mult
                                          ).then_inc(o_done[im], 1)
                for im in range(2):
                    dve.wait_ge(projected[im], i + 1)
                    link(dve.tensor_tensor(x1[im][:].rearrange("p c f -> p (c f)"), ps[im][0:T, 2, 0:2 * D],
                                           xn[im][:].rearrange("p c f -> p (c f)"), ALU.add))
                    statistics(im, x1[im], "rms")
                for im in range(2):
                    dve.wait_ge(rstd[im], 3 * i + 2)
                    for c in range(2):
                        last = dve.tensor_scalar(xr[im][:, c, :], x1[im][:, c, :], rr[im][:, 0, c:c + 1], None, ALU.mult)
                    last.then_inc(normed[im], 1)
                    dve.tensor_tensor(xn[im][:], x1[im][:], h0[im][:], ALU.add).then_inc(x1_done[im], 1)
                for im in range(2):
                    dve.wait_ge(down_done[im], i + 1)
                    dve.wait_ge(x1_done[im], i + 1)
                    dve.wait_ge(out_sent[im], 48 * i + 48)
                    dve.tensor_tensor(h1[im][:].rearrange("p c f -> p (c f)"), ps[im][0:T, 0, 0:2 * D],
                                      xn[im][:].rearrange("p c f -> p (c f)"), ALU.add).then_inc(h1_done[im], 1)
                    dve.wait_ge(h1_done[im], i + 1)
                    statistics(im, h1[im], "layer")
                for im in range(2):
                    dve.wait_ge(rstd[im], 3 * i + 3)
                    for c in range(2):
                        last = dve.tensor_scalar(xf[im][:, c, :], h1[im][:, c, :], mv[im][:, c, 0:1],
                                                 rr[im][:, 0, c:c + 1], ALU.subtract, ALU.mult)
                    last.then_inc(normed[im], 1)
                for im in range(2):
                    dve.wait_ge(logits[im], i + 1)
                    dve.tensor_copy(lg[im][:].rearrange("p c e -> p (c e)"), ps[im][0:T, 2, 0:2 * E]).then_inc(lg_done[im], 1)
                link.end()


def stage_b(nc, dr, scattered):
    W = E * COLS
    with ExitStack() as ctx:
        sb, sb2, sem, sem2 = allocators(nc, ctx)
        lg = sb("b_lg", [T, COLS, E])
        ex = sb("b_ex", [T, COLS, E])
        top = sb("b_top", [T, COLS])
        gain = sb("b_gain", [T, COLS])
        total = sb("b_total", [T, COLS])
        order = sb("b_order", [T, E])
        offset = sb("b_offset", [T, E])
        spare = sb("b_spare", [T, COLS])
        before = sb("b_before", [T, T])
        ones = sb("b_ones", [T, T])
        flat1 = sb("b_flat1", [T, W])
        mine = sb("b_mine", [T, E, COLS])
        own = sb("b_own", [T, E, COLS])
        hit = sb("b_hit", [T, E, COLS])
        above = sb("b_above", [T, E, COLS])
        tie = sb("b_tie", [T, E, COLS])
        keep = sb("b_keep", [T, E, COLS])
        sums = sb("b_sums", [T, E, COLS])
        rank = sb("b_rank", [T, E, COLS])
        base = sb("b_base", [T, E])
        cnt = sb("b_cnt", [T, E])
        need = sb("b_need", [T, E])
        bit_f = sb("b_bit_f", [T, E])
        bit_i = sb("b_bit_i", [T, E], INT32)
        cand = sb("b_cand", [T, E], INT32)
        won = sb("b_won", [T, E], INT32)
        bound = sb("b_bound", [T, E], INT32)
        kept = sb("b_kept", [T, COLS])
        slot_f = sb("b_slot_f", [T, COLS])
        slot = sb("b_slot", [T, COLS], INT32)
        xrow = [sb(f"b_xrow{n}", [T, 2, D]) for n in range(4)]
        idx = [sb(f"b_idx{n}", [T, 2], INT32) for n in range(4)]
        ps = ctx.enter_context(nc.psum_tensor("b_ps", [128, 8, 512], FP32))
        ps_pre = ps[0:T, 0:2, :].rearrange("p b n -> p (b n)")
        ps_tot = ps[0:T, 2:4, :].rearrange("p b n -> p (b n)")
        ps_cnt = ps[0:T, 4, 0:E]
        ps_above = ps[0:T, 5, 0:E]

        loaded = sem("b_loaded")
        shifted = sem("b_shifted")
        exped = sem("b_exped")
        v_link = sem("b_v_link")
        s_link = sem("b_s_link")
        counted = sem("b_counted")
        summed = sem("b_summed")
        above_counted = sem("b_above_counted")
        above_summed = sem("b_above_summed")
        marked = sem("b_marked")
        prefixed = sem("b_prefixed")
        slots_done = sem("b_slots_done")
        tables_out = sem("b_tables_out")
        fence = sem("b_fence")
        x_in = [sem(f"b_x_in{n}") for n in range(4)]
        idx_done = [sem(f"b_idx_done{n}") for n in range(4)]
        row_free = [sem(f"b_row_free{n}") for n in range(4)]
        BITS = 30

        block = ctx.enter_context(nc.Block())

        @block.sync
        def _(sp):
            load_all(sp, [(lg[:].rearrange("p (i c) e -> p i (c e)", c=2), dr["lg"].rearrange("i p f -> p i f")),
                          (order[:], dr["order"]), (offset[:], dr["offset"]), (spare[:], dr["spare"]),
                          (before[:], dr["before"]), (ones[:], dr["ones"])], loaded)
            sp.wait_ge(slots_done, 1)
            sp.dma_start(dr["slot"], slot[:]).then_inc(tables_out, 16)
            sp.dma_start(dr["gain"], gain[:]).then_inc(tables_out, 16)
            with sp.Fori(0, IMAGES // 4) as i:
                for n in range(4):
                    sp.wait_ge(row_free[n], i + 1)
                    sp.dma_start(xrow[n][:].rearrange("p c f -> p (c f)"),
                                 dr["xf"][bass.ds(4 * i + n, 1)].rearrange("a p f -> (a p) f")).then_inc(x_in[n], 16)
            sp.wait_ge(tables_out, 32)

        @block.gpsimd
        def _(pool):
            pool.wait_ge(slots_done, 1)
            for n in range(4):
                pool.sem_inc(row_free[n], 1)
            with pool.Fori(0, IMAGES // 4) as i:
                for n in range(4):
                    pool.tensor_copy(idx[n][:], slot[:, bass.ds(8 * i + 2 * n, 2)]).then_inc(idx_done[n], 1)
                for n in range(4):
                    pool.wait_ge(x_in[n], 16 * i + 16)
                    pool.wait_ge(idx_done[n], i + 1)
                    pool.sem_inc(fence, 1)
                    for c in range(2):
                        pool.indirect_dma_start(out=dr["rows"], out_offset=bass.IndirectOffsetOnAxis(
                            ap=idx[n][:, c:c + 1], axis=0), in_=xrow[n][:, c, :], in_offset=None
                            ).then_inc(scattered[n], 16)
                for n in range(4):
                    pool.wait_ge(scattered[n], 32 * i + 32)
                    pool.sem_inc(row_free[n], 1)

        @block.scalar
        def _(act):
            act.wait_ge(shifted, 1)
            act.activation(ex[:], ex[:], ACT.Exp).then_inc(exped, 1)

        @block.tensor
        def _(pe):
            pe.wait_ge(loaded, 16 * 6)
            with pe.Fori(0, BITS) as i:
                pe.wait_ge(counted, i + 1)
                pe.matmul(ps_cnt, ones[:], cnt[:], start=True, stop=True).then_inc(summed, 1)
            pe.wait_ge(above_counted, 1)
            pe.matmul(ps_above, ones[:], cnt[:], start=True, stop=True).then_inc(above_summed, 1)
            for n, marks in enumerate((tie, keep)):
                flat = marks[:].rearrange("p e c -> p (e c)")
                pe.wait_ge(marked, n + 1)
                for b in range(2):
                    at = slice(512 * b, 512 * b + 512)
                    pe.matmul(ps_pre[:, at], before[:], flat[:, at], start=True, stop=True)
                    last = pe.matmul(ps_tot[:, at], ones[:], flat[:, at], start=True, stop=True)
                last.then_inc(prefixed, 1)

        @block.vector
        def _(dve):
            link = Link(dve, v_link, 0)
            link.per = None

            def vlink(ins):
                link.n += 1
                ins.then_inc(v_link, 1)
                dve.wait_ge(v_link, link.n)

            def cols(ap):
                return ap.rearrange("p e c -> p c e")

            dve.memset(flat1[:], 1.0)
            dve.memset(bound[:], 0)
            dve.memset(bit_f[:], float(2 ** (BITS - 1)))
            dve.wait_ge(loaded, 16 * 6)
            vlink(dve.tensor_reduce(top[:], lg[:], AX.X, ALU.max))
            dve.tensor_tensor(ex[:], lg[:], spread(top[:], 2, E), ALU.subtract).then_inc(shifted, 1)
            dve.wait_ge(exped, 1)
            dve.tensor_reduce(total[:], ex[:], AX.X, ALU.add)
            vlink(dve.tensor_reduce(top[:], ex[:], AX.X, ALU.max))
            dve.reciprocal(gain[:], total[:])
            vlink(dve.tensor_tensor(cols(mine[:]), ex[:], spread(top[:], 2, E), ALU.is_equal))
            vlink(dve.tensor_tensor(cols(hit[:]), cols(mine[:]), spread(order[:], 1, COLS), ALU.mult))
            vlink(dve.tensor_reduce(top[:], cols(hit[:]), AX.X, ALU.max))
            vlink(dve.tensor_tensor(mine[:], hit[:], spread(top[:], 1, E), ALU.is_equal))
            vlink(dve.tensor_tensor(own[:], mine[:], spread(gain[:], 1, E), ALU.mult))
            step = Link(dve, s_link, 6)
            with dve.Fori(0, BITS) as i:
                step.round(i)
                step(dve.tensor_copy(bit_i[:], bit_f[:]))
                step(dve.tensor_tensor(cand[:], bound[:], bit_i[:], ALU.bitwise_or))
                step(dve.tensor_tensor(hit[:], own[:], spread(cand[:].bitcast(FP32), 2, COLS), ALU.is_ge))
                dve.tensor_reduce(cnt[:], hit[:], AX.X, ALU.add).then_inc(counted, 1)
                dve.wait_ge(summed, i + 1)
                step(dve.scalar_tensor_tensor(won[:], ps_cnt, float(CAPACITY), bit_f[:], ALU.is_ge, ALU.mult))
                step(dve.tensor_tensor(bound[:], bound[:], won[:], ALU.bitwise_or))
                step(dve.tensor_scalar(bit_f[:], bit_f[:], 0.5, None, ALU.mult))
                step.end()
            level = spread(bound[:].bitcast(FP32), 2, COLS)
            dve.tensor_tensor(above[:], own[:], level, ALU.is_gt)
            vlink(dve.tensor_tensor(hit[:], own[:], level, ALU.is_equal))
            dve.tensor_reduce(cnt[:], above[:], AX.X, ALU.add).then_inc(above_counted, 1)
            dve.tensor_tensor(tie[:], hit[:], mine[:], ALU.mult).then_inc(marked, 1)
            dve.wait_ge(above_summed, 1)
            vlink(dve.tensor_scalar(need[:], ps_above, -1.0, float(CAPACITY), ALU.mult, ALU.add))

            def prefix(n):
                dve.wait_ge(prefixed, n)
                flat = sums[:].rearrange("p e c -> p (e c)")
                out = rank[:].rearrange("p e c -> p (e c)")
                vlink(dve.tensor_tensor_scan(flat, flat1[:], ps_tot, 0.0, ALU.mult, ALU.add))
                vlink(dve.tensor_tensor(flat, flat, ps_tot, ALU.subtract))
                dve.tensor_copy(base[:], sums[:, :, 0])
                vlink(dve.tensor_tensor(out, flat, ps_pre, ALU.add))
                vlink(dve.tensor_tensor(rank[:], rank[:], spread(base[:], 2, COLS), ALU.subtract))

            prefix(1)
            vlink(dve.tensor_tensor(hit[:], rank[:], spread(need[:], 2, COLS), ALU.is_lt))
            vlink(dve.tensor_tensor(hit[:], hit[:], tie[:], ALU.mult))
            dve.tensor_tensor(keep[:], hit[:], above[:], ALU.add).then_inc(marked, 1)
            prefix(2)
            vlink(dve.tensor_tensor(rank[:], rank[:], spread(offset[:], 2, COLS), ALU.add))
            dve.tensor_reduce(kept[:], cols(keep[:]), AX.X, ALU.add)
            vlink(dve.tensor_tensor(hit[:], rank[:], keep[:], ALU.mult))
            vlink(dve.tensor_reduce(slot_f[:], cols(hit[:]), AX.X, ALU.add))
            vlink(dve.tensor_tensor(total[:], kept[:], spare[:], ALU.mult))
            vlink(dve.tensor_tensor(slot_f[:], slot_f[:], total[:], ALU.subtract))
            dve.tensor_tensor(slot[:], slot_f[:], spare[:], ALU.add).then_inc(slots_done, 1)


def stage_c(nc, dr, y_out):
    PER = SLOTS // BATCH
    SUB = BATCH // 128
    M = HID // 128
    with ExitStack() as ctx:
        sb, sb2, sem, sem2 = allocators(nc, ctx)
        ident = sb("c_ident", [128, 128])
        ones_row = sb("c_ones_row", [1, 128])
        w1 = sb2("c_w1", [FB, 2, HID])
        w2 = sb2("c_w2", [128, M, D])
        b2 = sb2("c_b2", [1, D])
        xs = sb2("c_xs", [128, SUB, D])
        xT = sb2("c_xT", [FB, 2, BATCH])
        gT = sb2("c_gT", [128, M, BATCH])
        yo = sb2("c_yo", [128, SUB, D])
        ps = ctx.enter_context(nc.psum_tensor("c_ps", [128, 8, 512], FP32))
        UP, DOWN, UPS = 2, 6, 4

        loaded = sem("c_loaded")
        ones_set = sem("c_ones_set")
        w_in = sem2("c_w_in")
        w_free = sem2("c_w_free")
        x_in = sem2("c_x_in")
        flipped = sem2("c_flipped")
        xT_done = sem2("c_xT_done")
        up_done = sem("c_up_done")
        gelued = sem("c_gelued")
        down_done = sem("c_down_done")
        y_done = sem("c_y_done")
        yo_free = sem2("c_yo_free")

        view = dr["rows"][0:E * SLOTS, :].rearrange("(n p s) f -> n p (s f)", p=128, s=SUB)
        batches = [(e2, b) for e2 in range(2) for b in range(PER)]
        NB = len(batches)
        block = ctx.enter_context(nc.Block())

        @block.sync
        def _(sp):
            sp.dma_start(ident[:], dr["ident"]).then_inc(loaded, 16)
            for e2 in range(2):
                sp.sem_inc(w_free[e2], 1)
                sp.sem_inc(flipped[e2], 1)
            with sp.Fori(0, E // 2) as i:
                for n, (e2, b) in enumerate(batches):
                    if b == 0:
                        e = 2 * i + e2
                        sp.wait_ge(w_free[e2], i + 1)
                        sp.dma_start(w1[e2][:], dr["we1"][bass.ds(e, 1)].rearrange("a p k m -> (a p) k m")).then_inc(w_in[e2], 16)
                        sp.dma_start(w2[e2][:], dr["we2"][bass.ds(e, 1)].rearrange("a p k m -> (a p) k m")).then_inc(w_in[e2], 16)
                        sp.dma_start(b2[e2][:], dr["be2"][bass.ds(e, 1)]).then_inc(w_in[e2], 16)
                    sp.wait_ge(flipped[n % 2], i * (NB // 2) + n // 2 + 1)
                    sp.dma_start(xs[n % 2][:].rearrange("p s f -> p (s f)"),
                                 view[bass.ds(NB * i + n, 1)].rearrange("a p f -> (a p) f")).then_inc(x_in[n % 2], 16)

        @block.gpsimd
        def _(pool):
            pool.sem_inc(yo_free[0], 1)
            pool.sem_inc(yo_free[1], 1)
            with pool.Fori(0, E // 2) as i:
                for n in range(NB):
                    pool.wait_ge(y_done, i * NB + n + 2)
                    pool.dma_start(view[bass.ds(NB * i + n, 1)].rearrange("a p f -> (a p) f"),
                                   yo[n % 2][:].rearrange("p s f -> p (s f)")).then_inc(y_out[n % 2], 16)
                    pool.wait_ge(y_out[n % 2], 16 * (i * (NB // 2) + n // 2 + 1))
                    pool.sem_inc(yo_free[n % 2], 1)

        @block.scalar
        def _(act):
            with act.Fori(0, E // 2) as i:
                for n in range(NB):
                    for m in range(M):
                        at = n * M + m
                        act.wait_ge(up_done, i * NB * M + at + 1)
                        act.activation(gT[n % 2][:, m, :], ps[:, UP + at % UPS, :], ACT.Gelu).then_inc(gelued, 1)

        @block.tensor
        def _(pe):
            pe.wait_ge(loaded, 16)
            pe.wait_ge(ones_set, 3)
            pe.sem_inc(gelued, UPS)
            pe.sem_inc(y_done, 1)

            def flip(i, n):
                pe.wait_ge(x_in[n % 2], 16 * (i * (NB // 2) + n // 2 + 1))
                for k in range(2):
                    for s in range(SUB):
                        last = pe.transpose(ps[0:F, k, s * 128:(s + 1) * 128], xs[n % 2][:, s, k * F:(k + 1) * F], ident[:])
                last.then_inc(flipped[n % 2], 1)

            with pe.Fori(0, E // 2) as i:
                for n, (e2, b) in enumerate(batches):
                    if n == 0:
                        flip(i, 0)
                    if b == 0:
                        pe.wait_ge(w_in[e2], 48 * i + 48)
                    pe.wait_ge(xT_done[n % 2], i * (NB // 2) + n // 2 + 1)
                    for m in range(M):
                        at = n * M + m
                        pe.wait_ge(gelued, i * NB * M + at + 1)
                        for k in range(2):
                            last = pe.matmul(ps[:, UP + at % UPS, :], w1[e2][:, k, m * 128:(m + 1) * 128],
                                             xT[n % 2][:, k, :], start=(k == 0), stop=(k == 1))
                        last.then_inc(up_done, 1)
                    if n + 1 < NB:
                        flip(i, n + 1)
                    pe.wait_ge(gelued, i * NB * M + (n + 1) * M + UPS)
                    pe.wait_ge(y_done, i * NB + n + 1)
                    for s in range(SUB):
                        out = ps[:, DOWN + s // 2, (s % 2) * D:(s % 2 + 1) * D]
                        for m in range(M):
                            pe.matmul(out, gT[n % 2][:, m, s * 128:(s + 1) * 128], w2[e2][:, m, :],
                                      start=(m == 0), stop=False)
                        last = pe.matmul(out, ones_row[0:1, :], b2[e2][0:1, :], start=False, stop=True)
                    last.then_inc(down_done, 1)
                    if b == PER - 1:
                        pe.sem_inc(w_free[e2], 1)

        @block.vector
        def _(dve):
            dve.memset(ones_row[:], 1.0).then_inc(ones_set, 1)
            for q in range(2):
                dve.memset(xT[q][F:FB, :, :], 1.0).then_inc(ones_set, 1)

            def features(i, n):
                dve.wait_ge(flipped[n % 2], i * (NB // 2) + n // 2 + 2)
                dve.tensor_copy(xT[n % 2][0:F, :, :], ps[0:F, 0:2, :]).then_inc(xT_done[n % 2], 1)

            with dve.Fori(0, E // 2) as i:
                for n in range(NB):
                    if n == 0:
                        features(i, 0)
                    if n + 1 < NB:
                        features(i, n + 1)
                    dve.wait_ge(down_done, i * NB + n + 1)
                    dve.wait_ge(yo_free[n % 2], i * (NB // 2) + n // 2 + 1)
                    dve.tensor_copy(yo[n % 2][:].rearrange("p (b s) f -> p b (s f)", b=2), ps[:, DOWN:DOWN + 2, 0:2 * D]
                                    ).then_inc(y_done, 1)


def stage_d(nc, dr, gathered):
    KR = K_ROUTED
    G4 = 3 * KR
    CW = 3 * T
    PAIRS = H1N // 2
    with ExitStack() as ctx:
        sb, sb2, sem, sem2 = allocators(nc, ctx)
        ident = sb("d_ident", [128, 128])
        ones_row = sb("d_ones_row", [1, 128])
        half = sb("d_half", [T, 4])
        rope = sb("d_rope", [F, 2, SEQ])
        causal = sb("d_causal", [T, CW])
        earlier = sb("d_earlier", [T, 2, SEQ])
        places = sb("d_places", [T, KR])
        blocks = sb("d_blocks", [F, 2, 6, KR])
        wq = sb("d_wq", [FB, 2, 2, D])
        wk = sb("d_wk", [FB, 2, 2, D])
        wv = sb("d_wv", [FB, 2, D])
        wp = sb("d_wp", [FB, 2, D])
        wr = sb("d_wr", [FB, 2, 1])
        uq = sb("d_uq", [FB, 2, D])
        uk = sb("d_uk", [FB, 2, D])
        uv = sb("d_uv", [FB, 2, D])
        uo = sb("d_uo", [FB, 2, D])
        um = sb("d_um", [FB, 2, D])
        w1 = sb("d_w1", [FB, 2, HID])
        w2 = sb("d_w2", [128, 6, D])
        b2 = sb("d_b2", [1, D])
        g1 = sb("d_g1", [F, 2])
        c1 = sb("d_c1", [F, 2])
        g2 = sb("d_g2", [F, 2])
        c2 = sb("d_c2", [F, 2])

        h1 = sb2("d_h1", [T, 2, D])
        yx = sb2("d_yx", [T, 2, D])
        idx = sb2("d_idx", [T, 2], INT32)
        gain = sb2("d_gain", [T, 2])
        h2 = sb2("d_h2", [T, 2, D])
        st = sb2("d_st", [T, 2, 6])
        mv = sb2("d_mv", [T, 2, 2])
        vv = sb2("d_vv", [T, 2, 2])
        rr = sb2("d_rr", [T, 2, 2])
        xr = sb2("d_xr", [T, 2, D])
        aT = sb2("d_aT", [FB, 2, SEQ])
        rot = sb2("d_rot", [F, 2, 2, SEQ])
        qT = sb2("d_qT", [F, 2, SEQ])
        qz = sb2("d_qz", [F, 2, 6, SEQ])
        kT = sb2("d_kT", [F, 2, SEQ])
        vx = sb2("d_vx", [T, 2, H1N, DH + 1])
        s_sb = sb2("d_s", [T, 4, CW])
        mx = sb2("d_mx", [T, PAIRS, 2, 2])
        nmx = sb2("d_nmx", [T, PAIRS, 2, 2])
        pT = sb2("d_pT", [T, 4, CW])
        rs = sb2("d_rs", [T, 2, 2])
        o_sb = sb2("d_o", [T, 2, D])
        h3 = sb2("d_h3", [T, 2, D])
        hid = sb2("d_hid", [T, 2, D])
        nT = sb2("d_nT", [FB, 2, SEQ])
        kT2 = sb2("d_kT2", [F, 2, SEQ])
        v2 = sb2("d_v2", [T, 2, D])
        sg = sb2("d_sg", [T, 2])
        score = sb2("d_score", [T, 2])
        wide = sb2("d_wide", [T, 2, T])
        srow = sb2("d_srow", [T, SEQ])
        junk = sb2("d_junk", [T, SEQ])
        less = sb2("d_less", [T, 2])
        ties = sb2("d_ties", [T, 2])
        rank = sb2("d_rank", [T, 2])
        away = sb2("d_away", [T, 2])
        sel = sb2("d_sel", [T, 2, KR])
        selT = sb2("d_selT", [KR, SEQ])
        ssum = sb2("d_ssum", [T, 1])
        pool_r = sb2("d_pool_r", [F, 2])
        pool_t = sb2("d_pool_t", [F, 2])
        mT = sb2("d_mT", [FB, 2, SEQ])
        xq = sb2("d_xq", [FB, 2, KR])
        qb = sb2("d_qb", [F, 2, 6, KR])
        mx2 = sb2("d_mx2", [G4, 4])
        nmx2 = sb2("d_nmx2", [G4, 4])
        p2 = sb2("d_p2", [G4, 4, SEQ])
        sum2 = sb2("d_sum2", [G4, 4])
        rs2 = sb2("d_rs2", [G4, 4])
        pT2 = sb2("d_pT2", [T, 4, 2, G4])
        cb = sb2("d_cb", [F, 2, 6, KR])
        cT = sb2("d_cT", [FB, 2, KR])
        ao = sb2("d_ao", [KR, D])
        hm = sb2("d_hm", [T, 2, D])
        gT = sb2("d_gT", [128, 6, SEQ])
        y = sb2("d_y", [T, 2, D])
        ps = [ctx.enter_context(nc.psum_tensor(f"d_ps{im}", [128, 4, 512], FP32)) for im in range(2)]

        weights = [(ident, "ident"), (rope, "rope"), (causal, "causal"), (earlier, "earlier"), (places, "places"),
                   (blocks, "blocks"), (wq, "dq"), (wk, "dk"), (wv, "dv"), (wp, "dp"), (wr, "wr"), (uq, "uq"),
                   (uk, "uk"), (uv, "uv"), (uo, "uo"), (um, "um"), (w1, "u1"), (w2, "u2"), (b2, "ub2"),
                   (g1, "g1"), (c1, "c1"), (g2, "g2"), (c2, "c2")]
        W_IN = 16 * len(weights)
        CONSTS = 12
        weights_in = sem("d_weights_in")
        consts_set = sem("d_consts_set")
        v_link = sem("d_v_link")
        fence = sem("d_fence")
        rows_in = sem2("d_rows_in")
        h2_done = sem2("d_h2_done")
        stats = sem2("d_stats")
        rstd = sem2("d_rstd")
        normed = sem2("d_normed")
        flipped = sem2("d_flipped")
        feat = sem2("d_feat")
        q_proj = sem2("d_q_proj")
        v_proj = sem2("d_v_proj")
        k_proj = sem2("d_k_proj")
        turned = sem2("d_turned")
        q_done = sem2("d_q_done")
        q_spread = sem2("d_q_spread")
        k_done = sem2("d_k_done")
        v_copied = sem2("d_v_copied")
        scored = sem2("d_scored")
        masked = sem2("d_masked")
        maxed = sem2("d_maxed")
        exped = sem2("d_exped")
        p_flipped = sem2("d_p_flipped")
        p_copied = sem2("d_p_copied")
        pv_done = sem2("d_pv_done")
        o_done = sem2("d_o_done")
        projected = sem2("d_projected")
        z_done = sem2("d_z_done")
        z_exped = sem2("d_z_exped")
        kv2_proj = sem2("d_kv2_proj")
        kv2_copied = sem2("d_kv2_copied")
        wide_done = sem2("d_wide_done")
        srow_done = sem2("d_srow_done")
        sel_done = sem2("d_sel_done")
        mix_in = sem2("d_mix_in")
        mixed = sem2("d_mixed")
        picked = sem2("d_picked")
        xq_copied = sem2("d_xq_copied")
        selT_copied = sem2("d_selT_copied")
        q2_proj = sem2("d_q2_proj")
        qb_done = sem2("d_qb_done")
        scored2 = sem2("d_scored2")
        maxed2 = sem2("d_maxed2")
        exped2 = sem2("d_exped2")
        p2_done = sem2("d_p2_done")
        p2_flipped = sem2("d_p2_flipped")
        p2_copied = sem2("d_p2_copied")
        pv2_done = sem2("d_pv2_done")
        c_done = sem2("d_c_done")
        ao_proj = sem2("d_ao_proj")
        ao_copied = sem2("d_ao_copied")
        placed = sem2("d_placed")
        up_done = sem2("d_up_done")
        gelued = sem2("d_gelued")
        down_done = sem2("d_down_done")
        y_done = sem2("d_y_done")
        y_out = sem2("d_y_out")

        block = ctx.enter_context(nc.Block())

        @block.sync
        def _(sp):
            load_all(sp, [(tile[:], dr[name]) for tile, name in weights], weights_in)
            with sp.Fori(0, ROUNDS) as i:
                for im in range(2):
                    img = 2 * i + im
                    sp.wait_ge(h2_done[im], i + 1)
                    sp.dma_start(idx[im][:], dr["slot"][:, bass.ds(2 * img, 2)]).then_inc(rows_in[im], 16)
                    sp.dma_start(gain[im][:], dr["gain"][:, bass.ds(2 * img, 2)]).then_inc(rows_in[im], 16)
                    sp.dma_start(h1[im][:].rearrange("p c f -> p (c f)"),
                                 dr["h1"][bass.ds(img, 1)].rearrange("a p f -> (a p) f")).then_inc(rows_in[im], 16)
                for im in range(2):
                    sp.wait_ge(y_done[im], i + 2)
                    sp.dma_start(dr["out"][bass.ds(2 * i + im, 1)].rearrange("a c p f -> p (a c) f"),
                                 y[im][:]).then_inc(y_out[im], 16)
            for im in range(2):
                sp.wait_ge(y_out[im], 16 * ROUNDS + 16)

        @block.gpsimd
        def _(pool):
            pool.memset(half[:], -0.5).then_inc(consts_set, 1)
            pool.wait_ge(consts_set, CONSTS)
            for im in range(2):
                pool.sem_inc(h2_done[im], 1)

            def scale(im, n, kinds):
                pool.wait_ge(stats[im], n)
                pool.tensor_tensor(rr[im][:, 0:kinds, :], vv[im][:, 0:kinds, :],
                                   half[:, 0:2 * kinds].rearrange("p (a c) -> p a c", c=2), ALU.pow
                                   ).then_inc(rstd[im], 1)

            with pool.Fori(0, ROUNDS) as i:
                for im in range(2):
                    pool.wait_ge(rows_in[im], 48 * i + 48)
                    pool.sem_inc(fence, 1)
                    for c in range(2):
                        pool.indirect_dma_start(out=yx[im][:, c, :], out_offset=None, in_=dr["rows"],
                                                in_offset=bass.IndirectOffsetOnAxis(ap=idx[im][:, c:c + 1], axis=0)
                                                ).then_inc(gathered[im], 16)
                for im in range(2):
                    scale(im, 3 * i + 1, 1)
                for im in range(2):
                    pool.wait_ge(turned[im], 2 * i + 1)
                    pool.tensor_tensor(qT[im][:], rot[im][:, :, 0, :], rot[im][:, :, 1, :], ALU.add).then_inc(q_done[im], 1)
                for im in range(2):
                    pool.wait_ge(turned[im], 2 * i + 2)
                    pool.tensor_tensor(kT[im][:], rot[im][:, :, 0, :], rot[im][:, :, 1, :], ALU.add).then_inc(k_done[im], 1)
                for im in range(2):
                    scale(im, 3 * i + 2, 2)
                for im in range(2):
                    scale(im, 3 * i + 3, 1)

        @block.scalar
        def _(act):
            act.wait_ge(weights_in, W_IN)
            act.wait_ge(consts_set, CONSTS)

            def features(i, n, im, bank, out, g=None, b=None):
                act.wait_ge(flipped[im], 4 * i + n)
                if g is None:
                    act.activation(out[0:F, :, :].rearrange("p k n -> p (k n)"), ps[im][0:F, bank, 0:2 * SEQ],
                                   ACT.Copy).then_inc(feat[im], 1)
                else:
                    for k in range(2):
                        last = act.activation(out[0:F, k, :], ps[im][0:F, bank, k * SEQ:(k + 1) * SEQ], ACT.Identity,
                                              scale=g[:, k:k + 1], bias=b[:, k:k + 1])
                    last.then_inc(feat[im], 1)

            with act.Fori(0, ROUNDS) as i:
                for im in range(2):
                    features(i, 1, im, 3, aT[im])
                for im in range(2):
                    act.wait_ge(v_proj[im], i + 1)
                    act.activation(vx[im][:, :, :, 0:DH],
                                   ps[im][0:T, 3, 0:2 * D].rearrange("p (c h d) -> p c h d", c=2, d=DH),
                                   ACT.Copy).then_inc(v_copied[im], 1)
                for im in range(2):
                    act.wait_ge(q_done[im], i + 1)
                    for h in range(6):
                        last = act.activation(qz[im][:, 1, h, :], qT[im][:, 1, :], ACT.Copy, scale=blocks[:, 1, h, 0:1])
                    last.then_inc(q_spread[im], 1)

                def exps(p, im):
                    act.wait_ge(maxed[im], PAIRS * i + p + 1)
                    for n in range(2):
                        rows = s_sb[im][:, 2 * (p % 2) + n, :]
                        for ci, at in enumerate((slice(0, T), slice(T, CW))):
                            last = act.activation(rows[:, at], rows[:, at], ACT.Exp, scale=DH ** -0.5,
                                                  bias=nmx[im][:, p, n, ci:ci + 1])
                    last.then_inc(exped[im], 1)

                for im in range(2):
                    exps(0, im)
                for p in range(PAIRS):
                    bank = 2 * (p % 2) + 1
                    for im in range(2):
                        act.wait_ge(p_flipped[im], PAIRS * i + p + 1)
                        act.activation(pT[im][:, bank, :], ps[im][0:T, bank, 0:CW], ACT.Copy).then_inc(p_copied[im], 1)
                    for im in range(2):
                        if p < PAIRS - 1:
                            exps(p + 1, im)
                for im in range(2):
                    features(i, 2, im, 1, aT[im])
                for im in range(2):
                    features(i, 3, im, 0, nT[im], g1, c1)
                for im in range(2):
                    act.wait_ge(z_done[im], i + 1)
                    act.activation(sg[im][:], ps[im][0:T, 1, 0:2], ACT.Exp, scale=-1.0).then_inc(z_exped[im], 1)
                for im in range(2):
                    act.wait_ge(kv2_proj[im], i + 1)
                    act.activation(kT2[im][:].rearrange("p m n -> p (m n)"), ps[im][0:F, 2, 0:2 * SEQ], ACT.Copy)
                    act.activation(v2[im][:].rearrange("p c f -> p (c f)"), ps[im][0:T, 3, 0:2 * D],
                                   ACT.Copy).then_inc(kv2_copied[im], 1)
                for im in range(2):
                    act.wait_ge(picked[im], i + 1)
                    for k in range(2):
                        act.activation(xq[im][0:F, k, :], ps[im][0:F, 2, k * KR:(k + 1) * KR], ACT.Identity,
                                       scale=g1[:, k:k + 1], bias=c1[:, k:k + 1]).then_inc(xq_copied[im], 1)
                    act.activation(selT[im][:], ps[im][0:KR, 3, 0:SEQ], ACT.Copy).then_inc(selT_copied[im], 1)
                for im in range(2):
                    act.wait_ge(maxed2[im], i + 1)
                    for gr in range(4):
                        src = ps[im][0:G4, 1 + 2 * (gr // 2), (gr % 2) * SEQ:(gr % 2 + 1) * SEQ]
                        last = act.activation(p2[im][:, gr, :], src, ACT.Exp, scale=DH ** -0.5,
                                              bias=nmx2[im][:, gr:gr + 1], accum_out=sum2[im][:, gr:gr + 1])
                    last.then_inc(exped2[im], 1)
                for im in range(2):
                    act.wait_ge(p2_flipped[im], i + 1)
                    act.activation(pT2[im][:].rearrange("p (b g) c n -> p b (g c n)", b=2), ps[im][0:T, 1:4:2, 0:4 * G4],
                                   ACT.Copy).then_inc(p2_copied[im], 1)
                for im in range(2):
                    act.wait_ge(ao_proj[im], i + 1)
                    act.activation(ao[im][:], ps[im][0:KR, 1, 0:D], ACT.Copy).then_inc(ao_copied[im], 1)
                for im in range(2):
                    features(i, 4, im, 0, aT[im], g2, c2)
                for im in range(2):
                    act.wait_ge(up_done[im], i + 1)
                    act.activation(gT[im][:].rearrange("p (b m) n -> p b (m n)", m=2), ps[im][:, 1:4, 0:2 * SEQ],
                                   ACT.Gelu).then_inc(gelued[im], 1)

        @block.tensor
        def _(pe):
            pe.wait_ge(weights_in, W_IN)
            pe.wait_ge(consts_set, CONSTS)
            for im in range(2):
                pe.sem_inc(y_done[im], 1)

            def flip(im, src, bank):
                for k in range(2):
                    for c in range(2):
                        last = pe.transpose(ps[im][0:F, bank, k * SEQ + c * T:k * SEQ + (c + 1) * T],
                                            src[:, c, k * F:(k + 1) * F], ident[0:T, 0:T])
                last.then_inc(flipped[im], 1)

            def to_tokens(im, bank, src, w, n):
                for c in range(2):
                    for k in range(2):
                        last = pe.matmul(ps[im][0:T, bank, c * n:(c + 1) * n], src[:, k, c * T:(c + 1) * T],
                                         w[:, k, :], start=(k == 0), stop=(k == 1))
                return last

            def rotary(im, w):
                for m in range(2):
                    for v in range(2):
                        for k in range(2):
                            last = pe.matmul(ps[im][0:F, m, v * SEQ:(v + 1) * SEQ], w[:, k, v, m * F:(m + 1) * F],
                                             aT[im][:, k, :], start=(k == 0), stop=(k == 1))
                return last

            with pe.Fori(0, ROUNDS) as i:
                for im in range(2):
                    pe.wait_ge(normed[im], 3 * i + 1)
                    pe.wait_ge(y_done[im], i + 1)
                    flip(im, xr[im], 3)
                for im in range(2):
                    pe.wait_ge(feat[im], 4 * i + 1)
                    rotary(im, wq).then_inc(q_proj[im], 1)
                    to_tokens(im, 3, aT[im], wv, D).then_inc(v_proj[im], 1)
                for im in range(2):
                    pe.wait_ge(turned[im], 2 * i + 1)
                    rotary(im, wk).then_inc(k_proj[im], 1)

                def score(p, im):
                    if p == 0:
                        pe.wait_ge(q_spread[im], 2 * i + 2)
                        pe.wait_ge(k_done[im], i + 1)
                        pe.wait_ge(v_copied[im], i + 1)
                    elif p > 1:
                        pe.wait_ge(o_done[im], PAIRS * i + p - 1)
                    m = p // 3
                    for n in range(2):
                        out = ps[im][0:T, 2 * (p % 2) + n, 0:CW]
                        q = qz[im][:, m, 2 * p - 6 * m + n, :]
                        pe.matmul(out[:, 0:T], q[:, 0:T], kT[im][:, m, 0:T], start=True, stop=True)
                        last = pe.matmul(out[:, T:CW], q[:, T:SEQ], kT[im][:, m, :], start=True, stop=True)
                    last.then_inc(scored[im], 1)

                for im in range(2):
                    score(0, im)
                for p in range(PAIRS):
                    for im in range(2):
                        pe.wait_ge(exped[im], PAIRS * i + p + 1)
                        for n in range(2):
                            bank = 2 * (p % 2) + n
                            for b in range(3):
                                last = pe.transpose(ps[im][0:T, bank, b * T:(b + 1) * T],
                                                    s_sb[im][:, bank, b * T:(b + 1) * T], ident[0:T, 0:T])
                        last.then_inc(p_flipped[im], 1)
                    for im in range(2):
                        if p < PAIRS - 1:
                            score(p + 1, im)
                    for im in range(2):
                        pe.wait_ge(p_copied[im], 2 * (PAIRS * i + p) + 2)
                        for ci in range(2):
                            for n in range(2):
                                at = (2 * ci + n) * (DH + 1)
                                for cj in range(ci + 1):
                                    b = ci + cj
                                    last = pe.matmul(ps[im][0:T, 2 * (p % 2), at:at + DH + 1],
                                                     pT[im][:, 2 * (p % 2) + n, b * T:(b + 1) * T],
                                                     vx[im][:, cj, 2 * p + n, :], start=(cj == 0), stop=(cj == ci))
                        last.then_inc(pv_done[im], 1)
                for im in range(2):
                    pe.wait_ge(o_done[im], PAIRS * i + PAIRS)
                    flip(im, o_sb[im], 1)
                for im in range(2):
                    pe.wait_ge(feat[im], 4 * i + 2)
                    to_tokens(im, 2, aT[im], wp, D).then_inc(projected[im], 1)
                for im in range(2):
                    pe.wait_ge(normed[im], 3 * i + 2)
                    flip(im, xr[im], 0)
                for im in range(2):
                    pe.wait_ge(feat[im], 4 * i + 3)
                    to_tokens(im, 1, nT[im], wr, 1).then_inc(z_done[im], 1)
                    for m in range(2):
                        for k in range(2):
                            pe.matmul(ps[im][0:F, 2, m * SEQ:(m + 1) * SEQ], uk[:, k, m * F:(m + 1) * F], nT[im][:, k, :],
                                      start=(k == 0), stop=(k == 1))
                    to_tokens(im, 3, nT[im], uv, D).then_inc(kv2_proj[im], 1)
                for im in range(2):
                    pe.wait_ge(wide_done[im], i + 1)
                    for c in range(2):
                        last = pe.transpose(ps[im][0:T, 1, c * T:(c + 1) * T], wide[im][:, c, :], ident[0:T, 0:T])
                    last.then_inc(srow_done[im], 1)
                for im in range(2):
                    pe.wait_ge(sel_done[im], i + 1)
                    pe.wait_ge(kv2_copied[im], i + 1)
                    for k in range(2):
                        for c in range(2):
                            pe.matmul(ps[im][0:F, 2, k * KR:(k + 1) * KR], xr[im][:, c, k * F:(k + 1) * F],
                                      sel[im][:, c, :], start=(c == 0), stop=(c == 1))
                    for c in range(2):
                        last = pe.transpose(ps[im][0:KR, 3, c * T:(c + 1) * T], sel[im][:, c, :], ident[0:T, 0:T])
                    last.then_inc(picked[im], 1)
                for im in range(2):
                    pe.wait_ge(mix_in[im], i + 1)
                    to_tokens(im, 0, mT[im], um, D).then_inc(mixed[im], 1)
                for im in range(2):
                    pe.wait_ge(xq_copied[im], 2 * i + 2)
                    for m in range(2):
                        for k in range(2):
                            last = pe.matmul(ps[im][0:F, 2, m * KR:(m + 1) * KR], uq[:, k, m * F:(m + 1) * F],
                                             xq[im][:, k, :], start=(k == 0), stop=(k == 1))
                    last.then_inc(q2_proj[im], 1)
                for im in range(2):
                    pe.wait_ge(qb_done[im], i + 1)
                    pe.wait_ge(selT_copied[im], i + 1)
                    for m in range(2):
                        for t in range(2):
                            last = pe.matmul(ps[im][0:G4, 1 + 2 * m, t * SEQ:(t + 1) * SEQ],
                                             qb[im][:, m, 3 * t:3 * t + 3, :].rearrange("p h r -> p (h r)"),
                                             kT2[im][:, m, :], start=True, stop=True)
                    last.then_inc(scored2[im], 1)
                for im in range(2):
                    pe.wait_ge(p2_done[im], i + 1)
                    for gr in range(4):
                        for cj in range(2):
                            at = ((gr % 2) * 2 + cj) * G4
                            last = pe.transpose(ps[im][0:T, 1 + 2 * (gr // 2), at:at + G4],
                                                p2[im][:, gr, cj * T:(cj + 1) * T], ident[0:G4, 0:G4])
                    last.then_inc(p2_flipped[im], 1)
                for im in range(2):
                    pe.wait_ge(p2_copied[im], i + 1)
                    for m in range(2):
                        for cj in range(2):
                            last = pe.matmul(ps[im][0:F, 2, m * 2 * G4:(m + 1) * 2 * G4], v2[im][:, cj, m * F:(m + 1) * F],
                                             pT2[im][:, 2 * m:2 * m + 2, cj, :], start=(cj == 0), stop=(cj == 1))
                    last.then_inc(pv2_done[im], 1)
                for im in range(2):
                    pe.wait_ge(c_done[im], i + 1)
                    for k in range(2):
                        last = pe.matmul(ps[im][0:KR, 1, 0:D], cT[im][:, k, :], uo[:, k, :], start=(k == 0), stop=(k == 1))
                    last.then_inc(ao_proj[im], 1)
                for im in range(2):
                    pe.wait_ge(ao_copied[im], i + 1)
                    for c in range(2):
                        last = pe.matmul(ps[im][0:T, 3, c * D:(c + 1) * D], selT[im][:, c * T:(c + 1) * T], ao[im][:],
                                         start=True, stop=True)
                    last.then_inc(placed[im], 1)
                for im in range(2):
                    pe.wait_ge(normed[im], 3 * i + 3)
                    flip(im, xr[im], 0)
                for im in range(2):
                    pe.wait_ge(feat[im], 4 * i + 4)
                    for m in range(6):
                        at = (m % 2) * SEQ
                        for k in range(2):
                            last = pe.matmul(ps[im][:, 1 + m // 2, at:at + SEQ], w1[:, k, m * 128:(m + 1) * 128],
                                             aT[im][:, k, :], start=(k == 0), stop=(k == 1))
                    last.then_inc(up_done[im], 1)
                for im in range(2):
                    pe.wait_ge(gelued[im], i + 1)
                    for c in range(2):
                        out = ps[im][0:T, 0, c * D:(c + 1) * D]
                        for m in range(6):
                            pe.matmul(out, gT[im][:, m, c * T:(c + 1) * T], w2[:, m, :], start=(m == 0), stop=False)
                        last = pe.matmul(out, ones_row[0:1, 0:T], b2[0:1, :], start=False, stop=True)
                    last.then_inc(down_done[im], 1)

        @block.vector
        def _(dve):
            dve.memset(ones_row[:], 1.0).then_inc(consts_set, 1)
            for im in range(2):
                for tile in (aT, nT, mT, xq):
                    dve.memset(tile[im][F:FB, :, :], 1.0).then_inc(consts_set, 1)
                dve.memset(cT[im][F:FB, :, :], 1.0)
                dve.memset(vx[im][:, :, :, DH:DH + 1], 1.0).then_inc(consts_set, 1)
                dve.sem_inc(y_out[im], 16)
            dve.wait_ge(weights_in, W_IN)
            link = Link(dve, v_link, 80)

            def statistics(im, rows, kind):
                dve.bn_stats(st[im][:, 0, :], rows[:, 0, :])
                link(dve.bn_stats(st[im][:, 1, :], rows[:, 1, :]))
                dve.sem_inc(fence, 1)
                dve.bn_aggr(mv[im][:, 0, :], st[im][:, 0, :])
                link(dve.bn_aggr(mv[im][:, 1, :], st[im][:, 1, :]))
                var = mv[im][:, :, 1]
                last = dve.tensor_scalar(vv[im][:, 0, :], var, EPS, None, ALU.add)
                if kind == "both":
                    last = dve.tensor_scalar(vv[im][:, 1, :], var, 1 + EPS, EPS * EPS, ALU.mult, ALU.add)
                last.then_inc(stats[im], 1)

            def normalise(i, n, im, rows, kind=0):
                dve.wait_ge(rstd[im], 3 * i + n)
                for c in range(2):
                    last = dve.tensor_scalar(xr[im][:, c, :], rows[:, c, :], mv[im][:, c, 0:1],
                                             rr[im][:, kind, c:c + 1], ALU.subtract, ALU.mult)
                last.then_inc(normed[im], 1)

            def flat(tile):
                return tile[:].rearrange("p c f -> p (c f)")

            with dve.Fori(0, ROUNDS) as i:
                link.round(i)
                for im in range(2):
                    dve.wait_ge(gathered[im], 32 * i + 32)
                    for c in range(2):
                        last = dve.scalar_tensor_tensor(h2[im][:, c, :], yx[im][:, c, :], gain[im][:, c:c + 1],
                                                        h1[im][:, c, :], ALU.mult, ALU.add)
                    last.then_inc(h2_done[im], 1)
                    dve.wait_ge(h2_done[im], i + 2)
                    statistics(im, h2[im], "one")
                for im in range(2):
                    normalise(i, 1, im, h2[im])
                for n, proj in enumerate((q_proj, k_proj)):
                    for im in range(2):
                        dve.wait_ge(proj[im], i + 1)
                        if n == 1:
                            dve.wait_ge(q_done[im], i + 1)
                        dve.tensor_tensor(rot[im][:].rearrange("p m v n -> p m (v n)"), ps[im][0:F, 0:2, 0:2 * SEQ],
                                          spread(rope[:].rearrange("p v n -> p (v n)"), 1, 2), ALU.mult
                                          ).then_inc(turned[im], 1)
                    for im in range(2):
                        if n == 0:
                            dve.wait_ge(q_done[im], i + 1)
                            dve.tensor_tensor(qz[im][:, 0, :, :], spread(qT[im][:, 0, :], 1, 6),
                                              spread(blocks[:, 0, :, 0], 2, SEQ), ALU.mult).then_inc(q_spread[im], 1)

                def mask_max(p, im):
                    at = slice(2 * (p % 2), 2 * (p % 2) + 2)
                    dve.wait_ge(scored[im], PAIRS * i + p + 1)
                    dve.tensor_tensor(s_sb[im][:, at, :], ps[im][0:T, at, 0:CW], spread(causal[:], 1, 2), ALU.add
                                      ).then_inc(masked[im], 1)
                    dve.wait_ge(masked[im], PAIRS * i + p + 1)
                    dve.tensor_reduce(mx[im][:, p, :, 0], s_sb[im][:, at, 0:T], AX.X, ALU.max)
                    link(dve.tensor_reduce(mx[im][:, p, :, 1], s_sb[im][:, at, T:CW], AX.X, ALU.max))
                    dve.tensor_scalar(nmx[im][:, p, :, :], mx[im][:, p, :, :], -(DH ** -0.5), None, ALU.mult
                                      ).then_inc(maxed[im], 1)

                for im in range(2):
                    mask_max(0, im)
                for p in range(PAIRS):
                    bank = 2 * (p % 2)
                    for im in range(2):
                        dve.wait_ge(p_flipped[im], PAIRS * i + p + 1)
                        dve.tensor_copy(pT[im][:, bank, :], ps[im][0:T, bank, 0:CW]).then_inc(p_copied[im], 1)
                    for im in range(2):
                        if p < PAIRS - 1:
                            mask_max(p + 1, im)
                    for im in range(2):
                        dve.wait_ge(pv_done[im], PAIRS * i + p + 1)
                        o_ps = ps[im][0:T, bank, 0:4 * (DH + 1)].rearrange("p (c h d) -> p c h d", c=2, d=DH + 1)
                        link(dve.reciprocal(rs[im][:], o_ps[:, :, :, DH]))
                        dve.tensor_tensor(o_sb[im][:, :, 2 * p * DH:2 * (p + 1) * DH].rearrange("p c (h d) -> p c h d", d=DH),
                                          o_ps[:, :, :, 0:DH], spread(rs[im][:], 3, DH), ALU.mult).then_inc(o_done[im], 1)
                for im in range(2):
                    dve.wait_ge(projected[im], i + 1)
                    link(dve.tensor_tensor(flat(h3[im]), ps[im][0:T, 2, 0:2 * D], flat(h2[im]), ALU.add))
                    statistics(im, h3[im], "both")
                for im in range(2):
                    normalise(i, 2, im, h3[im], kind=1)
                    for c in range(2):
                        dve.tensor_scalar(hid[im][:, c, :], h3[im][:, c, :], mv[im][:, c, 0:1],
                                          rr[im][:, 0, c:c + 1], ALU.subtract, ALU.mult)
                for im in range(2):
                    dve.wait_ge(z_exped[im], i + 1)
                    link(dve.tensor_scalar(sg[im][:], sg[im][:], 1.0, None, ALU.add))
                    link(dve.reciprocal(score[im][:], sg[im][:]))
                    dve.tensor_copy(wide[im][:], spread(score[im][:], 2, T)).then_inc(wide_done[im], 1)
                for im in range(2):
                    dve.wait_ge(srow_done[im], i + 1)
                    link(dve.tensor_copy(srow[im][:], ps[im][0:T, 1, 0:SEQ]))
                    for c in range(2):
                        link(dve.tensor_scalar(junk[im][:], srow[im][:], score[im][:, c:c + 1], None, ALU.is_lt, ALU.add,
                                               accum_out=less[im][:, c:c + 1]))
                        link(dve.scalar_tensor_tensor(junk[im][:], srow[im][:], score[im][:, c:c + 1], earlier[:, c, :],
                                                      ALU.is_equal, ALU.mult, accum_out=ties[im][:, c:c + 1]))
                    link(dve.tensor_tensor(rank[im][:], less[im][:], ties[im][:], ALU.add))
                    dve.tensor_scalar(away[im][:], rank[im][:], float(KR), None, ALU.is_ge)
                    for c in range(2):
                        last = dve.tensor_scalar(sel[im][:, c, :], places[:], rank[im][:, c:c + 1], None, ALU.is_equal)
                    last.then_inc(sel_done[im], 1)
                for im in range(2):
                    for k in range(2):
                        link(dve.tensor_tensor_reduce(out=junk[im][0:F, :], in0=nT[im][0:F, k, :], in1=srow[im][0:F, :],
                                                      scale=1.0, scalar=0.0, op0=ALU.mult, op1=ALU.add,
                                                      accum_out=pool_r[im][:, k:k + 1]))
                    link(dve.tensor_reduce(ssum[im][:], srow[im][:], AX.X, ALU.add))
                    link(dve.tensor_scalar(ssum[im][:], ssum[im][:], 1e-6, None, ALU.add))
                    link(dve.reciprocal(ssum[im][:], ssum[im][:]))
                    link(dve.tensor_scalar(pool_t[im][:], pool_r[im][:], ssum[im][0:F, :], None, ALU.mult))
                    for k in range(2):
                        last = dve.scalar_tensor_tensor(mT[im][0:F, k, :], srow[im][0:F, :], pool_t[im][:, k:k + 1],
                                                        nT[im][0:F, k, :], ALU.mult, ALU.add)
                    last.then_inc(mix_in[im], 1)
                for im in range(2):
                    dve.wait_ge(q2_proj[im], i + 1)
                    dve.tensor_tensor(qb[im][:], spread(ps[im][0:F, 2, 0:2 * KR].rearrange("p (m r) -> p m r", m=2), 2, 6),
                                      blocks[:], ALU.mult).then_inc(qb_done[im], 1)
                for im in range(2):
                    dve.wait_ge(mixed[im], i + 1)
                    for c in range(2):
                        link(dve.scalar_tensor_tensor(hm[im][:, c, :], ps[im][0:T, 0, c * D:(c + 1) * D],
                                                      away[im][:, c:c + 1], hid[im][:, c, :], ALU.mult, ALU.add))
                for im in range(2):
                    dve.wait_ge(scored2[im], i + 1)
                    link(dve.tensor_reduce(mx2[im][:].rearrange("p (b g) -> p b g", b=2),
                                           ps[im][0:G4, 1:4:2, 0:2 * SEQ].rearrange("p b (g n) -> p b g n", g=2),
                                           AX.X, ALU.max))
                    dve.tensor_scalar(nmx2[im][:], mx2[im][:], -(DH ** -0.5), None, ALU.mult).then_inc(maxed2[im], 1)
                for im in range(2):
                    dve.wait_ge(exped2[im], i + 1)
                    link(dve.reciprocal(rs2[im][:], sum2[im][:]))
                    dve.tensor_tensor(p2[im][:], p2[im][:], spread(rs2[im][:], 2, SEQ), ALU.mult).then_inc(p2_done[im], 1)
                for im in range(2):
                    dve.wait_ge(pv2_done[im], i + 1)
                    link(dve.tensor_tensor(cb[im][:].rearrange("p m h r -> p (m h r)"), ps[im][0:F, 2, 0:4 * G4],
                                           blocks[:].rearrange("p m h r -> p (m h r)"), ALU.mult))
                    dve.tensor_reduce(cT[im][0:F, :, :], cb[im][:].rearrange("p m h r -> p m r h"), AX.X, ALU.add
                                      ).then_inc(c_done[im], 1)
                for im in range(2):
                    dve.wait_ge(placed[im], i + 1)
                    link(dve.tensor_tensor(flat(hm[im]), flat(hm[im]), ps[im][0:T, 3, 0:2 * D], ALU.add))
                    statistics(im, hm[im], "one")
                for im in range(2):
                    normalise(i, 3, im, hm[im])
                    link(dve.tensor_tensor(flat(h3[im]), flat(h3[im]), flat(hm[im]), ALU.add))
                for im in range(2):
                    dve.wait_ge(down_done[im], i + 1)
                    dve.wait_ge(y_out[im], 16 * i + 16)
                    dve.tensor_tensor(flat(y[im]), ps[im][0:T, 0, 0:2 * D], flat(h3[im]), ALU.add).then_inc(y_done[im], 1)
                link.end()


def build(nc, dr):
    with ExitStack() as ctx:
        scattered = [ctx.enter_context(nc.semaphore(f"b_scattered{n}")) for n in range(4)]
        y_out = [ctx.enter_context(nc.semaphore(f"c_y_out{n}")) for n in range(2)]
        gathered = [ctx.enter_context(nc.semaphore(f"d_gathered{n}")) for n in range(2)]
        stage_a(nc, dr)
        stage_b(nc, dr, scattered)
        stage_c(nc, dr, y_out)
        stage_d(nc, dr, gathered)


def dram_views(nc, given):
    dr = dict(given)

    def scratch(name, shape, dt=FP32):
        return nc.dram_tensor(name, shape, dt, kind="Internal").ap()

    band = scratch("band_rows", [2, T, H0 * 2 * PITCH])
    row = H0 * 2 * PITCH
    dr["band"] = [band[im] for im in range(2)]
    dr["band_skew"] = [bass.AP(tensor=band.tensor, offset=im * T * row, ap=[[row + 1, T], [PITCH, 2 * H0], [1, BAND]])
                       for im in range(2)]
    dr["band_read"] = [bass.AP(tensor=band.tensor, offset=im * T * row + PITCH - SEQ,
                               ap=[[row, T], [2 * PITCH, H0], [1, 2 * SEQ]]) for im in range(2)]
    dr["h1"] = scratch("h1_rows", [IMAGES, T, 2 * D])
    dr["xf"] = scratch("xf_rows", [IMAGES, T, 2 * D])
    dr["lg"] = scratch("router_logits", [IMAGES, T, 2 * E])
    dr["slot"] = scratch("slots", [T, COLS], INT32)
    dr["gain"] = scratch("gains", [T, COLS])
    dr["rows"] = scratch("rows", [ROWS, D])
    share = ROWS * D // ROUNDS
    assert share * ROUNDS == ROWS * D and share % 128 == 0
    dr["rows_flat"] = bass.AP(tensor=dr["rows"].tensor, offset=0,
                              ap=[[share, ROUNDS], [share // 128, 128], [1, share // 128]])
    return dr


def lay_out(np, a):
    f32 = np.float32

    def chunks(w, bias=None):
        out = np.zeros((FB, 2, w.shape[1]), w.dtype)
        out[:F] = w.reshape(2, F, -1).transpose(1, 0, 2)
        if bias is not None:
            out[F, 1] = bias.reshape(-1)
        return out

    def cols(v):
        return np.ascontiguousarray(v.reshape(2, F).T)

    def rows128(w):
        return np.ascontiguousarray(w.reshape(-1, 128, w.shape[1]).transpose(1, 0, 2))

    out = {}
    x = a["x"].reshape(IMAGES, 3, 14, 16, 14, 16).transpose(0, 1, 2, 4, 5, 3).reshape(IMAGES, SEQ, 6, 128)
    out["x"] = np.ascontiguousarray(x.transpose(0, 3, 2, 1))
    out["we"] = rows128(a["L0_tok_W"].T)
    out["be"] = a["L0_tok_b"].reshape(1, D)
    out["wq"] = chunks(a["L0_attn_wq"], a["L0_attn_u_param"])
    out["wk"] = chunks(a["L0_attn_wk"])
    out["wv"] = chunks(a["L0_attn_wv"])
    out["wo"] = chunks(a["L0_attn_wo"], a["L0_attn_bo"])
    out["w1"] = chunks(a["L0_attn_w1"], a["L0_attn_b1"])
    out["w2"] = rows128(a["L0_attn_w2"])
    out["b2"] = a["L0_attn_b2"].reshape(1, D)
    out["ws"] = chunks(a["L0_ffn_switch_w"], a["L0_ffn_switch_b"])
    out["n1"] = cols(a["L0_attn_norm1_w"])
    out["n2"] = cols(a["L0_attn_norm2_w"])
    out["wq_t"] = np.ascontiguousarray(a["L0_attn_wq"].T.reshape(H0, DK0, D).transpose(1, 0, 2))
    out["wpos"] = np.ascontiguousarray(a["L0_attn_w_pos"].transpose(1, 0, 2))
    out["vpar"] = np.ascontiguousarray(a["L0_attn_v_param"].T)
    out["we1"] = np.stack([chunks(a["L0_ffn_w1"][e], a["L0_ffn_b1"][e]) for e in range(E)])
    out["we2"] = np.stack([rows128(a["L0_ffn_w2"][e]) for e in range(E)])
    out["be2"] = a["L0_ffn_b2"]
    def rotary(w, bias):
        w, bias = w.T.reshape(D, D // 2, 2), bias.reshape(1, D // 2, 2)
        both = []
        for swap in (slice(None), slice(None, None, -1)):
            both.append(chunks(np.ascontiguousarray(w[:, :, swap]).reshape(D, D),
                               np.ascontiguousarray(bias[:, :, swap]).reshape(1, D)))
        return np.stack(both, axis=2)

    out["dq"] = rotary(a["L1_attn_Wq"], a["L1_attn_bq"])
    out["dk"] = rotary(a["L1_attn_Wk"], a["L1_attn_bk"])
    out["dv"] = chunks(a["L1_attn_Wv"].T, a["L1_attn_bv"])
    out["dp"] = chunks(a["L1_attn_Wp"].T, a["L1_attn_bp"])
    out["wr"] = chunks(a["L1_ffn_Wr"].reshape(D, 1), a["L1_ffn_br"].reshape(1, 1))
    for name, w in (("uq", "q"), ("uk", "k"), ("uv", "v"), ("uo", "o"), ("um", "m")):
        out[name] = chunks(a["L1_ffn_W" + w], a["L1_ffn_b" + w])
    out["u1"] = chunks(a["L1_ffn_W1"], a["L1_ffn_bf1"])
    out["u2"] = rows128(a["L1_ffn_W2"])
    out["ub2"] = a["L1_ffn_bf2"].reshape(1, D)
    out["g1"], out["c1"] = cols(a["L1_ffn_g1"]), cols(a["L1_ffn_b1"])
    out["g2"], out["c2"] = cols(a["L1_ffn_g2"]), cols(a["L1_ffn_b2"])
    inv = (f32(1.0) / f32(10000.0) ** (f32(2.0) * np.arange(DH // 2, dtype=f32) / f32(DH))).astype(f32)
    angle = (np.arange(SEQ, dtype=f32)[:, None] * inv[None, :]).astype(f32)
    table = np.zeros((F // DH, DH, 2, SEQ), f32)
    for j in range(DH):
        table[:, j, 0] = np.cos(angle[:, j // 2])
        table[:, j, 1] = np.sin(angle[:, j // 2]) * (-1 if j % 2 == 0 else 1)
    out["rope"] = table.reshape(F, 2, SEQ)
    later = np.where(np.arange(T)[None, :] > np.arange(T)[:, None], f32(-1e30), f32(0))
    out["causal"] = np.concatenate([later, np.zeros((T, T)), later], axis=1).astype(f32)
    token = np.arange(2)[None, :, None] * T + np.arange(T)[:, None, None]
    out["earlier"] = (np.arange(SEQ)[None, None, :] < token).astype(f32)
    out["places"] = np.tile(np.arange(K_ROUTED, dtype=f32), (T, 1))
    head = (np.arange(F)[:, None] // DH == np.arange(6)[None, :]).astype(f32)
    out["blocks"] = np.ascontiguousarray(np.broadcast_to(head[:, None, :, None], (F, 2, 6, K_ROUTED)))
    out["order"] = np.tile(np.arange(E, 0, -1, dtype=f32), (T, 1))
    out["offset"] = np.tile(np.arange(E, dtype=f32) * SLOTS, (T, 1))
    out["spare"] = (E * SLOTS + np.arange(COLS)[None, :] * T + np.arange(T)[:, None]).astype(f32)
    out["before"] = np.triu(np.ones((T, T), f32), 1)
    out["ones"] = np.ones((T, T), f32)
    out["ident"] = np.eye(128, dtype=f32)
    rate = np.exp(np.log(f32((SEQ + 1) / 2.0)) / f32(NPOS // 2))
    widths = rate ** np.arange(1, NPOS // 2 + 1, dtype=f32)
    d = np.arange(-98, 99)[None, :].astype(f32)
    near = (np.abs(d) <= widths[:, None]).astype(f32)
    assert widths[-1] < 99
    basis = np.zeros((4, NPOS, 4, BAND), f32)
    for hh in range(4):
        basis[hh, :, hh] = np.concatenate([near, np.sign(d) * near])
    out["basis"] = basis.reshape(128, 4, BAND)
    return out


def kernel(**inputs):
    import numpy as np
    import concourse.bacc as bacc
    from concourse.bass_utils import run_bass_kernel_spmd

    nc = bacc.Bacc("TRN2", target_bir_lowering=False, num_devices=1)
    arrays = lay_out(np, {name: np.asarray(v) for name, v in inputs.items()})
    given = {name: nc.dram_tensor(f"in_{name}", v.shape, mybir.dt.from_np(v.dtype), kind="ExternalInput").ap()
             for name, v in arrays.items()}
    given["out"] = nc.dram_tensor("out", [IMAGES, 2, T, D], FP32, kind="ExternalOutput").ap()
    build(nc, dram_views(nc, given))
    run = run_bass_kernel_spmd(nc, [{f"in_{name}": v for name, v in arrays.items()}], core_ids=[0])
    return run.results[0]["out"].reshape(IMAGES, SEQ, D)
```

```python
from contextlib import ExitStack

import concourse.bass as bass
from concourse import mybir

FP32 = mybir.dt.float32
INT32 = mybir.dt.int32
ALU = mybir.AluOpType
ACT = mybir.ActivationFunctionType
AX = mybir.AxisListType

IMAGES, SEQ, D = 64, 196, 192
T = 98
F = 96
FB = F + 1
COLS = 2 * IMAGES
TOKENS = IMAGES * SEQ
ROUNDS = IMAGES // 2
H0, DK0, DV0, NPOS = 8, 64, 24, 32
BAND = 197
PITCH = 294
E, HID = 8, 768
CAPACITY = int(1.25 * TOKENS / E)
SLOTS = 2048
BATCH = 512
ROWS = E * SLOTS + TOKENS
H1N, DH = 12, 16
K_ROUTED = max(1, int(round(0.15 * SEQ)))
EPS = 1e-5


def spread(ap, axis, n):
    dims = [list(d) for d in ap.ap]
    dims.insert(axis, [0, n])
    return bass.AP(tensor=ap.tensor, offset=ap.offset, ap=dims)


class Link:

    def __init__(self, eng, sem, per_round):
        self.eng, self.sem, self.per, self.i, self.n = eng, sem, per_round, 0, 0

    def round(self, i):
        assert self.n in (0, self.per), (self.sem, self.n)
        self.i, self.n = i, 0

    def __call__(self, ins):
        self.n += 1
        ins.then_inc(self.sem, 1)
        self.eng.wait_ge(self.sem, self.i * self.per + self.n)

    def end(self):
        assert self.n == self.per, f"links in a round: {self.n}, not {self.per}"


def allocators(nc, ctx):
    def sb(name, shape, dt=FP32):
        return ctx.enter_context(nc.sbuf_tensor(name, shape, dt))

    def sb2(name, shape, dt=FP32):
        return [sb(f"{name}_{im}", shape, dt) for im in range(2)]

    taken = []

    def sem(name):
        taken.append(nc.alloc_semaphore(name=name))
        return taken[-1]

    def hand_back():
        nc.clear_and_free_semaphores(taken)
        nc.all_engine_barrier()

    ctx.callback(hand_back)

    def sem2(name):
        return [sem(f"{name}_{im}") for im in range(2)]

    return sb, sb2, sem, sem2


def load_all(sp, pairs, arrived):
    for tile, dram in pairs:
        sp.dma_start(tile, dram).then_inc(arrived, 16)
    sp.wait_ge(arrived, 16 * len(pairs))


def stage_a(nc, dr):
    with ExitStack() as ctx:
        sb, sb2, sem, sem2 = allocators(nc, ctx)
        ident = sb("a_ident", [128, 128])
        basis = sb("a_basis", [128, 4, BAND])
        we = sb("a_we", [128, 6, D])
        be = sb("a_be", [1, D])
        ones_row = sb("a_ones_row", [1, 128])
        zero = sb("a_zero", [128, 1356])
        half_neg = sb("a_half_neg", [T, 4])
        wq = sb("a_wq", [FB, 2, H0 * DK0])
        wk = sb("a_wk", [FB, 2, H0 * DK0])
        wv = sb("a_wv", [FB, 2, D])
        wqp = sb("a_wqp", [FB, 2, H0 * NPOS])
        wo = sb("a_wo", [FB, 2, D])
        w1 = sb("a_w1", [FB, 2, 2 * D])
        w2 = sb("a_w2", [128, 3, D])
        b2 = sb("a_b2", [1, D])
        ws = sb("a_ws", [FB, 2, E])
        n1 = sb("a_n1", [F, 2])
        n2 = sb("a_n2", [F, 2])
        wq_t = sb("a_wq_t", [DK0, H0, D])
        wpos = sb("a_wpos", [DK0, H0, NPOS])
        vpar = sb("a_vpar", [DK0, H0])
        vw = sb("a_vw", [1, H0 * NPOS])

        xin = sb2("a_xin", [128, 6, SEQ])
        h0 = sb2("a_h0", [T, 2, D])
        xn = sb2("a_xn", [T, 2, D])
        xr = sb2("a_xr", [T, 2, D])
        st = sb2("a_st", [T, 2, 6])
        mv = sb2("a_mv", [T, 2, 2])
        sq = sb2("a_sq", [T, 2])
        vv = sb2("a_vv", [T, 2])
        rr = sb2("a_rr", [T, 2])
        st_e = sb2("a_st_e", [T, 2, 6])
        mv_e = sb2("a_mv_e", [T, 2, 2])
        vv_e = sb2("a_vv_e", [T, 2, 2])
        rr_e = sb2("a_rr_e", [T, 2, 2])
        xe = sb2("a_xe", [T, 2, D])
        eT = sb2("a_eT", [FB, 2, SEQ])
        skip = sb2("a_skip", [T, 2, D])
        hT = sb2("a_hT", [FB, 2, SEQ])
        qz = sb2("a_qz", [128, H0, SEQ])
        kT = sb2("a_kT", [128, 4, SEQ])
        qwT = sb2("a_qwT", [128, 2, SEQ])
        vx = sb2("a_vx", [T, 2, H0, DV0 + 1])
        band = sb2("a_band", [T, H0, 2 * BAND])
        pos = sb2("a_pos", [T, H0, 2 * SEQ])
        s_sb = sb2("a_s", [T, 4, 2 * SEQ])
        mx = sb2("a_mx", [T, 4, 4])
        nmx = sb2("a_nmx", [T, 4, 4])
        pT = sb2("a_pT", [T, 4, 2 * SEQ])
        rs = sb2("a_rs", [T, 2, 2])
        o_sb = sb2("a_o", [T, 2, D])
        x1 = sb2("a_x1", [T, 2, D])
        gT = sb2("a_gT", [128, 3, SEQ])
        h1 = sb2("a_h1", [T, 2, D])
        xf = sb2("a_xf", [T, 2, D])
        lg = sb2("a_lg", [T, 2, E])
        ps = [ctx.enter_context(nc.psum_tensor(f"a_ps{im}", [128, 4, 512], FP32)) for im in range(2)]

        weights_in = sem("a_weights_in")
        vw_done = sem("a_vw_done")
        wqp_done = sem("a_wqp_done")
        wqp_copied = sem("a_wqp_copied")
        vw_placed = sem("a_vw_placed")
        consts_set = sem("a_consts_set")
        pads_zero = sem("a_pads_zero")
        rows_zero = sem("a_rows_zero")
        fence = sem("a_fence")
        head_links = sem2("a_head_links")
        att_links = sem2("a_att_links")
        x1_links = sem2("a_x1_links")
        tail_links = sem2("a_tail_links")
        x_in = sem2("a_x_in")
        embedded = sem2("a_embedded")
        e_stats = sem2("a_e_stats")
        e_rstd = sem2("a_e_rstd")
        e_normed = sem2("a_e_normed")
        e_flipped = sem2("a_e_flipped")
        e_feat = sem2("a_e_feat")
        stats = sem2("a_stats")
        rstd = sem2("a_rstd")
        normed = sem2("a_normed")
        flipped = sem2("a_flipped")
        feat = sem2("a_feat")
        q_proj = sem2("a_q_proj")
        qw_proj = sem2("a_qw_proj")
        v_proj = sem2("a_v_proj")
        k_proj = sem2("a_k_proj")
        q_copied = sem2("a_q_copied")
        qw_copied = sem2("a_qw_copied")
        v_copied = sem2("a_v_copied")
        k_copied = sem2("a_k_copied")
        band_done = sem2("a_band_done")
        band_copied = sem2("a_band_copied")
        band_out = [sem2(f"a_band_out{g}") for g in range(2)]
        pos_in = [sem2(f"a_pos_in{g}") for g in range(2)]
        scored = sem2("a_scored")
        added = sem2("a_added")
        maxed = sem2("a_maxed")
        exped = sem2("a_exped")
        p_flipped = sem2("a_p_flipped")
        p_copied = sem2("a_p_copied")
        pv_done = sem2("a_pv_done")
        o_done = sem2("a_o_done")
        projected = sem2("a_projected")
        x1_done = sem2("a_x1_done")
        up_done = sem2("a_up_done")
        gelued = sem2("a_gelued")
        down_done = sem2("a_down_done")
        h1_done = sem2("a_h1_done")
        logits = sem2("a_logits")
        lg_done = sem2("a_lg_done")
        out_sent = sem2("a_out_sent")

        block = ctx.enter_context(nc.Block())

        @block.sync
        def _(sp):
            load_all(sp, [(ident[:], dr["ident"]), (basis[:], dr["basis"]), (we[:], dr["we"]), (be[:], dr["be"]),
                          (wq[:], dr["wq"]), (wk[:], dr["wk"]), (wv[:], dr["wv"]), (wo[:], dr["wo"]),
                          (w1[:], dr["w1"]), (w2[:], dr["w2"]), (b2[:], dr["b2"]), (ws[:], dr["ws"]),
                          (n1[:], dr["n1"]), (n2[:], dr["n2"]), (wq_t[:], dr["wq_t"]), (wpos[:], dr["wpos"]),
                          (vpar[:], dr["vpar"])], weights_in)
            sp.wait_ge(wqp_copied, 3)
            sp.dma_start(wqp[F:FB, 1, :], vw[0:1, :]).then_inc(vw_placed, 16)
            sp.wait_ge(consts_set, 7)
            for im in range(2):
                sp.dma_start(dr["band"][im].rearrange("p (a f) -> p a f", f=1176),
                             spread(zero[0:T, 0:1176], 1, 4)).then_inc(pads_zero, 16)
            sp.wait_ge(pads_zero, 32)
            for im in range(2):
                sp.sem_inc(added[im], 4)

            def band_trip(im, i):
                for g in range(2):
                    at = slice(8 * g, 8 * g + 8)
                    sp.wait_ge(band_copied[im], 4 * i + 2 * g + 2)
                    sp.dma_start(dr["band_skew"][im][:, at], band[im][:].rearrange("p h (c b) -> p (h c) b", c=2)[:, at]
                                 ).then_inc(band_out[g][im], 16)
                for g in range(2):
                    at = slice(4 * g, 4 * g + 4)
                    sp.wait_ge(band_out[g][im], 16 * i + 32)
                    if g == 0:
                        sp.wait_ge(added[im], 4 * i + 4)
                    sp.dma_start(pos[im][:, at], dr["band_read"][im][:, at]).then_inc(pos_in[g][im], 16)

            def rows_out(im, i):
                at = bass.ds(2 * i + im, 1)
                sp.wait_ge(h1_done[im], i + 2)
                sp.dma_start(dr["h1"][at].rearrange("a p f -> (a p) f"), h1[im][:].rearrange("p c f -> p (c f)")
                             ).then_inc(out_sent[im], 16)
                sp.wait_ge(normed[im], 2 * i + 2)
                sp.dma_start(dr["xf"][at].rearrange("a p f -> (a p) f"), xf[im][:].rearrange("p c f -> p (c f)")
                             ).then_inc(out_sent[im], 16)
                sp.wait_ge(lg_done[im], i + 2)
                sp.dma_start(dr["lg"][at].rearrange("a p f -> (a p) f"), lg[im][:].rearrange("p c f -> p (c f)")
                             ).then_inc(out_sent[im], 16)

            def zero_rows(i):
                sp.dma_start(dr["rows_flat"][bass.ds(i, 1)].rearrange("a p f -> (a p) f"), zero[:]).then_inc(rows_zero, 16)

            def half(im, i):
                rows_out(im, i)
                band_trip(im, i + 1)

            for im in range(2):
                band_trip(im, 0)
            with sp.Fori(0, ROUNDS - 1) as i:
                zero_rows(i)
                for im in range(2):
                    half(im, i)
            zero_rows(ROUNDS - 1)
            for im in range(2):
                rows_out(im, ROUNDS - 1)
            sp.wait_ge(rows_zero, 16 * ROUNDS)
            for im in range(2):
                sp.wait_ge(out_sent[im], 48 * ROUNDS + 48)

        @block.gpsimd
        def _(pool):
            pool.memset(zero[:], 0.0).then_inc(consts_set, 1)
            pool.memset(half_neg[:], -0.5).then_inc(consts_set, 1)
            pool.wait_ge(consts_set, 7)

            def scale(im, i, n):
                pool.wait_ge(stats[im], 2 * i + n)
                pool.tensor_tensor(rr[im][:], vv[im][:], half_neg[:, 0:2], ALU.pow).then_inc(rstd[im], 1)

            def scale_e(im, i):
                pool.wait_ge(e_stats[im], i + 1)
                pool.tensor_tensor(rr_e[im][:], vv_e[im][:], half_neg[:].rearrange("p (a c) -> p a c", c=2), ALU.pow
                                   ).then_inc(e_rstd[im], 1)

            def half(im, i):
                scale(im, i, 1)
                scale_e(im, i + 1)
                scale(im, i, 2)

            for im in range(2):
                scale_e(im, 0)
            with pool.Fori(0, ROUNDS - 1) as i:
                for im in range(2):
                    half(im, i)
            for im in range(2):
                scale(im, ROUNDS - 1, 1)
                scale(im, ROUNDS - 1, 2)

        @block.scalar
        def _(act):
            act.wait_ge(weights_in, 16 * 17)
            act.wait_ge(consts_set, 7)
            for im in range(2):
                act.sem_inc(band_out[0][im], 16)
                act.sem_inc(band_out[1][im], 16)
                act.sem_inc(embedded[im], 1)

            def load_x(im, i):
                act.wait_ge(embedded[im], i + 1)
                act.dma_start(xin[im][:], dr["x"][bass.ds(2 * i + im, 1)].rearrange("a p k n -> (a p) k n")
                              ).then_inc(x_in[im], 16)

            def features_e(im, i):
                act.wait_ge(e_flipped[im], i + 1)
                for k in range(2):
                    last = act.activation(eT[im][0:F, k, :], ps[im][0:F, 1, k * SEQ:(k + 1) * SEQ], ACT.Identity,
                                          scale=n1[:, k:k + 1])
                last.then_inc(e_feat[im], 1)

            def features(im, i, n, g=None):
                act.wait_ge(flipped[im], 3 * i + n)
                if g is None:
                    act.activation(hT[im][0:F, :, :].rearrange("p k n -> p (k n)"), ps[im][0:F, 1, 0:2 * SEQ],
                                   ACT.Copy).then_inc(feat[im], 1)
                else:
                    for k in range(2):
                        last = act.activation(hT[im][0:F, k, :], ps[im][0:F, 1, k * SEQ:(k + 1) * SEQ], ACT.Identity,
                                              scale=g[:, k:k + 1])
                    last.then_inc(feat[im], 1)

            def copy_band(im, i, p):
                bank = 2 * (p % 2)
                act.wait_ge(band_done[im], 4 * i + p + 1)
                if p % 2 == 0:
                    act.wait_ge(band_out[p // 2][im], 16 * i + 16)
                act.activation(band[im][:, 2 * p:2 * p + 2, :], ps[im][0:T, bank:bank + 2, 0:2 * BAND],
                               ACT.Copy).then_inc(band_copied[im], 1)

            def copy_q(im, i):
                act.wait_ge(q_proj[im], i + 1)
                act.activation(qz[im][0:64, 0:H0:2, :].rearrange("p (b m) n -> p b m n", b=2),
                               ps[im][0:64, 0:2, 0:2 * SEQ].rearrange("p b (m n) -> p b m n", m=2),
                               ACT.Copy).then_inc(q_copied[im], 1)

            def copy_k(im, i):
                act.wait_ge(k_proj[im], i + 1)
                act.activation(kT[im][:].rearrange("p (b m) n -> p b (m n)", b=2), ps[im][:, 2:4, 0:2 * SEQ],
                               ACT.Copy).then_inc(k_copied[im], 1)

            def exps(im, i, p):
                act.wait_ge(maxed[im], 4 * i + p + 1)
                for n in range(4):
                    part = s_sb[im][:, 2 * (p % 2) + n // 2, (n % 2) * SEQ:(n % 2 + 1) * SEQ]
                    last = act.activation(part, part, ACT.Exp, scale=DK0 ** -0.5, bias=nmx[im][:, p, n:n + 1])
                last.then_inc(exped[im], 1)

            def copy_p(im, i, p):
                bank = 2 * (p % 2) + 1
                act.wait_ge(p_flipped[im], 4 * i + p + 1)
                act.activation(pT[im][:, bank, :], ps[im][0:T, bank, 0:2 * SEQ], ACT.Copy).then_inc(p_copied[im], 1)

            def gelu(im, i):
                act.wait_ge(up_done[im], i + 1)
                act.activation(gT[im][:, 0:2, :].rearrange("p m n -> p (m n)"), ps[im][:, 2, 0:2 * SEQ], ACT.Gelu)
                act.activation(gT[im][:, 2, :], ps[im][:, 3, 0:SEQ], ACT.Gelu).then_inc(gelued[im], 1)

            def half(a, ia, b, ib, more):
                if more:
                    load_x(a, ia + 1)
                exps(b, ib, 0)
                copy_p(b, ib, 0)
                exps(b, ib, 1)
                features(a, ia, 2, n2)
                copy_p(b, ib, 1)
                exps(b, ib, 2)
                gelu(a, ia)
                if more:
                    features_e(a, ia + 1)
                copy_p(b, ib, 2)
                exps(b, ib, 3)
                copy_p(b, ib, 3)
                features(a, ia, 3)
                if more:
                    bands_q_k(a, ia + 1)
                features(b, ib, 1)

            def bands_q_k(im, i):
                for p in range(4):
                    copy_band(im, i, p)
                copy_q(im, i)
                copy_k(im, i)

            def head(im, i):
                load_x(im, i)
                features_e(im, i)
                bands_q_k(im, i)

            def attention(im, i):
                for p in range(4):
                    exps(im, i, p)
                    copy_p(im, i, p)

            head(0, 0)
            attention(0, 0)
            head(1, 0)
            features(0, 0, 1)
            with act.Fori(0, ROUNDS - 1) as i:
                half(0, i, 1, i, True)
                half(1, i, 0, i + 1, True)
            half(0, ROUNDS - 1, 1, ROUNDS - 1, False)
            features(1, ROUNDS - 1, 2, n2)
            gelu(1, ROUNDS - 1)
            features(1, ROUNDS - 1, 3)

        @block.tensor
        def _(pe):
            pe.wait_ge(weights_in, 16 * 17)
            pe.wait_ge(consts_set, 7)
            for k in range(2):
                for h in range(H0):
                    last = pe.matmul(ps[0][0:F, k, h * NPOS:(h + 1) * NPOS], wq_t[:, h, F * k:F * k + F],
                                     wpos[:, h, :], start=True, stop=True)
            last.then_inc(wqp_done, 1)
            for h in range(H0):
                last = pe.matmul(ps[0][0:1, 2, h * NPOS:(h + 1) * NPOS], vpar[:, h:h + 1],
                                 wpos[:, h, :], start=True, stop=True)
            last.then_inc(vw_done, 1)
            pe.wait_ge(wqp_copied, 3)
            pe.wait_ge(vw_placed, 16)
            for im in range(2):
                pe.sem_inc(h1_done[im], 1)
                pe.sem_inc(lg_done[im], 1)

            def flip(im, src, done):
                for k in range(2):
                    for c in range(2):
                        last = pe.transpose(ps[im][0:F, 1, k * SEQ + c * T:k * SEQ + (c + 1) * T],
                                            src[:, c, k * F:(k + 1) * F], ident[0:T, 0:T])
                last.then_inc(done[im], 1)

            def to_tokens(im, bank, src, w, n, done):
                for c in range(2):
                    for k in range(2):
                        last = pe.matmul(ps[im][0:T, bank, c * n:(c + 1) * n], src[im][:, k, c * T:(c + 1) * T],
                                         w[:, k, :], start=(k == 0), stop=(k == 1))
                last.then_inc(done[im], 1)

            def to_features(im, banks, src, w, done):
                for m in range(w.shape[2] // 128):
                    at = (m % 2) * SEQ
                    for k in range(2):
                        last = pe.matmul(ps[im][:, banks[m // 2], at:at + SEQ], w[:, k, m * 128:(m + 1) * 128],
                                         src[im][:, k, :], start=(k == 0), stop=(k == 1))
                last.then_inc(done[im], 1)

            def embed(im, i):
                pe.wait_ge(x_in[im], 16 * i + 16)
                for c in range(2):
                    out = ps[im][0:T, 0, c * D:(c + 1) * D]
                    for k in range(6):
                        pe.matmul(out, xin[im][:, k, c * T:(c + 1) * T], we[:, k, :], start=(k == 0), stop=False)
                    last = pe.matmul(out, ones_row[0:1, 0:T], be[0:1, :], start=False, stop=True)
                last.then_inc(embedded[im], 1)

            def flip_x(im, i):
                pe.wait_ge(e_normed[im], i + 1)
                flip(im, xe[im], e_flipped)

            def pos_queries(im, i):
                pe.wait_ge(e_feat[im], i + 1)
                to_features(im, (0,), eT, wqp, qw_proj)

            def bands(im, i, p):
                if p == 0:
                    pe.wait_ge(qw_copied[im], i + 1)
                elif p == 1:
                    pe.wait_ge(h1_done[im], i + 1)
                    pe.wait_ge(lg_done[im], i + 1)
                else:
                    pe.wait_ge(band_copied[im], 4 * i + p - 1)
                for n in range(2):
                    hh = 2 * (p % 2) + n
                    for c in range(2):
                        last = pe.matmul(ps[im][0:T, hh, c * BAND:(c + 1) * BAND],
                                         qwT[im][:, p // 2, c * T:(c + 1) * T], basis[:, hh, :], start=True, stop=True)
                last.then_inc(band_done[im], 1)

            def queries(im, i):
                pe.wait_ge(band_copied[im], 4 * i + 3)
                to_features(im, (0, 1), eT, wq, q_proj)

            def keys(im, i):
                pe.wait_ge(band_copied[im], 4 * i + 4)
                to_features(im, (2, 3), eT, wk, k_proj)

            def values_in(im, i):
                pe.wait_ge(q_copied[im], 2 * i + 2)
                to_tokens(im, 0, eT, wv, D, v_proj)

            def score(im, i, p):
                if p == 0:
                    pe.wait_ge(v_copied[im], i + 1)
                    pe.wait_ge(k_copied[im], i + 1)
                elif p > 1:
                    pe.wait_ge(o_done[im], 4 * i + p - 1)
                for n in range(2):
                    for c in range(2):
                        last = pe.matmul(ps[im][0:T, 2 * (p % 2) + n, c * SEQ:(c + 1) * SEQ],
                                         qz[im][:, 2 * p + n, c * T:(c + 1) * T], kT[im][:, p, :],
                                         start=True, stop=True)
                last.then_inc(scored[im], 1)

            def flip_p(im, i, p):
                pe.wait_ge(exped[im], 4 * i + p + 1)
                for n in range(2):
                    b = 2 * (p % 2) + n
                    for cj in range(2):
                        for ci in range(2):
                            last = pe.transpose(ps[im][0:T, b, cj * SEQ + ci * T:cj * SEQ + (ci + 1) * T],
                                                s_sb[im][:, b, ci * SEQ + cj * T:ci * SEQ + (cj + 1) * T],
                                                ident[0:T, 0:T])
                last.then_inc(p_flipped[im], 1)

            def values(im, i, p):
                pe.wait_ge(p_copied[im], 8 * i + 2 * p + 2)
                for ci in range(2):
                    for n in range(2):
                        b = 2 * (p % 2) + n
                        at = (2 * ci + n) * (DV0 + 1)
                        for cj in range(2):
                            last = pe.matmul(ps[im][0:T, 2 * (p % 2), at:at + DV0 + 1],
                                             pT[im][:, b, cj * SEQ + ci * T:cj * SEQ + (ci + 1) * T],
                                             vx[im][:, cj, 2 * p + n, :], start=(cj == 0), stop=(cj == 1))
                last.then_inc(pv_done[im], 1)

            def flip_o(im, i):
                pe.wait_ge(o_done[im], 4 * i + 4)
                flip(im, o_sb[im], flipped)

            def project(im, i):
                pe.wait_ge(feat[im], 3 * i + 1)
                to_tokens(im, 2, hT, wo, D, projected)

            def flip_x1(im, i):
                pe.wait_ge(normed[im], 2 * i + 1)
                flip(im, xr[im], flipped)

            def up(im, i):
                pe.wait_ge(feat[im], 3 * i + 2)
                to_features(im, (2, 3), hT, w1, up_done)

            def down(im, i):
                pe.wait_ge(gelued[im], i + 1)
                for c in range(2):
                    out = ps[im][0:T, 3, c * D:(c + 1) * D]
                    for m in range(3):
                        pe.matmul(out, gT[im][:, m, c * T:(c + 1) * T], w2[:, m, :], start=(m == 0), stop=False)
                    last = pe.matmul(out, ones_row[0:1, 0:T], b2[0:1, :], start=False, stop=True)
                last.then_inc(down_done[im], 1)

            def flip_f(im, i):
                pe.wait_ge(normed[im], 2 * i + 2)
                flip(im, xf[im], flipped)

            def switch(im, i):
                pe.wait_ge(feat[im], 3 * i + 3)
                to_tokens(im, 2, hT, ws, E, logits)

            def half(a, ia, b, ib, more):
                score(b, ib, 0)
                score(b, ib, 1)
                if more:
                    embed(a, ia + 1)
                flip_p(b, ib, 0)
                values(b, ib, 0)
                flip_x1(a, ia)
                flip_p(b, ib, 1)
                score(b, ib, 2)
                up(a, ia)
                values(b, ib, 1)
                if more:
                    flip_x(a, ia + 1)
                score(b, ib, 3)
                flip_p(b, ib, 2)
                if more:
                    pos_queries(a, ia + 1)
                down(a, ia)
                values(b, ib, 2)
                flip_p(b, ib, 3)
                values(b, ib, 3)
                flip_f(a, ia)
                switch(a, ia)
                if more:
                    bands_q_k(a, ia + 1)
                flip_o(b, ib)
                if more:
                    values_in(a, ia + 1)
                project(b, ib)

            def bands_q_k(im, i):
                for p in range(4):
                    bands(im, i, p)
                queries(im, i)
                keys(im, i)

            def head(im, i):
                embed(im, i)
                flip_x(im, i)
                pos_queries(im, i)
                bands_q_k(im, i)
                values_in(im, i)

            def attention(im, i):
                for p in range(4):
                    score(im, i, p)
                    flip_p(im, i, p)
                    values(im, i, p)

            head(0, 0)
            attention(0, 0)
            head(1, 0)
            flip_o(0, 0)
            project(0, 0)
            with pe.Fori(0, ROUNDS - 1) as i:
                half(0, i, 1, i, True)
                half(1, i, 0, i + 1, True)
            half(0, ROUNDS - 1, 1, ROUNDS - 1, False)
            flip_x1(1, ROUNDS - 1)
            up(1, ROUNDS - 1)
            down(1, ROUNDS - 1)
            flip_f(1, ROUNDS - 1)
            switch(1, ROUNDS - 1)

        @block.vector
        def _(dve):
            dve.memset(ones_row[:], 1.0).then_inc(consts_set, 1)
            for im in range(2):
                dve.memset(hT[im][F:FB, :, :], 1.0)
                dve.memset(eT[im][F:FB, :, :], 1.0).then_inc(consts_set, 1)
                dve.memset(vx[im][:, :, :, DV0:DV0 + 1], 1.0).then_inc(consts_set, 1)
                dve.memset(qz[im][:], 0.0)
            dve.memset(wqp[F:FB, 0, :], 0.0)
            dve.wait_ge(wqp_done, 1)
            for k in range(2):
                dve.tensor_copy(wqp[0:F, k, :], ps[0][0:F, k, 0:H0 * NPOS]).then_inc(wqp_copied, 1)
            dve.wait_ge(vw_done, 1)
            dve.tensor_copy(vw[0:1, :], ps[0][0:1, 2, 0:H0 * NPOS]).then_inc(wqp_copied, 1)
            for im in range(2):
                dve.sem_inc(out_sent[im], 48)
            head_link = [Link(dve, head_links[im], 3) for im in range(2)]
            att_link = [Link(dve, att_links[im], 8) for im in range(2)]
            x1_link = [Link(dve, x1_links[im], 4) for im in range(2)]
            tail_link = [Link(dve, tail_links[im], 2) for im in range(2)]

            def flat(tile):
                return tile[:].rearrange("p c f -> p (c f)")

            def mean_var(st, mv, link, rows):
                dve.bn_stats(st[:, 0, :], rows[:, 0, :])
                link(dve.bn_stats(st[:, 1, :], rows[:, 1, :]))
                dve.sem_inc(fence, 1)
                dve.bn_aggr(mv[:, 0, :], st[:, 0, :])
                link(dve.bn_aggr(mv[:, 1, :], st[:, 1, :]))
                return mv[:, :, 0], mv[:, :, 1]

            def embedding(im, i):
                link = head_link[im]
                link.round(i)
                dve.wait_ge(embedded[im], i + 2)
                rows = ps[im][0:T, 0, 0:2 * D]
                _, var = mean_var(st_e[im], mv_e[im], link, rows.rearrange("p (c f) -> p c f", c=2))
                dve.tensor_scalar(vv_e[im][:, 0, :], var, EPS, None, ALU.add)
                dve.tensor_scalar(vv_e[im][:, 1, :], var, 1 + EPS, EPS * EPS, ALU.mult, ALU.add
                                  ).then_inc(e_stats[im], 1)
                link(dve.tensor_copy(flat(h0[im]), rows))

            def normalise_e(im, i):
                dve.wait_ge(e_rstd[im], i + 1)
                for kind, out in ((1, xe), (0, xn)):
                    for c in range(2):
                        last = dve.tensor_scalar(out[im][:, c, :], h0[im][:, c, :], mv_e[im][:, c, 0:1],
                                                 rr_e[im][:, kind, c:c + 1], ALU.subtract, ALU.mult)
                    if kind == 1:
                        last.then_inc(e_normed[im], 1)

            def copy_pos_queries(im, i):
                dve.wait_ge(qw_proj[im], i + 1)
                dve.tensor_copy(qwT[im][:].rearrange("p m n -> p (m n)"), ps[im][:, 0, 0:2 * SEQ]
                                ).then_inc(qw_copied[im], 1)

            def copy_q_v(im, i):
                dve.wait_ge(q_proj[im], i + 1)
                dve.tensor_copy(qz[im][64:128, 1:H0:2, :].rearrange("p (b m) n -> p b m n", b=2),
                                ps[im][64:128, 0:2, 0:2 * SEQ].rearrange("p b (m n) -> p b m n", m=2)
                                ).then_inc(q_copied[im], 1)
                dve.wait_ge(v_proj[im], i + 1)
                dve.tensor_copy(vx[im][:, :, :, 0:DV0],
                                ps[im][0:T, 0, 0:2 * D].rearrange("p (c h d) -> p c h d", c=2, d=DV0)
                                ).then_inc(v_copied[im], 1)

            def add_max(im, i, p):
                at = slice(2 * (p % 2), 2 * (p % 2) + 2)
                link = att_link[im]
                if p == 0:
                    link.round(i)
                dve.wait_ge(scored[im], 4 * i + p + 1)
                if p % 2 == 0:
                    dve.wait_ge(pos_in[p // 2][im], 16 * i + 16)
                dve.tensor_tensor(s_sb[im][:, at, :], ps[im][0:T, at, 0:2 * SEQ], pos[im][:, 2 * p:2 * p + 2, :],
                                  ALU.add).then_inc(added[im], 1)
                dve.wait_ge(added[im], 4 * i + p + 5)
                link(dve.tensor_reduce(mx[im][:, p, :], s_sb[im][:, at, :].rearrange("p h (c j) -> p (h c) j", c=2),
                                       AX.X, ALU.max))
                dve.tensor_scalar(nmx[im][:, p, :], mx[im][:, p, :], -(DK0 ** -0.5), None, ALU.mult
                                  ).then_inc(maxed[im], 1)

            def copy_p(im, i, p):
                bank = 2 * (p % 2)
                dve.wait_ge(p_flipped[im], 4 * i + p + 1)
                dve.tensor_copy(pT[im][:, bank, :], ps[im][0:T, bank, 0:2 * SEQ]).then_inc(p_copied[im], 1)

            def divide(im, i, p):
                dve.wait_ge(pv_done[im], 4 * i + p + 1)
                o_ps = ps[im][0:T, 2 * (p % 2), 0:4 * (DV0 + 1)].rearrange("p (c h d) -> p c h d", c=2, d=DV0 + 1)
                att_link[im](dve.reciprocal(rs[im][:], o_ps[:, :, :, DV0]))
                at = slice(2 * p * DV0, 2 * (p + 1) * DV0)
                dve.tensor_tensor(o_sb[im][:, :, at].rearrange("p c (h d) -> p c h d", d=DV0),
                                  o_ps[:, :, :, 0:DV0], spread(rs[im][:], 3, DV0), ALU.mult).then_inc(o_done[im], 1)

            def attended(im, i):
                link = x1_link[im]
                link.round(i)
                dve.wait_ge(projected[im], i + 1)
                link(dve.tensor_tensor(flat(x1[im]), ps[im][0:T, 2, 0:2 * D], flat(xn[im]), ALU.add))
                mean, var = mean_var(st[im], mv[im], link, x1[im])
                link(dve.tensor_tensor(sq[im][:], mean, mean, ALU.mult))
                dve.scalar_tensor_tensor(vv[im][:], sq[im][:], EPS, var, ALU.add, ALU.add).then_inc(stats[im], 1)

            def normalise_x1(im, i):
                dve.wait_ge(rstd[im], 2 * i + 1)
                for c in range(2):
                    last = dve.tensor_scalar(xr[im][:, c, :], x1[im][:, c, :], rr[im][:, c:c + 1], None, ALU.mult)
                last.then_inc(normed[im], 1)
                dve.tensor_tensor(skip[im][:], x1[im][:], h0[im][:], ALU.add).then_inc(x1_done[im], 1)

            def ffn_done(im, i):
                tail_link[im].round(i)
                dve.wait_ge(down_done[im], i + 1)
                dve.wait_ge(x1_done[im], i + 1)
                dve.wait_ge(out_sent[im], 48 * i + 48)
                dve.tensor_tensor(flat(h1[im]), ps[im][0:T, 3, 0:2 * D], flat(skip[im]), ALU.add).then_inc(h1_done[im], 1)
                dve.wait_ge(h1_done[im], i + 2)
                _, var = mean_var(st[im], mv[im], tail_link[im], h1[im])
                dve.tensor_scalar(vv[im][:], var, EPS, None, ALU.add).then_inc(stats[im], 1)

            def normalise_f(im, i):
                dve.wait_ge(rstd[im], 2 * i + 2)
                for c in range(2):
                    last = dve.tensor_scalar(xf[im][:, c, :], h1[im][:, c, :], mv[im][:, c, 0:1],
                                             rr[im][:, c:c + 1], ALU.subtract, ALU.mult)
                last.then_inc(normed[im], 1)

            def copy_logits(im, i):
                dve.wait_ge(logits[im], i + 1)
                dve.tensor_copy(flat(lg[im]), ps[im][0:T, 2, 0:2 * E]).then_inc(lg_done[im], 1)

            def half(a, ia, b, ib, more):
                add_max(b, ib, 0)
                normalise_x1(a, ia)
                add_max(b, ib, 1)
                copy_p(b, ib, 0)
                if more:
                    embedding(a, ia + 1)
                divide(b, ib, 0)
                copy_p(b, ib, 1)
                if more:
                    normalise_e(a, ia + 1)
                add_max(b, ib, 2)
                divide(b, ib, 1)
                add_max(b, ib, 3)
                copy_p(b, ib, 2)
                if more:
                    copy_pos_queries(a, ia + 1)
                ffn_done(a, ia)
                divide(b, ib, 2)
                copy_p(b, ib, 3)
                normalise_f(a, ia)
                divide(b, ib, 3)
                copy_logits(a, ia)
                if more:
                    copy_q_v(a, ia + 1)
                attended(b, ib)

            def head(im, i):
                embedding(im, i)
                normalise_e(im, i)
                copy_pos_queries(im, i)
                copy_q_v(im, i)

            def attention(im, i):
                for p in range(4):
                    add_max(im, i, p)
                    copy_p(im, i, p)
                    divide(im, i, p)

            head(0, 0)
            attention(0, 0)
            head(1, 0)
            attended(0, 0)
            with dve.Fori(0, ROUNDS - 1) as i:
                half(0, i, 1, i, True)
                half(1, i, 0, i + 1, True)
            half(0, ROUNDS - 1, 1, ROUNDS - 1, False)
            normalise_x1(1, ROUNDS - 1)
            ffn_done(1, ROUNDS - 1)
            normalise_f(1, ROUNDS - 1)
            copy_logits(1, ROUNDS - 1)


def stage_b(nc, dr, scattered):
    W = E * COLS
    with ExitStack() as ctx:
        sb, sb2, sem, sem2 = allocators(nc, ctx)
        lg = sb("b_lg", [T, COLS, E])
        ex = sb("b_ex", [T, COLS, E])
        top = sb("b_top", [T, COLS])
        gain = sb("b_gain", [T, COLS])
        total = sb("b_total", [T, COLS])
        order = sb("b_order", [T, E])
        offset = sb("b_offset", [T, E])
        spare = sb("b_spare", [T, COLS])
        before = sb("b_before", [T, T])
        ones = sb("b_ones", [T, T])
        flat1 = sb("b_flat1", [T, W])
        mine = sb("b_mine", [T, E, COLS])
        own = sb("b_own", [T, E, COLS])
        hit = sb("b_hit", [T, E, COLS])
        above = sb("b_above", [T, E, COLS])
        tie = sb("b_tie", [T, E, COLS])
        keep = sb("b_keep", [T, E, COLS])
        sums = sb("b_sums", [T, E, COLS])
        rank = sb("b_rank", [T, E, COLS])
        base = sb("b_base", [T, E])
        cnt = sb("b_cnt", [T, E])
        need = sb("b_need", [T, E])
        bit_f = sb("b_bit_f", [T, E])
        bit_i = sb("b_bit_i", [T, E], INT32)
        cand = sb("b_cand", [T, E], INT32)
        won = sb("b_won", [T, E], INT32)
        bound = sb("b_bound", [T, E], INT32)
        kept = sb("b_kept", [T, COLS])
        slot_f = sb("b_slot_f", [T, COLS])
        slot = sb("b_slot", [T, COLS], INT32)
        xrow = [sb(f"b_xrow{n}", [T, 2, D]) for n in range(4)]
        idx = [sb(f"b_idx{n}", [T, 2], INT32) for n in range(4)]
        ps = ctx.enter_context(nc.psum_tensor("b_ps", [128, 8, 512], FP32))
        ps_pre = ps[0:T, 0:2, :].rearrange("p b n -> p (b n)")
        ps_tot = ps[0:T, 2:4, :].rearrange("p b n -> p (b n)")
        ps_cnt = ps[0:T, 4, 0:E]
        ps_above = ps[0:T, 5, 0:E]

        loaded = sem("b_loaded")
        shifted = sem("b_shifted")
        exped = sem("b_exped")
        v_link = sem("b_v_link")
        s_link = sem("b_s_link")
        counted = sem("b_counted")
        summed = sem("b_summed")
        above_counted = sem("b_above_counted")
        above_summed = sem("b_above_summed")
        marked = sem("b_marked")
        prefixed = sem("b_prefixed")
        slots_done = sem("b_slots_done")
        tables_out = sem("b_tables_out")
        fence = sem("b_fence")
        x_in = [sem(f"b_x_in{n}") for n in range(4)]
        idx_done = [sem(f"b_idx_done{n}") for n in range(4)]
        row_free = [sem(f"b_row_free{n}") for n in range(4)]
        BITS = 30

        block = ctx.enter_context(nc.Block())

        @block.sync
        def _(sp):
            load_all(sp, [(lg[:].rearrange("p (i c) e -> p i (c e)", c=2), dr["lg"].rearrange("i p f -> p i f")),
                          (order[:], dr["order"]), (offset[:], dr["offset"]), (spare[:], dr["spare"]),
                          (before[:], dr["before"]), (ones[:], dr["ones"])], loaded)
            sp.wait_ge(slots_done, 1)
            sp.dma_start(dr["slot"], slot[:]).then_inc(tables_out, 16)
            sp.dma_start(dr["gain"], gain[:]).then_inc(tables_out, 16)
            with sp.Fori(0, IMAGES // 4) as i:
                for n in range(4):
                    sp.wait_ge(row_free[n], i + 1)
                    sp.dma_start(xrow[n][:].rearrange("p c f -> p (c f)"),
                                 dr["xf"][bass.ds(4 * i + n, 1)].rearrange("a p f -> (a p) f")).then_inc(x_in[n], 16)
            sp.wait_ge(tables_out, 32)

        @block.gpsimd
        def _(pool):
            pool.wait_ge(slots_done, 1)
            for n in range(4):
                pool.sem_inc(row_free[n], 1)
            with pool.Fori(0, IMAGES // 4) as i:
                for n in range(4):
                    pool.tensor_copy(idx[n][:], slot[:, bass.ds(8 * i + 2 * n, 2)]).then_inc(idx_done[n], 1)
                for n in range(4):
                    pool.wait_ge(x_in[n], 16 * i + 16)
                    pool.wait_ge(idx_done[n], i + 1)
                    pool.sem_inc(fence, 1)
                    for c in range(2):
                        pool.indirect_dma_start(out=dr["rows"], out_offset=bass.IndirectOffsetOnAxis(
                            ap=idx[n][:, c:c + 1], axis=0), in_=xrow[n][:, c, :], in_offset=None
                            ).then_inc(scattered[n], 16)
                for n in range(4):
                    pool.wait_ge(scattered[n], 32 * i + 32)
                    pool.sem_inc(row_free[n], 1)

        @block.scalar
        def _(act):
            act.wait_ge(shifted, 1)
            act.activation(ex[:], ex[:], ACT.Exp).then_inc(exped, 1)

        @block.tensor
        def _(pe):
            pe.wait_ge(loaded, 16 * 6)
            with pe.Fori(0, BITS) as i:
                pe.wait_ge(counted, i + 1)
                pe.matmul(ps_cnt, ones[:], cnt[:], start=True, stop=True).then_inc(summed, 1)
            pe.wait_ge(above_counted, 1)
            pe.matmul(ps_above, ones[:], cnt[:], start=True, stop=True).then_inc(above_summed, 1)
            for n, marks in enumerate((tie, keep)):
                flat = marks[:].rearrange("p e c -> p (e c)")
                pe.wait_ge(marked, n + 1)
                for b in range(2):
                    at = slice(512 * b, 512 * b + 512)
                    pe.matmul(ps_pre[:, at], before[:], flat[:, at], start=True, stop=True)
                    last = pe.matmul(ps_tot[:, at], ones[:], flat[:, at], start=True, stop=True)
                last.then_inc(prefixed, 1)

        @block.vector
        def _(dve):
            link = Link(dve, v_link, 0)
            link.per = None

            def vlink(ins):
                link.n += 1
                ins.then_inc(v_link, 1)
                dve.wait_ge(v_link, link.n)

            def cols(ap):
                return ap.rearrange("p e c -> p c e")

            dve.memset(flat1[:], 1.0)
            dve.memset(bound[:], 0)
            dve.memset(bit_f[:], float(2 ** (BITS - 1)))
            dve.wait_ge(loaded, 16 * 6)
            vlink(dve.tensor_reduce(top[:], lg[:], AX.X, ALU.max))
            dve.tensor_tensor(ex[:], lg[:], spread(top[:], 2, E), ALU.subtract).then_inc(shifted, 1)
            dve.wait_ge(exped, 1)
            dve.tensor_reduce(total[:], ex[:], AX.X, ALU.add)
            vlink(dve.tensor_reduce(top[:], ex[:], AX.X, ALU.max))
            dve.reciprocal(gain[:], total[:])
            vlink(dve.tensor_tensor(cols(mine[:]), ex[:], spread(top[:], 2, E), ALU.is_equal))
            vlink(dve.tensor_tensor(cols(hit[:]), cols(mine[:]), spread(order[:], 1, COLS), ALU.mult))
            vlink(dve.tensor_reduce(top[:], cols(hit[:]), AX.X, ALU.max))
            vlink(dve.tensor_tensor(mine[:], hit[:], spread(top[:], 1, E), ALU.is_equal))
            vlink(dve.tensor_tensor(own[:], mine[:], spread(gain[:], 1, E), ALU.mult))
            step = Link(dve, s_link, 6)
            with dve.Fori(0, BITS) as i:
                step.round(i)
                step(dve.tensor_copy(bit_i[:], bit_f[:]))
                step(dve.tensor_tensor(cand[:], bound[:], bit_i[:], ALU.bitwise_or))
                step(dve.tensor_tensor(hit[:], own[:], spread(cand[:].bitcast(FP32), 2, COLS), ALU.is_ge))
                dve.tensor_reduce(cnt[:], hit[:], AX.X, ALU.add).then_inc(counted, 1)
                dve.wait_ge(summed, i + 1)
                step(dve.scalar_tensor_tensor(won[:], ps_cnt, float(CAPACITY), bit_f[:], ALU.is_ge, ALU.mult))
                step(dve.tensor_tensor(bound[:], bound[:], won[:], ALU.bitwise_or))
                step(dve.tensor_scalar(bit_f[:], bit_f[:], 0.5, None, ALU.mult))
                step.end()
            level = spread(bound[:].bitcast(FP32), 2, COLS)
            dve.tensor_tensor(above[:], own[:], level, ALU.is_gt)
            vlink(dve.tensor_tensor(hit[:], own[:], level, ALU.is_equal))
            dve.tensor_reduce(cnt[:], above[:], AX.X, ALU.add).then_inc(above_counted, 1)
            dve.tensor_tensor(tie[:], hit[:], mine[:], ALU.mult).then_inc(marked, 1)
            dve.wait_ge(above_summed, 1)
            vlink(dve.tensor_scalar(need[:], ps_above, -1.0, float(CAPACITY), ALU.mult, ALU.add))

            def prefix(n):
                dve.wait_ge(prefixed, n)
                flat = sums[:].rearrange("p e c -> p (e c)")
                out = rank[:].rearrange("p e c -> p (e c)")
                vlink(dve.tensor_tensor_scan(flat, flat1[:], ps_tot, 0.0, ALU.mult, ALU.add))
                vlink(dve.tensor_tensor(flat, flat, ps_tot, ALU.subtract))
                dve.tensor_copy(base[:], sums[:, :, 0])
                vlink(dve.tensor_tensor(out, flat, ps_pre, ALU.add))
                vlink(dve.tensor_tensor(rank[:], rank[:], spread(base[:], 2, COLS), ALU.subtract))

            prefix(1)
            vlink(dve.tensor_tensor(hit[:], rank[:], spread(need[:], 2, COLS), ALU.is_lt))
            vlink(dve.tensor_tensor(hit[:], hit[:], tie[:], ALU.mult))
            dve.tensor_tensor(keep[:], hit[:], above[:], ALU.add).then_inc(marked, 1)
            prefix(2)
            vlink(dve.tensor_tensor(rank[:], rank[:], spread(offset[:], 2, COLS), ALU.add))
            dve.tensor_reduce(kept[:], cols(keep[:]), AX.X, ALU.add)
            vlink(dve.tensor_tensor(hit[:], rank[:], keep[:], ALU.mult))
            vlink(dve.tensor_reduce(slot_f[:], cols(hit[:]), AX.X, ALU.add))
            vlink(dve.tensor_tensor(total[:], kept[:], spare[:], ALU.mult))
            vlink(dve.tensor_tensor(slot_f[:], slot_f[:], total[:], ALU.subtract))
            dve.tensor_tensor(slot[:], slot_f[:], spare[:], ALU.add).then_inc(slots_done, 1)


def stage_c(nc, dr, y_out):
    PER = SLOTS // BATCH
    SUB = BATCH // 128
    M = HID // 128
    with ExitStack() as ctx:
        sb, sb2, sem, sem2 = allocators(nc, ctx)
        ident = sb("c_ident", [128, 128])
        ones_row = sb("c_ones_row", [1, 128])
        w1 = sb2("c_w1", [FB, 2, HID])
        w2 = sb2("c_w2", [128, M, D])
        b2 = sb2("c_b2", [1, D])
        xs = sb2("c_xs", [128, SUB, D])
        xT = sb2("c_xT", [FB, 2, BATCH])
        gT = sb2("c_gT", [128, M, BATCH])
        yo = sb2("c_yo", [128, SUB, D])
        ps = ctx.enter_context(nc.psum_tensor("c_ps", [128, 8, 512], FP32))
        UP, DOWN, UPS = 2, 6, 4

        loaded = sem("c_loaded")
        ones_set = sem("c_ones_set")
        w_in = sem2("c_w_in")
        w_free = sem2("c_w_free")
        x_in = sem2("c_x_in")
        flipped = sem2("c_flipped")
        xT_done = sem2("c_xT_done")
        up_done = sem("c_up_done")
        gelued = sem("c_gelued")
        down_done = sem("c_down_done")
        y_done = sem("c_y_done")
        yo_free = sem2("c_yo_free")

        view = dr["rows"][0:E * SLOTS, :].rearrange("(n p s) f -> n p (s f)", p=128, s=SUB)
        batches = [(e2, b) for e2 in range(2) for b in range(PER)]
        NB = len(batches)
        block = ctx.enter_context(nc.Block())

        @block.sync
        def _(sp):
            sp.dma_start(ident[:], dr["ident"]).then_inc(loaded, 16)
            for e2 in range(2):
                sp.sem_inc(w_free[e2], 1)
                sp.sem_inc(flipped[e2], 1)
            with sp.Fori(0, E // 2) as i:
                for n, (e2, b) in enumerate(batches):
                    if b == 0:
                        e = 2 * i + e2
                        sp.wait_ge(w_free[e2], i + 1)
                        sp.dma_start(w1[e2][:], dr["we1"][bass.ds(e, 1)].rearrange("a p k m -> (a p) k m")).then_inc(w_in[e2], 16)
                        sp.dma_start(w2[e2][:], dr["we2"][bass.ds(e, 1)].rearrange("a p k m -> (a p) k m")).then_inc(w_in[e2], 16)
                        sp.dma_start(b2[e2][:], dr["be2"][bass.ds(e, 1)]).then_inc(w_in[e2], 16)
                    sp.wait_ge(flipped[n % 2], i * (NB // 2) + n // 2 + 1)
                    sp.dma_start(xs[n % 2][:].rearrange("p s f -> p (s f)"),
                                 view[bass.ds(NB * i + n, 1)].rearrange("a p f -> (a p) f")).then_inc(x_in[n % 2], 16)

        @block.gpsimd
        def _(pool):
            pool.sem_inc(yo_free[0], 1)
            pool.sem_inc(yo_free[1], 1)
            with pool.Fori(0, E // 2) as i:
                for n in range(NB):
                    pool.wait_ge(y_done, i * NB + n + 2)
                    pool.dma_start(view[bass.ds(NB * i + n, 1)].rearrange("a p f -> (a p) f"),
                                   yo[n % 2][:].rearrange("p s f -> p (s f)")).then_inc(y_out[n % 2], 16)
                    pool.wait_ge(y_out[n % 2], 16 * (i * (NB // 2) + n // 2 + 1))
                    pool.sem_inc(yo_free[n % 2], 1)

        @block.scalar
        def _(act):
            with act.Fori(0, E // 2) as i:
                for n in range(NB):
                    for m in range(M):
                        at = n * M + m
                        act.wait_ge(up_done, i * NB * M + at + 1)
                        act.activation(gT[n % 2][:, m, :], ps[:, UP + at % UPS, :], ACT.Gelu).then_inc(gelued, 1)

        @block.tensor
        def _(pe):
            pe.wait_ge(loaded, 16)
            pe.wait_ge(ones_set, 3)
            pe.sem_inc(gelued, UPS)
            pe.sem_inc(y_done, 1)

            def flip(i, n):
                pe.wait_ge(x_in[n % 2], 16 * (i * (NB // 2) + n // 2 + 1))
                for k in range(2):
                    for s in range(SUB):
                        last = pe.transpose(ps[0:F, k, s * 128:(s + 1) * 128], xs[n % 2][:, s, k * F:(k + 1) * F], ident[:])
                last.then_inc(flipped[n % 2], 1)

            with pe.Fori(0, E // 2) as i:
                for n, (e2, b) in enumerate(batches):
                    if n == 0:
                        flip(i, 0)
                    if b == 0:
                        pe.wait_ge(w_in[e2], 48 * i + 48)
                    pe.wait_ge(xT_done[n % 2], i * (NB // 2) + n // 2 + 1)
                    for m in range(M):
                        at = n * M + m
                        pe.wait_ge(gelued, i * NB * M + at + 1)
                        for k in range(2):
                            last = pe.matmul(ps[:, UP + at % UPS, :], w1[e2][:, k, m * 128:(m + 1) * 128],
                                             xT[n % 2][:, k, :], start=(k == 0), stop=(k == 1))
                        last.then_inc(up_done, 1)
                    if n + 1 < NB:
                        flip(i, n + 1)
                    pe.wait_ge(gelued, i * NB * M + (n + 1) * M + UPS)
                    pe.wait_ge(y_done, i * NB + n + 1)
                    for s in range(SUB):
                        out = ps[:, DOWN + s // 2, (s % 2) * D:(s % 2 + 1) * D]
                        for m in range(M):
                            pe.matmul(out, gT[n % 2][:, m, s * 128:(s + 1) * 128], w2[e2][:, m, :],
                                      start=(m == 0), stop=False)
                        last = pe.matmul(out, ones_row[0:1, :], b2[e2][0:1, :], start=False, stop=True)
                    last.then_inc(down_done, 1)
                    if b == PER - 1:
                        pe.sem_inc(w_free[e2], 1)

        @block.vector
        def _(dve):
            dve.memset(ones_row[:], 1.0).then_inc(ones_set, 1)
            for q in range(2):
                dve.memset(xT[q][F:FB, :, :], 1.0).then_inc(ones_set, 1)

            def features(i, n):
                dve.wait_ge(flipped[n % 2], i * (NB // 2) + n // 2 + 2)
                dve.tensor_copy(xT[n % 2][0:F, :, :], ps[0:F, 0:2, :]).then_inc(xT_done[n % 2], 1)

            with dve.Fori(0, E // 2) as i:
                for n in range(NB):
                    if n == 0:
                        features(i, 0)
                    if n + 1 < NB:
                        features(i, n + 1)
                    dve.wait_ge(down_done, i * NB + n + 1)
                    dve.wait_ge(yo_free[n % 2], i * (NB // 2) + n // 2 + 1)
                    dve.tensor_copy(yo[n % 2][:].rearrange("p (b s) f -> p b (s f)", b=2), ps[:, DOWN:DOWN + 2, 0:2 * D]
                                    ).then_inc(y_done, 1)


def stage_d(nc, dr, gathered):
    KR = K_ROUTED
    G4 = 3 * KR
    CW = 3 * T
    PAIRS = H1N // 2
    with ExitStack() as ctx:
        sb, sb2, sem, sem2 = allocators(nc, ctx)
        ident = sb("d_ident", [128, 128])
        ones_row = sb("d_ones_row", [1, 128])
        half_neg = sb("d_half_neg", [T, 4])
        rope = sb("d_rope", [F, 2, SEQ])
        causal = sb("d_causal", [T, CW])
        earlier = sb("d_earlier", [T, 2, SEQ])
        places = sb("d_places", [T, KR])
        blocks = sb("d_blocks", [F, 2, 6, KR])
        wq = sb("d_wq", [FB, 2, 2, D])
        wk = sb("d_wk", [FB, 2, 2, D])
        wv = sb("d_wv", [FB, 2, D])
        wp = sb("d_wp", [FB, 2, D])
        wr = sb("d_wr", [FB, 2, 1])
        uq = sb("d_uq", [FB, 2, D])
        uk = sb("d_uk", [FB, 2, D])
        uv = sb("d_uv", [FB, 2, D])
        uo = sb("d_uo", [FB, 2, D])
        um = sb("d_um", [FB, 2, D])
        w1 = sb("d_w1", [FB, 2, HID])
        w2 = sb("d_w2", [128, 6, D])
        b2 = sb("d_b2", [1, D])
        g1 = sb("d_g1", [F, 2])
        c1 = sb("d_c1", [F, 2])
        g2 = sb("d_g2", [F, 2])
        c2 = sb("d_c2", [F, 2])

        h1 = sb2("d_h1", [T, 2, D])
        yx = sb2("d_yx", [T, 2, D])
        idx = sb2("d_idx", [T, 2], INT32)
        gain = sb2("d_gain", [T, 2])
        h2 = sb2("d_h2", [T, 2, D])
        st_e = sb2("d_st_e", [T, 2, 6])
        mv_e = sb2("d_mv_e", [T, 2, 2])
        vv_e = sb2("d_vv_e", [T, 2])
        rr_e = sb2("d_rr_e", [T, 2])
        xe = sb2("d_xe", [T, 2, D])
        eT = sb2("d_eT", [FB, 2, SEQ])
        st = sb2("d_st", [T, 2, 6])
        mv = sb2("d_mv", [T, 2, 2])
        vv = sb2("d_vv", [T, 2, 2])
        rr = sb2("d_rr", [T, 2, 2])
        xr = sb2("d_xr", [T, 2, D])
        xh = sb2("d_xh", [T, 2, D])
        skip = sb2("d_skip", [T, 2, D])
        aT = sb2("d_aT", [FB, 2, SEQ])
        rot = sb2("d_rot", [F, 2, 2, SEQ])
        qT = sb2("d_qT", [F, 2, SEQ])
        qz = sb2("d_qz", [F, 2, 6, SEQ])
        kT = sb2("d_kT", [F, 2, SEQ])
        vx = sb2("d_vx", [T, 2, H1N, DH + 1])
        s_sb = sb2("d_s", [T, 4, CW])
        mx = sb2("d_mx", [T, PAIRS, 2, 2])
        nmx = sb2("d_nmx", [T, PAIRS, 2, 2])
        pT = sb2("d_pT", [T, 4, CW])
        rs = sb2("d_rs", [T, 2, 2])
        o_sb = sb2("d_o", [T, 2, D])
        h3 = sb2("d_h3", [T, 2, D])
        hid = sb2("d_hid", [T, 2, D])
        nT = sb2("d_nT", [FB, 2, SEQ])
        kT2 = sb2("d_kT2", [F, 2, SEQ])
        v2 = sb2("d_v2", [T, 2, D])
        sg = sb2("d_sg", [T, 2])
        chance = sb2("d_chance", [T, 2])
        wide = sb2("d_wide", [T, 2, T])
        srow = sb2("d_srow", [T, SEQ])
        junk = sb2("d_junk", [T, 2, SEQ])
        junk2 = sb2("d_junk2", [T, 2, SEQ])
        less = sb2("d_less", [T, 2])
        ties = sb2("d_ties", [T, 2])
        rank = sb2("d_rank", [T, 2])
        away = sb2("d_away", [T, 2])
        sel = sb2("d_sel", [T, 2, KR])
        selT = sb2("d_selT", [KR, SEQ])
        ssum = sb2("d_ssum", [T, 1])
        pool_r = sb2("d_pool_r", [F, 2])
        pool_t = sb2("d_pool_t", [F, 2])
        mT = sb2("d_mT", [FB, 2, SEQ])
        xq = sb2("d_xq", [FB, 2, KR])
        qb = sb2("d_qb", [F, 2, 6, KR])
        mx2 = sb2("d_mx2", [G4, 4])
        nmx2 = sb2("d_nmx2", [G4, 4])
        p2 = sb2("d_p2", [G4, 4, SEQ])
        sum2 = sb2("d_sum2", [G4, 4])
        rs2 = sb2("d_rs2", [G4, 4])
        pT2 = sb2("d_pT2", [T, 4, 2, G4])
        cb = sb2("d_cb", [F, 2, 6, KR])
        cT = sb2("d_cT", [FB, 2, KR])
        ao = sb2("d_ao", [KR, D])
        hm = sb2("d_hm", [T, 2, D])
        gT = sb2("d_gT", [128, 6, SEQ])
        y = sb2("d_y", [T, 2, D])
        ps = [ctx.enter_context(nc.psum_tensor(f"d_ps{im}", [128, 4, 512], FP32)) for im in range(2)]

        weights = [(ident, "ident"), (rope, "rope"), (causal, "causal"), (earlier, "earlier"), (places, "places"),
                   (blocks, "blocks"), (wq, "dq"), (wk, "dk"), (wv, "dv"), (wp, "dp"), (wr, "wr"), (uq, "uq"),
                   (uk, "uk"), (uv, "uv"), (uo, "uo"), (um, "um"), (w1, "u1"), (w2, "u2"), (b2, "ub2"),
                   (g1, "g1"), (c1, "c1"), (g2, "g2"), (c2, "c2")]
        W_IN = 16 * len(weights)
        CONSTS = 12
        weights_in = sem("d_weights_in")
        consts_set = sem("d_consts_set")
        fence = sem("d_fence")
        rows_in = sem2("d_rows_in")
        head_links = sem2("d_head_links")
        att_links = sem2("d_att_links")
        h3_links = sem2("d_h3_links")
        tail_links = sem2("d_tail_links")
        h2_done = sem2("d_h2_done")
        e_stats = sem2("d_e_stats")
        e_rstd = sem2("d_e_rstd")
        e_normed = sem2("d_e_normed")
        e_flipped = sem2("d_e_flipped")
        e_feat = sem2("d_e_feat")
        stats = sem2("d_stats")
        rstd = sem2("d_rstd")
        normed = sem2("d_normed")
        flipped = sem2("d_flipped")
        feat = sem2("d_feat")
        q_proj = sem2("d_q_proj")
        v_proj = sem2("d_v_proj")
        k_proj = sem2("d_k_proj")
        turned = sem2("d_turned")
        q_done = sem2("d_q_done")
        q_spread = sem2("d_q_spread")
        k_done = sem2("d_k_done")
        v_copied = sem2("d_v_copied")
        scored = sem2("d_scored")
        masked = sem2("d_masked")
        maxed = sem2("d_maxed")
        exped = sem2("d_exped")
        p_flipped = sem2("d_p_flipped")
        p_copied = sem2("d_p_copied")
        pv_done = sem2("d_pv_done")
        o_done = sem2("d_o_done")
        projected = sem2("d_projected")
        z_done = sem2("d_z_done")
        z_exped = sem2("d_z_exped")
        kv2_proj = sem2("d_kv2_proj")
        kv2_copied = sem2("d_kv2_copied")
        wide_done = sem2("d_wide_done")
        srow_done = sem2("d_srow_done")
        sel_done = sem2("d_sel_done")
        mix_in = sem2("d_mix_in")
        mixed = sem2("d_mixed")
        mix_out = sem2("d_mix_out")
        skipped = sem2("d_skipped")
        picked = sem2("d_picked")
        xq_copied = sem2("d_xq_copied")
        selT_copied = sem2("d_selT_copied")
        q2_proj = sem2("d_q2_proj")
        qb_done = sem2("d_qb_done")
        scored2 = sem2("d_scored2")
        maxed2 = sem2("d_maxed2")
        exped2 = sem2("d_exped2")
        p2_done = sem2("d_p2_done")
        p2_flipped = sem2("d_p2_flipped")
        p2_copied = sem2("d_p2_copied")
        pv2_done = sem2("d_pv2_done")
        c_done = sem2("d_c_done")
        ao_proj = sem2("d_ao_proj")
        ao_copied = sem2("d_ao_copied")
        placed = sem2("d_placed")
        up_done = sem2("d_up_done")
        gelued = sem2("d_gelued")
        down_done = sem2("d_down_done")
        y_done = sem2("d_y_done")
        y_out = sem2("d_y_out")

        block = ctx.enter_context(nc.Block())

        @block.sync
        def _(sp):
            load_all(sp, [(tile[:], dr[name]) for tile, name in weights], weights_in)

            def load_rows(im, i):
                img = 2 * i + im
                sp.wait_ge(h2_done[im], i + 1)
                sp.dma_start(idx[im][:], dr["slot"][:, bass.ds(2 * img, 2)]).then_inc(rows_in[im], 16)
                sp.dma_start(gain[im][:], dr["gain"][:, bass.ds(2 * img, 2)]).then_inc(rows_in[im], 16)
                sp.dma_start(h1[im][:].rearrange("p c f -> p (c f)"),
                             dr["h1"][bass.ds(img, 1)].rearrange("a p f -> (a p) f")).then_inc(rows_in[im], 16)

            def send_y(im, i):
                sp.wait_ge(y_done[im], i + 2)
                sp.dma_start(dr["out"][bass.ds(2 * i + im, 1)].rearrange("a c p f -> p (a c) f"),
                             y[im][:]).then_inc(y_out[im], 16)

            def half(im, i):
                load_rows(im, i + 1)
                send_y(im, i)

            for im in range(2):
                load_rows(im, 0)
            with sp.Fori(0, ROUNDS - 1) as i:
                for im in range(2):
                    half(im, i)
            for im in range(2):
                send_y(im, ROUNDS - 1)
            for im in range(2):
                sp.wait_ge(y_out[im], 16 * ROUNDS + 16)

        @block.gpsimd
        def _(pool):
            pool.memset(half_neg[:], -0.5).then_inc(consts_set, 1)
            pool.wait_ge(weights_in, W_IN)
            pool.wait_ge(consts_set, CONSTS)
            for im in range(2):
                pool.sem_inc(h2_done[im], 1)

            def gather(im, i):
                pool.wait_ge(rows_in[im], 48 * i + 48)
                pool.sem_inc(fence, 1)
                for c in range(2):
                    pool.indirect_dma_start(out=yx[im][:, c, :], out_offset=None, in_=dr["rows"],
                                            in_offset=bass.IndirectOffsetOnAxis(ap=idx[im][:, c:c + 1], axis=0)
                                            ).then_inc(gathered[im], 16)

            def scale_e(im, i):
                pool.wait_ge(e_stats[im], i + 1)
                pool.tensor_tensor(rr_e[im][:], vv_e[im][:], half_neg[:, 0:2], ALU.pow).then_inc(e_rstd[im], 1)

            def scale_h3(im, i):
                pool.wait_ge(stats[im], 2 * i + 1)
                pool.tensor_tensor(rr[im][:], vv[im][:], half_neg[:].rearrange("p (a c) -> p a c", c=2), ALU.pow
                                   ).then_inc(rstd[im], 1)

            def scale_hm(im, i):
                pool.wait_ge(stats[im], 2 * i + 2)
                pool.tensor_tensor(rr[im][:, 0, :], vv[im][:, 0, :], half_neg[:, 0:2], ALU.pow).then_inc(rstd[im], 1)
                pool.tensor_tensor(skip[im][:], h3[im][:], hm[im][:], ALU.add).then_inc(skipped[im], 1)

            def turn_q(im, i):
                pool.wait_ge(turned[im], 2 * i + 1)
                pool.tensor_tensor(qT[im][:], rot[im][:, :, 0, :], rot[im][:, :, 1, :], ALU.add).then_inc(q_done[im], 1)
                pool.wait_ge(q_done[im], i + 1)
                pool.tensor_tensor(qz[im][:, 0, :, :], spread(qT[im][:, 0, :], 1, 6),
                                   spread(blocks[:, 0, :, 0], 2, SEQ), ALU.mult).then_inc(q_spread[im], 1)

            def turn_k(im, i):
                pool.wait_ge(turned[im], 2 * i + 2)
                pool.tensor_tensor(kT[im][:], rot[im][:, :, 0, :], rot[im][:, :, 1, :], ALU.add).then_inc(k_done[im], 1)

            def half(im, i):
                scale_h3(im, i)
                gather(im, i + 1)
                scale_e(im, i + 1)
                scale_hm(im, i)
                turn_q(im, i + 1)
                turn_k(im, i + 1)

            for im in range(2):
                gather(im, 0)
                scale_e(im, 0)
                turn_q(im, 0)
                turn_k(im, 0)
            with pool.Fori(0, ROUNDS - 1) as i:
                for im in range(2):
                    half(im, i)
            for im in range(2):
                scale_h3(im, ROUNDS - 1)
                scale_hm(im, ROUNDS - 1)

        @block.scalar
        def _(act):
            act.wait_ge(weights_in, W_IN)
            act.wait_ge(consts_set, CONSTS)

            def features_e(im, i):
                act.wait_ge(e_flipped[im], i + 1)
                act.activation(eT[im][0:F, :, :].rearrange("p k n -> p (k n)"), ps[im][0:F, 0, 0:2 * SEQ],
                               ACT.Copy).then_inc(e_feat[im], 1)

            def copy_v(im, i):
                act.wait_ge(v_proj[im], i + 1)
                act.activation(vx[im][:, :, :, 0:DH],
                               ps[im][0:T, 0, 0:2 * D].rearrange("p (c h d) -> p c h d", c=2, d=DH),
                               ACT.Copy).then_inc(v_copied[im], 1)

            def spread_q(im, i):
                act.wait_ge(q_done[im], i + 1)
                for h in range(6):
                    last = act.activation(qz[im][:, 1, h, :], qT[im][:, 1, :], ACT.Copy, scale=blocks[:, 1, h, 0:1])
                last.then_inc(q_spread[im], 1)

            def exps(im, i, p):
                act.wait_ge(maxed[im], PAIRS * i + p + 1)
                for n in range(2):
                    rows = s_sb[im][:, 2 * (p % 2) + n, :]
                    for ci, at in enumerate((slice(0, T), slice(T, CW))):
                        last = act.activation(rows[:, at], rows[:, at], ACT.Exp, scale=DH ** -0.5,
                                              bias=nmx[im][:, p, n, ci:ci + 1])
                last.then_inc(exped[im], 1)

            def copy_p(im, i, p):
                bank = 2 * (p % 2) + 1
                act.wait_ge(p_flipped[im], PAIRS * i + p + 1)
                act.activation(pT[im][:, bank, :], ps[im][0:T, bank, 0:CW], ACT.Copy).then_inc(p_copied[im], 1)

            def features(im, i, n, bank, out, g=None, b=None):
                act.wait_ge(flipped[im], 3 * i + n)
                if g is None:
                    act.activation(out[0:F, :, :].rearrange("p k n -> p (k n)"), ps[im][0:F, bank, 0:2 * SEQ],
                                   ACT.Copy).then_inc(feat[im], 1)
                else:
                    for k in range(2):
                        last = act.activation(out[0:F, k, :], ps[im][0:F, bank, k * SEQ:(k + 1) * SEQ], ACT.Identity,
                                              scale=g[:, k:k + 1], bias=b[:, k:k + 1])
                    last.then_inc(feat[im], 1)

            def exp_z(im, i):
                act.wait_ge(z_done[im], i + 1)
                act.activation(sg[im][:], ps[im][0:T, 1, 0:2], ACT.Exp, scale=-1.0).then_inc(z_exped[im], 1)

            def copy_kv2(im, i):
                act.wait_ge(kv2_proj[im], i + 1)
                act.activation(kT2[im][:].rearrange("p m n -> p (m n)"), ps[im][0:F, 2, 0:2 * SEQ], ACT.Copy)
                act.activation(v2[im][:].rearrange("p c f -> p (c f)"), ps[im][0:T, 3, 0:2 * D],
                               ACT.Copy).then_inc(kv2_copied[im], 1)

            def copy_picked(im, i):
                act.wait_ge(picked[im], i + 1)
                for k in range(2):
                    act.activation(xq[im][0:F, k, :], ps[im][0:F, 2, k * KR:(k + 1) * KR], ACT.Identity,
                                   scale=g1[:, k:k + 1], bias=c1[:, k:k + 1]).then_inc(xq_copied[im], 1)
                act.activation(selT[im][:], ps[im][0:KR, 3, 0:SEQ], ACT.Copy).then_inc(selT_copied[im], 1)

            def exps2(im, i):
                act.wait_ge(maxed2[im], i + 1)
                for gr in range(4):
                    src = ps[im][0:G4, 1 + 2 * (gr // 2), (gr % 2) * SEQ:(gr % 2 + 1) * SEQ]
                    last = act.activation(p2[im][:, gr, :], src, ACT.Exp, scale=DH ** -0.5,
                                          bias=nmx2[im][:, gr:gr + 1], accum_out=sum2[im][:, gr:gr + 1])
                last.then_inc(exped2[im], 1)

            def copy_p2(im, i):
                act.wait_ge(p2_flipped[im], i + 1)
                act.activation(pT2[im][:].rearrange("p (b g) c n -> p b (g c n)", b=2), ps[im][0:T, 1:4:2, 0:4 * G4],
                               ACT.Copy).then_inc(p2_copied[im], 1)

            def copy_ao(im, i):
                act.wait_ge(ao_proj[im], i + 1)
                act.activation(ao[im][:], ps[im][0:KR, 1, 0:D], ACT.Copy).then_inc(ao_copied[im], 1)

            def gelu(im, i):
                act.wait_ge(up_done[im], i + 1)
                act.activation(gT[im][:].rearrange("p (b m) n -> p b (m n)", m=2), ps[im][:, 1:4, 0:2 * SEQ],
                               ACT.Gelu).then_inc(gelued[im], 1)

            def half(a, ia, b, ib, more):
                exps(b, ib, 0)
                features(a, ia, 2, 0, nT[a], g1, c1)
                copy_p(b, ib, 0)
                exps(b, ib, 1)
                exp_z(a, ia)
                copy_p(b, ib, 1)
                exps(b, ib, 2)
                copy_kv2(a, ia)
                copy_p(b, ib, 2)
                copy_picked(a, ia)
                exps(b, ib, 3)
                copy_p(b, ib, 3)
                exps(b, ib, 4)
                exps2(a, ia)
                copy_p(b, ib, 4)
                exps(b, ib, 5)
                copy_p2(a, ia)
                copy_p(b, ib, 5)
                copy_ao(a, ia)
                if more:
                    features_e(a, ia + 1)
                features(a, ia, 3, 0, aT[a], g2, c2)
                gelu(a, ia)
                if more:
                    copy_v(a, ia + 1)
                    spread_q(a, ia + 1)
                features(b, ib, 1, 1, aT[b])

            def head(im, i):
                features_e(im, i)
                copy_v(im, i)
                spread_q(im, i)

            def attention(im, i):
                for p in range(PAIRS):
                    exps(im, i, p)
                    copy_p(im, i, p)

            def tail(im, i):
                features(im, i, 2, 0, nT[im], g1, c1)
                exp_z(im, i)
                copy_kv2(im, i)
                copy_picked(im, i)
                exps2(im, i)
                copy_p2(im, i)
                copy_ao(im, i)
                features(im, i, 3, 0, aT[im], g2, c2)
                gelu(im, i)

            head(0, 0)
            attention(0, 0)
            head(1, 0)
            features(0, 0, 1, 1, aT[0])
            with act.Fori(0, ROUNDS - 1) as i:
                half(0, i, 1, i, True)
                half(1, i, 0, i + 1, True)
            half(0, ROUNDS - 1, 1, ROUNDS - 1, False)
            tail(1, ROUNDS - 1)

        @block.tensor
        def _(pe):
            pe.wait_ge(weights_in, W_IN)
            pe.wait_ge(consts_set, CONSTS)
            for im in range(2):
                pe.sem_inc(y_done[im], 1)
                pe.sem_inc(mix_out[im], 1)

            def flip(im, src, bank, done):
                for k in range(2):
                    for c in range(2):
                        last = pe.transpose(ps[im][0:F, bank, k * SEQ + c * T:k * SEQ + (c + 1) * T],
                                            src[:, c, k * F:(k + 1) * F], ident[0:T, 0:T])
                last.then_inc(done[im], 1)

            def to_tokens(im, bank, src, w, n):
                for c in range(2):
                    for k in range(2):
                        last = pe.matmul(ps[im][0:T, bank, c * n:(c + 1) * n], src[:, k, c * T:(c + 1) * T],
                                         w[:, k, :], start=(k == 0), stop=(k == 1))
                return last

            def flip_e(im, i):
                pe.wait_ge(e_normed[im], i + 1)
                pe.wait_ge(mix_out[im], i + 1)
                flip(im, xe[im], 0, e_flipped)

            def rotary(im, w):
                for m in range(2):
                    for v in range(2):
                        for k in range(2):
                            last = pe.matmul(ps[im][0:F, 1 + m, v * SEQ:(v + 1) * SEQ], w[:, k, v, m * F:(m + 1) * F],
                                             eT[im][:, k, :], start=(k == 0), stop=(k == 1))
                return last

            def queries(im, i):
                pe.wait_ge(e_feat[im], i + 1)
                rotary(im, wq).then_inc(q_proj[im], 1)

            def values_in(im, i):
                to_tokens(im, 0, eT[im], wv, D).then_inc(v_proj[im], 1)

            def keys(im, i):
                pe.wait_ge(turned[im], 2 * i + 1)
                rotary(im, wk).then_inc(k_proj[im], 1)

            def score(im, i, p):
                if p == 0:
                    pe.wait_ge(q_spread[im], 2 * i + 2)
                    pe.wait_ge(k_done[im], i + 1)
                    pe.wait_ge(v_copied[im], i + 1)
                elif p == 1:
                    pe.wait_ge(y_done[im], i + 1)
                else:
                    pe.wait_ge(o_done[im], PAIRS * i + p - 1)
                m = p // 3
                for n in range(2):
                    out = ps[im][0:T, 2 * (p % 2) + n, 0:CW]
                    q = qz[im][:, m, 2 * p - 6 * m + n, :]
                    pe.matmul(out[:, 0:T], q[:, 0:T], kT[im][:, m, 0:T], start=True, stop=True)
                    last = pe.matmul(out[:, T:CW], q[:, T:SEQ], kT[im][:, m, :], start=True, stop=True)
                last.then_inc(scored[im], 1)

            def flip_p(im, i, p):
                pe.wait_ge(exped[im], PAIRS * i + p + 1)
                for n in range(2):
                    bank = 2 * (p % 2) + n
                    for b in range(3):
                        last = pe.transpose(ps[im][0:T, bank, b * T:(b + 1) * T],
                                            s_sb[im][:, bank, b * T:(b + 1) * T], ident[0:T, 0:T])
                last.then_inc(p_flipped[im], 1)

            def values(im, i, p):
                pe.wait_ge(p_copied[im], 2 * (PAIRS * i + p) + 2)
                for ci in range(2):
                    for n in range(2):
                        at = (2 * ci + n) * (DH + 1)
                        for cj in range(ci + 1):
                            b = ci + cj
                            last = pe.matmul(ps[im][0:T, 2 * (p % 2), at:at + DH + 1],
                                             pT[im][:, 2 * (p % 2) + n, b * T:(b + 1) * T],
                                             vx[im][:, cj, 2 * p + n, :], start=(cj == 0), stop=(cj == ci))
                last.then_inc(pv_done[im], 1)

            def flip_o(im, i):
                pe.wait_ge(o_done[im], PAIRS * i + PAIRS)
                flip(im, o_sb[im], 1, flipped)

            def project(im, i):
                pe.wait_ge(feat[im], 3 * i + 1)
                to_tokens(im, 2, aT[im], wp, D).then_inc(projected[im], 1)

            def flip_h3(im, i):
                pe.wait_ge(normed[im], 2 * i + 1)
                flip(im, xr[im], 0, flipped)

            def router(im, i):
                pe.wait_ge(feat[im], 3 * i + 2)
                to_tokens(im, 1, nT[im], wr, 1).then_inc(z_done[im], 1)

            def keys_values2(im, i):
                for m in range(2):
                    for k in range(2):
                        pe.matmul(ps[im][0:F, 2, m * SEQ:(m + 1) * SEQ], uk[:, k, m * F:(m + 1) * F], nT[im][:, k, :],
                                  start=(k == 0), stop=(k == 1))
                to_tokens(im, 3, nT[im], uv, D).then_inc(kv2_proj[im], 1)

            def score_rows(im, i):
                pe.wait_ge(wide_done[im], i + 1)
                for c in range(2):
                    last = pe.transpose(ps[im][0:T, 1, c * T:(c + 1) * T], wide[im][:, c, :], ident[0:T, 0:T])
                last.then_inc(srow_done[im], 1)

            def pick(im, i):
                pe.wait_ge(sel_done[im], i + 1)
                pe.wait_ge(kv2_copied[im], i + 1)
                for k in range(2):
                    for c in range(2):
                        pe.matmul(ps[im][0:F, 2, k * KR:(k + 1) * KR], xr[im][:, c, k * F:(k + 1) * F],
                                  sel[im][:, c, :], start=(c == 0), stop=(c == 1))
                for c in range(2):
                    last = pe.transpose(ps[im][0:KR, 3, c * T:(c + 1) * T], sel[im][:, c, :], ident[0:T, 0:T])
                last.then_inc(picked[im], 1)

            def queries2(im, i):
                pe.wait_ge(xq_copied[im], 2 * i + 2)
                for m in range(2):
                    for k in range(2):
                        last = pe.matmul(ps[im][0:F, 2, m * KR:(m + 1) * KR], uq[:, k, m * F:(m + 1) * F],
                                         xq[im][:, k, :], start=(k == 0), stop=(k == 1))
                last.then_inc(q2_proj[im], 1)

            def score2(im, i):
                pe.wait_ge(qb_done[im], i + 1)
                pe.wait_ge(selT_copied[im], i + 1)
                for m in range(2):
                    for t in range(2):
                        last = pe.matmul(ps[im][0:G4, 1 + 2 * m, t * SEQ:(t + 1) * SEQ],
                                         qb[im][:, m, 3 * t:3 * t + 3, :].rearrange("p h r -> p (h r)"),
                                         kT2[im][:, m, :], start=True, stop=True)
                last.then_inc(scored2[im], 1)

            def mix(im, i):
                pe.wait_ge(mix_in[im], i + 1)
                to_tokens(im, 0, mT[im], um, D).then_inc(mixed[im], 1)

            def flip_p2(im, i):
                pe.wait_ge(p2_done[im], i + 1)
                for gr in range(4):
                    for cj in range(2):
                        at = ((gr % 2) * 2 + cj) * G4
                        last = pe.transpose(ps[im][0:T, 1 + 2 * (gr // 2), at:at + G4],
                                            p2[im][:, gr, cj * T:(cj + 1) * T], ident[0:G4, 0:G4])
                last.then_inc(p2_flipped[im], 1)

            def values2(im, i):
                pe.wait_ge(p2_copied[im], i + 1)
                for m in range(2):
                    for cj in range(2):
                        last = pe.matmul(ps[im][0:F, 2, m * 2 * G4:(m + 1) * 2 * G4], v2[im][:, cj, m * F:(m + 1) * F],
                                         pT2[im][:, 2 * m:2 * m + 2, cj, :], start=(cj == 0), stop=(cj == 1))
                last.then_inc(pv2_done[im], 1)

            def project2(im, i):
                pe.wait_ge(c_done[im], i + 1)
                for k in range(2):
                    last = pe.matmul(ps[im][0:KR, 1, 0:D], cT[im][:, k, :], uo[:, k, :], start=(k == 0), stop=(k == 1))
                last.then_inc(ao_proj[im], 1)

            def place(im, i):
                pe.wait_ge(ao_copied[im], i + 1)
                for c in range(2):
                    last = pe.matmul(ps[im][0:T, 3, c * D:(c + 1) * D], selT[im][:, c * T:(c + 1) * T], ao[im][:],
                                     start=True, stop=True)
                last.then_inc(placed[im], 1)

            def flip_hm(im, i):
                pe.wait_ge(normed[im], 2 * i + 2)
                flip(im, xh[im], 0, flipped)

            def up(im, i, more):
                pe.wait_ge(feat[im], 3 * i + 3)
                if more:
                    pe.wait_ge(turned[im], 2 * i + 3)
                for m in range(6):
                    at = (m % 2) * SEQ
                    for k in range(2):
                        last = pe.matmul(ps[im][:, 1 + m // 2, at:at + SEQ], w1[:, k, m * 128:(m + 1) * 128],
                                         aT[im][:, k, :], start=(k == 0), stop=(k == 1))
                last.then_inc(up_done[im], 1)

            def down(im, i):
                pe.wait_ge(gelued[im], i + 1)
                for c in range(2):
                    out = ps[im][0:T, 3, c * D:(c + 1) * D]
                    for m in range(6):
                        pe.matmul(out, gT[im][:, m, c * T:(c + 1) * T], w2[:, m, :], start=(m == 0), stop=False)
                    last = pe.matmul(out, ones_row[0:1, 0:T], b2[0:1, :], start=False, stop=True)
                last.then_inc(down_done[im], 1)

            def half(a, ia, b, ib, more):
                score(b, ib, 0)
                score(b, ib, 1)
                flip_h3(a, ia)
                flip_p(b, ib, 0)
                values(b, ib, 0)
                router(a, ia)
                flip_p(b, ib, 1)
                score(b, ib, 2)
                score_rows(a, ia)
                values(b, ib, 1)
                keys_values2(a, ia)
                flip_p(b, ib, 2)
                score(b, ib, 3)
                pick(a, ia)
                values(b, ib, 2)
                queries2(a, ia)
                flip_p(b, ib, 3)
                score(b, ib, 4)
                score2(a, ia)
                values(b, ib, 3)
                flip_p(b, ib, 4)
                score(b, ib, 5)
                mix(a, ia)
                values(b, ib, 4)
                flip_p2(a, ia)
                flip_p(b, ib, 5)
                values2(a, ia)
                values(b, ib, 5)
                project2(a, ia)
                if more:
                    flip_e(a, ia + 1)
                place(a, ia)
                if more:
                    queries(a, ia + 1)
                flip_hm(a, ia)
                up(a, ia, more)
                if more:
                    values_in(a, ia + 1)
                down(a, ia)
                flip_o(b, ib)
                if more:
                    keys(a, ia + 1)
                project(b, ib)

            def head(im, i):
                flip_e(im, i)
                queries(im, i)
                values_in(im, i)
                keys(im, i)

            def attention(im, i):
                for p in range(PAIRS):
                    score(im, i, p)
                    flip_p(im, i, p)
                    values(im, i, p)

            def tail(im, i):
                flip_h3(im, i)
                router(im, i)
                keys_values2(im, i)
                score_rows(im, i)
                pick(im, i)
                queries2(im, i)
                score2(im, i)
                mix(im, i)
                flip_p2(im, i)
                values2(im, i)
                project2(im, i)
                place(im, i)
                flip_hm(im, i)
                up(im, i, False)
                down(im, i)

            head(0, 0)
            attention(0, 0)
            head(1, 0)
            flip_o(0, 0)
            project(0, 0)
            with pe.Fori(0, ROUNDS - 1) as i:
                half(0, i, 1, i, True)
                half(1, i, 0, i + 1, True)
            half(0, ROUNDS - 1, 1, ROUNDS - 1, False)
            tail(1, ROUNDS - 1)

        @block.vector
        def _(dve):
            dve.memset(ones_row[:], 1.0).then_inc(consts_set, 1)
            for im in range(2):
                dve.memset(eT[im][F:FB, :, :], 1.0)
                for tile in (aT, nT, mT, xq):
                    dve.memset(tile[im][F:FB, :, :], 1.0).then_inc(consts_set, 1)
                dve.memset(cT[im][F:FB, :, :], 1.0)
                dve.memset(vx[im][:, :, :, DH:DH + 1], 1.0).then_inc(consts_set, 1)
                dve.sem_inc(y_out[im], 16)
            dve.wait_ge(weights_in, W_IN)
            head_link = [Link(dve, head_links[im], 2) for im in range(2)]
            att_link = [Link(dve, att_links[im], 2 * PAIRS) for im in range(2)]
            h3_link = [Link(dve, h3_links[im], 3) for im in range(2)]
            tail_link = [Link(dve, tail_links[im], 17) for im in range(2)]

            def flat(tile):
                return tile[:].rearrange("p c f -> p (c f)")

            def mean_var(st, mv, link, rows):
                dve.bn_stats(st[:, 0, :], rows[:, 0, :])
                link(dve.bn_stats(st[:, 1, :], rows[:, 1, :]))
                dve.sem_inc(fence, 1)
                dve.bn_aggr(mv[:, 0, :], st[:, 0, :])
                link(dve.bn_aggr(mv[:, 1, :], st[:, 1, :]))
                return mv[:, :, 1]

            def input_rows(im, i):
                link = head_link[im]
                link.round(i)
                dve.wait_ge(gathered[im], 32 * i + 32)
                for c in range(2):
                    last = dve.scalar_tensor_tensor(h2[im][:, c, :], yx[im][:, c, :], gain[im][:, c:c + 1],
                                                    h1[im][:, c, :], ALU.mult, ALU.add)
                last.then_inc(h2_done[im], 1)
                dve.wait_ge(h2_done[im], i + 2)
                var = mean_var(st_e[im], mv_e[im], link, h2[im])
                dve.tensor_scalar(vv_e[im][:], var, EPS, None, ALU.add).then_inc(e_stats[im], 1)

            def normalise_e(im, i):
                dve.wait_ge(e_rstd[im], i + 1)
                for c in range(2):
                    last = dve.tensor_scalar(xe[im][:, c, :], h2[im][:, c, :], mv_e[im][:, c, 0:1],
                                             rr_e[im][:, c:c + 1], ALU.subtract, ALU.mult)
                last.then_inc(e_normed[im], 1)

            def turn(im, i, n):
                dve.wait_ge((q_proj, k_proj)[n][im], i + 1)
                if n == 1:
                    dve.wait_ge(q_done[im], i + 1)
                dve.tensor_tensor(rot[im][:].rearrange("p m v n -> p m (v n)"), ps[im][0:F, 1:3, 0:2 * SEQ],
                                  spread(rope[:].rearrange("p v n -> p (v n)"), 1, 2), ALU.mult
                                  ).then_inc(turned[im], 1)

            def mask_max(im, i, p):
                at = slice(2 * (p % 2), 2 * (p % 2) + 2)
                link = att_link[im]
                if p == 0:
                    link.round(i)
                dve.wait_ge(scored[im], PAIRS * i + p + 1)
                dve.tensor_tensor(s_sb[im][:, at, :], ps[im][0:T, at, 0:CW], spread(causal[:], 1, 2), ALU.add
                                  ).then_inc(masked[im], 1)
                dve.wait_ge(masked[im], PAIRS * i + p + 1)
                dve.tensor_reduce(mx[im][:, p, :, 0], s_sb[im][:, at, 0:T], AX.X, ALU.max)
                link(dve.tensor_reduce(mx[im][:, p, :, 1], s_sb[im][:, at, T:CW], AX.X, ALU.max))
                dve.tensor_scalar(nmx[im][:, p, :, :], mx[im][:, p, :, :], -(DH ** -0.5), None, ALU.mult
                                  ).then_inc(maxed[im], 1)

            def copy_p(im, i, p):
                bank = 2 * (p % 2)
                dve.wait_ge(p_flipped[im], PAIRS * i + p + 1)
                dve.tensor_copy(pT[im][:, bank, :], ps[im][0:T, bank, 0:CW]).then_inc(p_copied[im], 1)

            def divide(im, i, p):
                dve.wait_ge(pv_done[im], PAIRS * i + p + 1)
                o_ps = ps[im][0:T, 2 * (p % 2), 0:4 * (DH + 1)].rearrange("p (c h d) -> p c h d", c=2, d=DH + 1)
                att_link[im](dve.reciprocal(rs[im][:], o_ps[:, :, :, DH]))
                dve.tensor_tensor(o_sb[im][:, :, 2 * p * DH:2 * (p + 1) * DH].rearrange("p c (h d) -> p c h d", d=DH),
                                  o_ps[:, :, :, 0:DH], spread(rs[im][:], 3, DH), ALU.mult).then_inc(o_done[im], 1)

            def attended(im, i):
                link = h3_link[im]
                link.round(i)
                dve.wait_ge(projected[im], i + 1)
                link(dve.tensor_tensor(flat(h3[im]), ps[im][0:T, 2, 0:2 * D], flat(h2[im]), ALU.add))
                var = mean_var(st[im], mv[im], link, h3[im])
                dve.tensor_scalar(vv[im][:, 0, :], var, EPS, None, ALU.add)
                dve.tensor_scalar(vv[im][:, 1, :], var, 1 + EPS, EPS * EPS, ALU.mult, ALU.add).then_inc(stats[im], 1)

            def normalise_h3(im, i):
                dve.wait_ge(rstd[im], 2 * i + 1)
                for c in range(2):
                    last = dve.tensor_scalar(xr[im][:, c, :], h3[im][:, c, :], mv[im][:, c, 0:1],
                                             rr[im][:, 1, c:c + 1], ALU.subtract, ALU.mult)
                last.then_inc(normed[im], 1)
                for c in range(2):
                    dve.tensor_scalar(hid[im][:, c, :], h3[im][:, c, :], mv[im][:, c, 0:1],
                                      rr[im][:, 0, c:c + 1], ALU.subtract, ALU.mult)

            def sigmoid(im, i):
                link = tail_link[im]
                link.round(i)
                dve.wait_ge(z_exped[im], i + 1)
                link(dve.tensor_scalar(sg[im][:], sg[im][:], 1.0, None, ALU.add))
                link(dve.reciprocal(chance[im][:], sg[im][:]))
                dve.tensor_copy(wide[im][:], spread(chance[im][:], 2, T)).then_inc(wide_done[im], 1)

            def select(im, i):
                link = tail_link[im]
                dve.wait_ge(srow_done[im], i + 1)
                link(dve.tensor_copy(srow[im][:], ps[im][0:T, 1, 0:SEQ]))
                for c in range(2):
                    dve.tensor_scalar(junk[im][:, c, :], srow[im][:], chance[im][:, c:c + 1], None, ALU.is_lt, ALU.add,
                                      accum_out=less[im][:, c:c + 1])
                    last = dve.scalar_tensor_tensor(junk2[im][:, c, :], srow[im][:], chance[im][:, c:c + 1],
                                                    earlier[:, c, :], ALU.is_equal, ALU.mult,
                                                    accum_out=ties[im][:, c:c + 1])
                link(last)
                link(dve.tensor_tensor(rank[im][:], less[im][:], ties[im][:], ALU.add))
                dve.tensor_scalar(away[im][:], rank[im][:], float(KR), None, ALU.is_ge)
                for c in range(2):
                    last = dve.tensor_scalar(sel[im][:, c, :], places[:], rank[im][:, c:c + 1], None, ALU.is_equal)
                last.then_inc(sel_done[im], 1)

            def pooled(im, i):
                link = tail_link[im]
                link(dve.tensor_reduce(ssum[im][:], srow[im][:], AX.X, ALU.add))
                link(dve.tensor_scalar(ssum[im][:], ssum[im][:], 1e-6, None, ALU.add))
                link(dve.reciprocal(ssum[im][:], ssum[im][:]))
                for k in range(2):
                    link(dve.tensor_tensor_reduce(out=junk[im][0:F, k, :], in0=nT[im][0:F, k, :], in1=srow[im][0:F, :],
                                                  scale=1.0, scalar=0.0, op0=ALU.mult, op1=ALU.add,
                                                  accum_out=pool_r[im][:, k:k + 1]))
                link(dve.tensor_scalar(pool_t[im][:], pool_r[im][:], ssum[im][0:F, :], None, ALU.mult))
                for k in range(2):
                    last = dve.scalar_tensor_tensor(mT[im][0:F, k, :], srow[im][0:F, :], pool_t[im][:, k:k + 1],
                                                    nT[im][0:F, k, :], ALU.mult, ALU.add)
                last.then_inc(mix_in[im], 1)

            def heads_of_q2(im, i):
                dve.wait_ge(q2_proj[im], i + 1)
                dve.tensor_tensor(qb[im][:], spread(ps[im][0:F, 2, 0:2 * KR].rearrange("p (m r) -> p m r", m=2), 2, 6),
                                  blocks[:], ALU.mult).then_inc(qb_done[im], 1)

            def max2(im, i):
                dve.wait_ge(scored2[im], i + 1)
                tail_link[im](dve.tensor_reduce(mx2[im][:].rearrange("p (b g) -> p b g", b=2),
                                                ps[im][0:G4, 1:4:2, 0:2 * SEQ].rearrange("p b (g n) -> p b g n", g=2),
                                                AX.X, ALU.max))
                dve.tensor_scalar(nmx2[im][:], mx2[im][:], -(DH ** -0.5), None, ALU.mult).then_inc(maxed2[im], 1)

            def mixed_rows(im, i):
                dve.wait_ge(mixed[im], i + 1)
                for c in range(2):
                    last = dve.scalar_tensor_tensor(hm[im][:, c, :], ps[im][0:T, 0, c * D:(c + 1) * D],
                                                    away[im][:, c:c + 1], hid[im][:, c, :], ALU.mult, ALU.add)
                last.then_inc(mix_out[im], 1)

            def divide2(im, i):
                dve.wait_ge(exped2[im], i + 1)
                tail_link[im](dve.reciprocal(rs2[im][:], sum2[im][:]))
                dve.tensor_tensor(p2[im][:], p2[im][:], spread(rs2[im][:], 2, SEQ), ALU.mult).then_inc(p2_done[im], 1)

            def own_heads(im, i):
                dve.wait_ge(pv2_done[im], i + 1)
                tail_link[im](dve.tensor_tensor(cb[im][:].rearrange("p m h r -> p (m h r)"), ps[im][0:F, 2, 0:4 * G4],
                                                blocks[:].rearrange("p m h r -> p (m h r)"), ALU.mult))
                dve.tensor_reduce(cT[im][0:F, :, :], cb[im][:].rearrange("p m h r -> p m r h"), AX.X, ALU.add
                                  ).then_inc(c_done[im], 1)

            def routed_rows(im, i):
                link = tail_link[im]
                dve.wait_ge(placed[im], i + 1)
                dve.wait_ge(mix_out[im], i + 2)
                link(dve.tensor_tensor(flat(hm[im]), flat(hm[im]), ps[im][0:T, 3, 0:2 * D], ALU.add))
                var = mean_var(st[im], mv[im], link, hm[im])
                dve.tensor_scalar(vv[im][:, 0, :], var, EPS, None, ALU.add).then_inc(stats[im], 1)

            def normalise_hm(im, i):
                dve.wait_ge(rstd[im], 2 * i + 2)
                for c in range(2):
                    last = dve.tensor_scalar(xh[im][:, c, :], hm[im][:, c, :], mv[im][:, c, 0:1],
                                             rr[im][:, 0, c:c + 1], ALU.subtract, ALU.mult)
                last.then_inc(normed[im], 1)

            def result(im, i):
                dve.wait_ge(down_done[im], i + 1)
                dve.wait_ge(skipped[im], i + 1)
                dve.wait_ge(y_out[im], 16 * i + 16)
                dve.tensor_tensor(flat(y[im]), ps[im][0:T, 3, 0:2 * D], flat(skip[im]), ALU.add).then_inc(y_done[im], 1)

            def half(a, ia, b, ib, more):
                mask_max(b, ib, 0)
                normalise_h3(a, ia)
                copy_p(b, ib, 0)
                mask_max(b, ib, 1)
                divide(b, ib, 0)
                sigmoid(a, ia)
                copy_p(b, ib, 1)
                mask_max(b, ib, 2)
                divide(b, ib, 1)
                select(a, ia)
                if more:
                    input_rows(a, ia + 1)
                copy_p(b, ib, 2)
                mask_max(b, ib, 3)
                divide(b, ib, 2)
                if more:
                    normalise_e(a, ia + 1)
                heads_of_q2(a, ia)
                copy_p(b, ib, 3)
                mask_max(b, ib, 4)
                max2(a, ia)
                divide(b, ib, 3)
                pooled(a, ia)
                copy_p(b, ib, 4)
                mask_max(b, ib, 5)
                divide2(a, ia)
                mixed_rows(a, ia)
                divide(b, ib, 4)
                copy_p(b, ib, 5)
                own_heads(a, ia)
                divide(b, ib, 5)
                routed_rows(a, ia)
                normalise_hm(a, ia)
                if more:
                    turn(a, ia + 1, 0)
                result(a, ia)
                if more:
                    turn(a, ia + 1, 1)
                attended(b, ib)

            def head(im, i):
                input_rows(im, i)
                normalise_e(im, i)
                turn(im, i, 0)
                turn(im, i, 1)

            def attention(im, i):
                for p in range(PAIRS):
                    mask_max(im, i, p)
                    copy_p(im, i, p)
                    divide(im, i, p)

            def tail(im, i):
                normalise_h3(im, i)
                sigmoid(im, i)
                select(im, i)
                heads_of_q2(im, i)
                pooled(im, i)
                max2(im, i)
                mixed_rows(im, i)
                divide2(im, i)
                own_heads(im, i)
                routed_rows(im, i)
                normalise_hm(im, i)
                result(im, i)

            head(0, 0)
            attention(0, 0)
            head(1, 0)
            attended(0, 0)
            with dve.Fori(0, ROUNDS - 1) as i:
                half(0, i, 1, i, True)
                half(1, i, 0, i + 1, True)
            half(0, ROUNDS - 1, 1, ROUNDS - 1, False)
            tail(1, ROUNDS - 1)


def build(nc, dr):
    with ExitStack() as ctx:
        scattered = [ctx.enter_context(nc.semaphore(f"b_scattered{n}")) for n in range(4)]
        y_out = [ctx.enter_context(nc.semaphore(f"c_y_out{n}")) for n in range(2)]
        gathered = [ctx.enter_context(nc.semaphore(f"d_gathered{n}")) for n in range(2)]
        stage_a(nc, dr)
        stage_b(nc, dr, scattered)
        stage_c(nc, dr, y_out)
        stage_d(nc, dr, gathered)


def dram_views(nc, given):
    dr = dict(given)

    def scratch(name, shape, dt=FP32):
        return nc.dram_tensor(name, shape, dt, kind="Internal").ap()

    band = scratch("band_rows", [2, T, H0 * 2 * PITCH])
    row = H0 * 2 * PITCH
    dr["band"] = [band[im] for im in range(2)]
    dr["band_skew"] = [bass.AP(tensor=band.tensor, offset=im * T * row, ap=[[row + 1, T], [PITCH, 2 * H0], [1, BAND]])
                       for im in range(2)]
    dr["band_read"] = [bass.AP(tensor=band.tensor, offset=im * T * row + PITCH - SEQ,
                               ap=[[row, T], [2 * PITCH, H0], [1, 2 * SEQ]]) for im in range(2)]
    dr["h1"] = scratch("h1_rows", [IMAGES, T, 2 * D])
    dr["xf"] = scratch("xf_rows", [IMAGES, T, 2 * D])
    dr["lg"] = scratch("router_logits", [IMAGES, T, 2 * E])
    dr["slot"] = scratch("slots", [T, COLS], INT32)
    dr["gain"] = scratch("gains", [T, COLS])
    dr["rows"] = scratch("rows", [ROWS, D])
    share = ROWS * D // ROUNDS
    assert share * ROUNDS == ROWS * D and share % 128 == 0
    dr["rows_flat"] = bass.AP(tensor=dr["rows"].tensor, offset=0,
                              ap=[[share, ROUNDS], [share // 128, 128], [1, share // 128]])
    return dr


def lay_out(np, a):
    f32 = np.float32

    def chunks(w, bias=None):
        out = np.zeros((FB, 2, w.shape[1]), w.dtype)
        out[:F] = w.reshape(2, F, -1).transpose(1, 0, 2)
        if bias is not None:
            out[F, 1] = bias.reshape(-1)
        return out

    def cols(v):
        return np.ascontiguousarray(v.reshape(2, F).T)

    def rows128(w):
        return np.ascontiguousarray(w.reshape(-1, 128, w.shape[1]).transpose(1, 0, 2))

    out = {}
    x = a["x"].reshape(IMAGES, 3, 14, 16, 14, 16).transpose(0, 1, 2, 4, 5, 3).reshape(IMAGES, SEQ, 6, 128)
    out["x"] = np.ascontiguousarray(x.transpose(0, 3, 2, 1))
    out["we"] = rows128(a["L0_tok_W"].T)
    out["be"] = a["L0_tok_b"].reshape(1, D)
    out["wq"] = chunks(a["L0_attn_wq"], a["L0_attn_u_param"])
    out["wk"] = chunks(a["L0_attn_wk"])
    out["wv"] = chunks(a["L0_attn_wv"])
    out["wo"] = chunks(a["L0_attn_wo"], a["L0_attn_bo"])
    out["w1"] = chunks(a["L0_attn_w1"], a["L0_attn_b1"])
    out["w2"] = rows128(a["L0_attn_w2"])
    out["b2"] = a["L0_attn_b2"].reshape(1, D)
    out["ws"] = chunks(a["L0_ffn_switch_w"], a["L0_ffn_switch_b"])
    out["n1"] = cols(a["L0_attn_norm1_w"])
    out["n2"] = cols(a["L0_attn_norm2_w"])
    out["wq_t"] = np.ascontiguousarray(a["L0_attn_wq"].T.reshape(H0, DK0, D).transpose(1, 0, 2))
    out["wpos"] = np.ascontiguousarray(a["L0_attn_w_pos"].transpose(1, 0, 2))
    out["vpar"] = np.ascontiguousarray(a["L0_attn_v_param"].T)
    out["we1"] = np.stack([chunks(a["L0_ffn_w1"][e], a["L0_ffn_b1"][e]) for e in range(E)])
    out["we2"] = np.stack([rows128(a["L0_ffn_w2"][e]) for e in range(E)])
    out["be2"] = a["L0_ffn_b2"]
    def rotary(w, bias):
        w, bias = w.T.reshape(D, D // 2, 2), bias.reshape(1, D // 2, 2)
        both = []
        for swap in (slice(None), slice(None, None, -1)):
            both.append(chunks(np.ascontiguousarray(w[:, :, swap]).reshape(D, D),
                               np.ascontiguousarray(bias[:, :, swap]).reshape(1, D)))
        return np.stack(both, axis=2)

    out["dq"] = rotary(a["L1_attn_Wq"], a["L1_attn_bq"])
    out["dk"] = rotary(a["L1_attn_Wk"], a["L1_attn_bk"])
    out["dv"] = chunks(a["L1_attn_Wv"].T, a["L1_attn_bv"])
    out["dp"] = chunks(a["L1_attn_Wp"].T, a["L1_attn_bp"])
    out["wr"] = chunks(a["L1_ffn_Wr"].reshape(D, 1), a["L1_ffn_br"].reshape(1, 1))
    for name, w in (("uq", "q"), ("uk", "k"), ("uv", "v"), ("uo", "o"), ("um", "m")):
        out[name] = chunks(a["L1_ffn_W" + w], a["L1_ffn_b" + w])
    out["u1"] = chunks(a["L1_ffn_W1"], a["L1_ffn_bf1"])
    out["u2"] = rows128(a["L1_ffn_W2"])
    out["ub2"] = a["L1_ffn_bf2"].reshape(1, D)
    out["g1"], out["c1"] = cols(a["L1_ffn_g1"]), cols(a["L1_ffn_b1"])
    out["g2"], out["c2"] = cols(a["L1_ffn_g2"]), cols(a["L1_ffn_b2"])
    inv = (f32(1.0) / f32(10000.0) ** (f32(2.0) * np.arange(DH // 2, dtype=f32) / f32(DH))).astype(f32)
    angle = (np.arange(SEQ, dtype=f32)[:, None] * inv[None, :]).astype(f32)
    table = np.zeros((F // DH, DH, 2, SEQ), f32)
    for j in range(DH):
        table[:, j, 0] = np.cos(angle[:, j // 2])
        table[:, j, 1] = np.sin(angle[:, j // 2]) * (-1 if j % 2 == 0 else 1)
    out["rope"] = table.reshape(F, 2, SEQ)
    later = np.where(np.arange(T)[None, :] > np.arange(T)[:, None], f32(-1e30), f32(0))
    out["causal"] = np.concatenate([later, np.zeros((T, T)), later], axis=1).astype(f32)
    token = np.arange(2)[None, :, None] * T + np.arange(T)[:, None, None]
    out["earlier"] = (np.arange(SEQ)[None, None, :] < token).astype(f32)
    out["places"] = np.tile(np.arange(K_ROUTED, dtype=f32), (T, 1))
    head = (np.arange(F)[:, None] // DH == np.arange(6)[None, :]).astype(f32)
    out["blocks"] = np.ascontiguousarray(np.broadcast_to(head[:, None, :, None], (F, 2, 6, K_ROUTED)))
    out["order"] = np.tile(np.arange(E, 0, -1, dtype=f32), (T, 1))
    out["offset"] = np.tile(np.arange(E, dtype=f32) * SLOTS, (T, 1))
    out["spare"] = (E * SLOTS + np.arange(COLS)[None, :] * T + np.arange(T)[:, None]).astype(f32)
    out["before"] = np.triu(np.ones((T, T), f32), 1)
    out["ones"] = np.ones((T, T), f32)
    out["ident"] = np.eye(128, dtype=f32)
    rate = np.exp(np.log(f32((SEQ + 1) / 2.0)) / f32(NPOS // 2))
    widths = rate ** np.arange(1, NPOS // 2 + 1, dtype=f32)
    d = np.arange(-98, 99)[None, :].astype(f32)
    near = (np.abs(d) <= widths[:, None]).astype(f32)
    assert widths[-1] < 99
    basis = np.zeros((4, NPOS, 4, BAND), f32)
    for hh in range(4):
        basis[hh, :, hh] = np.concatenate([near, np.sign(d) * near])
    out["basis"] = basis.reshape(128, 4, BAND)
    return out


def kernel(**inputs):
    import numpy as np
    import concourse.bacc as bacc
    from concourse.bass_utils import run_bass_kernel_spmd

    nc = bacc.Bacc("TRN2", target_bir_lowering=False, num_devices=1)
    arrays = lay_out(np, {name: np.asarray(v) for name, v in inputs.items()})
    given = {name: nc.dram_tensor(f"in_{name}", v.shape, mybir.dt.from_np(v.dtype), kind="ExternalInput").ap()
             for name, v in arrays.items()}
    given["out"] = nc.dram_tensor("out", [IMAGES, 2, T, D], FP32, kind="ExternalOutput").ap()
    build(nc, dram_views(nc, given))
    run = run_bass_kernel_spmd(nc, [{f"in_{name}": v for name, v in arrays.items()}], core_ids=[0])
    return run.results[0]["out"].reshape(IMAGES, SEQ, D)
```
